# Optimizing a Trainium2 kernel written in Bass

```python
import numpy as np
import jax
import jax.numpy as jnp

def _softmax(x, axis=-1):
    return jax.nn.softmax(x, axis=axis)

def _gelu(x):
    return jax.nn.gelu(x, approximate=True)

def _silu(x):
    return jax.nn.silu(x)

def _sigmoid(x):
    return jax.nn.sigmoid(x)

def _layernorm(x, axis=-1, eps=1e-05):
    m = jnp.mean(x, axis=axis, keepdims=True)
    v = jnp.var(x, axis=axis, keepdims=True)
    return (x - m) / jnp.sqrt(v + eps)

def _scatter_add(tgt, idx, src, axis=0):
    return tgt.at[idx].add(src)

def _segment_sum(src, seg, n):
    return jax.ops.segment_sum(src, seg, n)
kernel_name = 'mk_decoder_preln_d2_seqx_r4_87e854'

def setup_inputs(seed: int=0):
    np.random.seed(seed)
    _w = jnp.asarray

    def _rec_inputs():
        import jax
        import jax.numpy as jnp
        _rk = jax.random.key(seed)
        x = -0.0002928 + 1 * jax.random.normal(jax.random.fold_in(_rk, 1), (16, 256, 256), jnp.float32)
        _lenS = 256 - jax.random.randint(jax.random.fold_in(_rk, 7), (16,), 0, max(1, 256 // 4) + 1, jnp.int32)
        _lenS2 = 256 - jax.random.randint(jax.random.fold_in(_rk, 8), (16,), 0, max(1, 256 // 4) + 1, jnp.int32)
        _ctx_1024P = jax.random.normal(jax.random.fold_in(_rk, 11), (16, 16, 256), jnp.float32)
        _ctx_1024c = jax.random.dirichlet(jax.random.fold_in(_rk, 511), 0.3 * jnp.ones((16,), jnp.float32), (16, 256))
        _ctx_1024t = jnp.einsum('bsk,bkd->bsd', _ctx_1024c, _ctx_1024P)
        _ctx_1024t = _ctx_1024t * jax.lax.rsqrt(jnp.mean(jnp.square(_ctx_1024t)) + 1e-12) * 0.953939
        ctx_1024 = -1.39393e-06 + 0.999914 * (_ctx_1024t + 0.3 * jax.random.normal(jax.random.fold_in(_rk, 611), (16, 256, 256), jnp.float32))
        fside_BxSxS2_0 = jax.random.uniform(jax.random.fold_in(_rk, 13), (16, 256, 256), jnp.float32, 0.0, 1.5)
        _validS = jnp.arange(256)[None, :] < _lenS[:, None]
        _validS2 = jnp.arange(256)[None, :] < _lenS2[:, None]
        _causal = jnp.tril(jnp.ones((256, 256), dtype=bool))
        mask_BxS2_if1 = jnp.where(jnp.ones((16, 256), dtype=bool), 1, 0).astype(jnp.int32)
        return (x, ctx_1024, fside_BxSxS2_0, mask_BxS2_if1)
    x, ctx_1024, fside_BxSxS2_0, mask_BxS2_if1 = _rec_inputs()

    def _L0_attn_setup():
        import jax, jax.numpy as jnp
        import numpy as np
        H = 16
        EPS = 1e-06
        key = jax.random.key(seed)
        ks = jax.random.split(key, 5)
        B, N, D = (4, 1024, 256)
        x = jax.random.normal(ks[0], (B, N, D), dtype=jnp.float32)
        q = jax.random.normal(ks[1], (D,), dtype=jnp.float32)
        k = jax.random.normal(ks[2], (D,), dtype=jnp.float32)
        log_decay = jax.random.normal(ks[3], (H,), dtype=jnp.float32)
        norm_weight = jnp.ones((D,), dtype=jnp.float32)
        o_w = jax.random.normal(ks[4], (D, D), dtype=jnp.float32) * 0.02
        return {'x': x, 'q': q, 'k': k, 'log_decay': log_decay, 'norm_weight': norm_weight, 'o_w': o_w}
    _L0_attn_all = _L0_attn_setup()
    _L0_attn_in = {k: v for k, v in _L0_attn_all.items() if k in ('q', 'k', 'log_decay', 'norm_weight', 'o_w')}
    del _L0_attn_all

    def _L0_xattn_setup():
        import jax, jax.numpy as jnp
        import numpy as np
        D_MODEL = 256
        N_HEADS = 16
        D_K = D_MODEL // N_HEADS
        B, L = (2, 512)

        def _dense_bf16(x, W, b):
            return jnp.matmul(x.astype(jnp.bfloat16), W.astype(jnp.bfloat16)) + b.astype(jnp.bfloat16)

        def _attention(q, k, v, mask):
            Lq, Ls, dk = (q.shape[2], k.shape[2], q.shape[3])
            scale = 1.0 / np.sqrt(dk)
            scores = jnp.einsum('bhqd,bhkd->bhqk', q, k) * scale
            causal = jnp.tril(jnp.ones((Lq, Ls), bool))
            full_mask = causal[None, None] & (mask[:, None, None, :] > 0)
            scores = jnp.where(full_mask, scores, -jnp.inf)
            p = jax.nn.softmax(scores, axis=-1)
            return jnp.einsum('bhqk,bhkd->bhqd', p, v)
        key = jax.random.key(seed)
        ks = jax.random.split(key, 8)
        inp = {'q': jax.random.normal(ks[0], (B, L, D_MODEL), jnp.float32), 'k': jax.random.normal(ks[1], (B, L, D_MODEL), jnp.float32), 'v': jax.random.normal(ks[2], (B, L, D_MODEL), jnp.float32), 'mask': jnp.ones((B, L), jnp.int32), 'Wq': jax.random.normal(ks[3], (D_MODEL, D_MODEL), jnp.float32) * 0.02, 'bq': jnp.zeros((D_MODEL,), jnp.float32), 'Wk': jax.random.normal(ks[4], (D_MODEL, D_MODEL), jnp.float32) * 0.02, 'bk': jnp.zeros((D_MODEL,), jnp.float32), 'Wv': jax.random.normal(ks[5], (D_MODEL, D_MODEL), jnp.float32) * 0.02, 'bv': jnp.zeros((D_MODEL,), jnp.float32), 'Wo': jax.random.normal(ks[6], (D_MODEL, D_MODEL), jnp.float32) * 0.02, 'bo': jnp.zeros((D_MODEL,), jnp.float32)}
        return inp
    _L0_xattn_all = _L0_xattn_setup()
    _L0_xattn_in = {k: v for k, v in _L0_xattn_all.items() if k in ('Wq', 'bq', 'Wk', 'bk', 'Wv', 'bv', 'Wo', 'bo')}
    del _L0_xattn_all

    def _L0_ffn_setup():
        import jax, jax.numpy as jnp
        import numpy as np
        EMBED_DIM = 256
        HIDDEN_DIM = 1024
        NUM_EXPERTS = 8
        TOP_K = 2
        key = jax.random.key(seed)
        k_x, k_g, k_w1, k_w2 = jax.random.split(key, 4)
        x = jax.random.normal(k_x, (2, 128, EMBED_DIM), dtype=jnp.float32)
        gate_w = jax.random.normal(k_g, (NUM_EXPERTS, EMBED_DIM), dtype=jnp.float32) * (1.0 / np.sqrt(EMBED_DIM))
        w1 = jax.random.normal(k_w1, (NUM_EXPERTS, EMBED_DIM, HIDDEN_DIM), dtype=jnp.float32) * np.sqrt(2.0 / EMBED_DIM)
        b1 = jnp.zeros((NUM_EXPERTS, HIDDEN_DIM), dtype=jnp.float32)
        w2 = jax.random.normal(k_w2, (NUM_EXPERTS, HIDDEN_DIM, EMBED_DIM), dtype=jnp.float32) * np.sqrt(2.0 / HIDDEN_DIM)
        b2 = jnp.zeros((NUM_EXPERTS, EMBED_DIM), dtype=jnp.float32)
        return {'x': x, 'gate_w': gate_w, 'w1': w1, 'b1': b1, 'w2': w2, 'b2': b2}
    _L0_ffn_all = _L0_ffn_setup()
    _L0_ffn_in = {k: v for k, v in _L0_ffn_all.items() if k in ('gate_w', 'w1', 'b1', 'w2', 'b2')}
    del _L0_ffn_all

    def _L1_attn_setup():
        import jax, jax.numpy as jnp
        import numpy as np
        B, T, C = (8, 512, 256)
        NL, LID = (12, 1)
        H = 4 * C

        def _ln(x, g, b):
            m = x.mean(-1, keepdims=True)
            v = ((x - m) ** 2).mean(-1, keepdims=True)
            return (x - m) * jax.lax.rsqrt(v + 1e-05) * g + b

        def _shift(x):
            return jnp.pad(x, ((0, 0), (1, 0), (0, 0)))[:, :-1]

        def _wkv(time_decay, time_first, k, v):
            w = -jnp.exp(time_decay)
            kt = jnp.moveaxis(k, 1, 0)
            vt = jnp.moveaxis(v, 1, 0)
            Bb, Cc = (k.shape[0], k.shape[2])
            init = (jnp.zeros((Bb, Cc), k.dtype), jnp.zeros((Bb, Cc), k.dtype), jnp.full((Bb, Cc), -1e+38, k.dtype))

            def step(carry, kv_t):
                aa, bb, pp = carry
                kk, vv = kv_t
                ww = time_first + kk
                p = jnp.maximum(pp, ww)
                e1 = jnp.exp(pp - p)
                e2 = jnp.exp(ww - p)
                out = (e1 * aa + e2 * vv) / (e1 * bb + e2)
                ww2 = pp + w
                p2 = jnp.maximum(ww2, kk)
                e1b = jnp.exp(ww2 - p2)
                e2b = jnp.exp(kk - p2)
                return ((e1b * aa + e2b * vv, e1b * bb + e2b, p2), out)
            _, out = jax.lax.scan(step, init, (kt, vt))
            return jnp.moveaxis(out, 0, 1)
        key = jax.random.key(seed)
        ks = jax.random.split(key, 8)
        f = lambda i, shape: 0.02 * jax.random.normal(ks[i], shape, jnp.float32)
        r01 = LID / (NL - 1)
        r10 = 1.0 - LID / NL
        h = np.arange(C, dtype=np.float64)
        decay = (-5 + 8 * (h / (C - 1)) ** (0.7 + 1.3 * r01)).astype(np.float32)
        zig = np.array([(i + 1) % 3 - 1 for i in range(C)]) * 0.5
        tfirst = (np.ones(C) * np.log(0.3) + zig).astype(np.float32)
        xpos = h / C
        tmk = (xpos ** r10).astype(np.float32)
        tmv = (xpos ** r10 + 0.3 * r01).astype(np.float32)
        tmr = (xpos ** (0.5 * r10)).astype(np.float32)
        cm = (xpos ** r10).astype(np.float32)
        return dict(x=jax.random.normal(ks[0], (B, T, C), jnp.float32), ln1_g=jnp.ones(C, jnp.float32), ln1_b=jnp.zeros(C, jnp.float32), ln2_g=jnp.ones(C, jnp.float32), ln2_b=jnp.zeros(C, jnp.float32), time_decay=jnp.asarray(decay), time_first=jnp.asarray(tfirst), time_mix_k=jnp.asarray(tmk), time_mix_v=jnp.asarray(tmv), time_mix_r=jnp.asarray(tmr), att_Wk=f(1, (C, C)), att_Wv=f(2, (C, C)), att_Wr=f(3, (C, C)), att_Wo=f(4, (C, C)), cm_k=jnp.asarray(cm), cm_r=jnp.asarray(cm), ffn_Wk=f(5, (H, C)), ffn_Wr=f(6, (C, C)), ffn_Wv=f(7, (C, H)))
    _L1_attn_all = _L1_attn_setup()
    _L1_attn_in = {k: v for k, v in _L1_attn_all.items() if k in ('ln1_g', 'ln1_b', 'ln2_g', 'ln2_b', 'time_decay', 'time_first', 'time_mix_k', 'time_mix_v', 'time_mix_r', 'att_Wk', 'att_Wv', 'att_Wr', 'att_Wo', 'cm_k', 'cm_r', 'ffn_Wk', 'ffn_Wr', 'ffn_Wv')}
    del _L1_attn_all

    def _L1_xattn_setup():
        import jax, jax.numpy as jnp
        import numpy as np
        B, S, D, H = (2, 512, 256, 16)
        HD = D // H
        SCALE = HD ** (-0.5)

        def _split_heads(x):
            b, s, _ = x.shape
            return x.reshape(b, s, H, HD).transpose(0, 2, 1, 3)
        key = jax.random.key(seed)
        ks = jax.random.split(key, 9)
        w = 0.02
        return {'query': jax.random.normal(ks[0], (B, S, D), jnp.float32), 'key': jax.random.normal(ks[1], (B, S, D), jnp.float32), 'value': jax.random.normal(ks[2], (B, S, D), jnp.float32), 'bias_struct': jax.random.uniform(ks[3], (B, S, S), jnp.float32, 0.0, 1.5), 'Wq': jax.random.normal(ks[4], (D, D), jnp.float32) * w, 'bq': jnp.zeros((D,), jnp.float32), 'Wk': jax.random.normal(ks[5], (D, D), jnp.float32) * w, 'bk': jnp.zeros((D,), jnp.float32), 'Wv': jax.random.normal(ks[6], (D, D), jnp.float32) * w, 'bv': jnp.zeros((D,), jnp.float32), 'Wo': jax.random.normal(ks[7], (D, D), jnp.float32) * w, 'bo': jnp.zeros((D,), jnp.float32), 'lambda_bias': jnp.array(1.0, jnp.float32)}
    _L1_xattn_all = _L1_xattn_setup()
    _L1_xattn_in = {k: v for k, v in _L1_xattn_all.items() if k in ('Wq', 'bq', 'Wk', 'bk', 'Wv', 'bv', 'Wo', 'bo', 'lambda_bias')}
    del _L1_xattn_all

    def _L1_ffn_setup():
        import jax, jax.numpy as jnp
        import numpy as np
        FP8_MAX = 448.0
        SCALE = 1.0
        _FP8_DTYPE = getattr(jnp, 'float8_e4m3fn', jnp.float16)

        def quantize_e4m3(t, scale):
            return jnp.clip(t / scale, -FP8_MAX, FP8_MAX).astype(_FP8_DTYPE)
        key = jax.random.key(seed)
        kx, kw = jax.random.split(key)
        B, N, C, F = (8, 1024, 256, 256)
        x = jax.random.normal(kx, (B, N, C), dtype=jnp.float32)
        weight = jax.random.normal(kw, (F, C), dtype=jnp.float32) * 0.02
        bias = jnp.zeros((F,), dtype=jnp.float32)
        return {'x': x, 'weight': weight, 'bias': bias}
    _L1_ffn_all = _L1_ffn_setup()
    _L1_ffn_in = {k: v for k, v in _L1_ffn_all.items() if k in ('weight', 'bias')}
    del _L1_ffn_all
    return {'x': x, 'ctx_1024': ctx_1024, 'fside_BxSxS2_0': fside_BxSxS2_0, 'mask_BxS2_if1': mask_BxS2_if1, 'L0_attn_q': _L0_attn_in['q'], 'L0_attn_k': _L0_attn_in['k'], 'L0_attn_log_decay': _L0_attn_in['log_decay'], 'L0_attn_norm_weight': _L0_attn_in['norm_weight'], 'L0_attn_o_w': _L0_attn_in['o_w'], 'L0_xattn_Wq': _L0_xattn_in['Wq'], 'L0_xattn_bq': _L0_xattn_in['bq'], 'L0_xattn_Wk': _L0_xattn_in['Wk'], 'L0_xattn_bk': _L0_xattn_in['bk'], 'L0_xattn_Wv': _L0_xattn_in['Wv'], 'L0_xattn_bv': _L0_xattn_in['bv'], 'L0_xattn_Wo': _L0_xattn_in['Wo'], 'L0_xattn_bo': _L0_xattn_in['bo'], 'L0_ffn_gate_w': _L0_ffn_in['gate_w'], 'L0_ffn_w1': _L0_ffn_in['w1'], 'L0_ffn_b1': _L0_ffn_in['b1'], 'L0_ffn_w2': _L0_ffn_in['w2'], 'L0_ffn_b2': _L0_ffn_in['b2'], 'L1_attn_ln1_g': _L1_attn_in['ln1_g'], 'L1_attn_ln1_b': _L1_attn_in['ln1_b'], 'L1_attn_ln2_g': _L1_attn_in['ln2_g'], 'L1_attn_ln2_b': _L1_attn_in['ln2_b'], 'L1_attn_time_decay': _L1_attn_in['time_decay'], 'L1_attn_time_first': _L1_attn_in['time_first'], 'L1_attn_time_mix_k': _L1_attn_in['time_mix_k'], 'L1_attn_time_mix_v': _L1_attn_in['time_mix_v'], 'L1_attn_time_mix_r': _L1_attn_in['time_mix_r'], 'L1_attn_att_Wk': _L1_attn_in['att_Wk'], 'L1_attn_att_Wv': _L1_attn_in['att_Wv'], 'L1_attn_att_Wr': _L1_attn_in['att_Wr'], 'L1_attn_att_Wo': _L1_attn_in['att_Wo'], 'L1_attn_cm_k': _L1_attn_in['cm_k'], 'L1_attn_cm_r': _L1_attn_in['cm_r'], 'L1_attn_ffn_Wk': _L1_attn_in['ffn_Wk'], 'L1_attn_ffn_Wr': _L1_attn_in['ffn_Wr'], 'L1_attn_ffn_Wv': _L1_attn_in['ffn_Wv'], 'L1_xattn_Wq': _L1_xattn_in['Wq'], 'L1_xattn_bq': _L1_xattn_in['bq'], 'L1_xattn_Wk': _L1_xattn_in['Wk'], 'L1_xattn_bk': _L1_xattn_in['bk'], 'L1_xattn_Wv': _L1_xattn_in['Wv'], 'L1_xattn_bv': _L1_xattn_in['bv'], 'L1_xattn_Wo': _L1_xattn_in['Wo'], 'L1_xattn_bo': _L1_xattn_in['bo'], 'L1_xattn_lambda_bias': _L1_xattn_in['lambda_bias'], 'L1_ffn_weight': _L1_ffn_in['weight'], 'L1_ffn_bias': _L1_ffn_in['bias']}

def reference(x, ctx_1024, fside_BxSxS2_0, mask_BxS2_if1, L0_attn_q, L0_attn_k, L0_attn_log_decay, L0_attn_norm_weight, L0_attn_o_w, L0_xattn_Wq, L0_xattn_bq, L0_xattn_Wk, L0_xattn_bk, L0_xattn_Wv, L0_xattn_bv, L0_xattn_Wo, L0_xattn_bo, L0_ffn_gate_w, L0_ffn_w1, L0_ffn_b1, L0_ffn_w2, L0_ffn_b2, L1_attn_ln1_g, L1_attn_ln1_b, L1_attn_ln2_g, L1_attn_ln2_b, L1_attn_time_decay, L1_attn_time_first, L1_attn_time_mix_k, L1_attn_time_mix_v, L1_attn_time_mix_r, L1_attn_att_Wk, L1_attn_att_Wv, L1_attn_att_Wr, L1_attn_att_Wo, L1_attn_cm_k, L1_attn_cm_r, L1_attn_ffn_Wk, L1_attn_ffn_Wr, L1_attn_ffn_Wv, L1_xattn_Wq, L1_xattn_bq, L1_xattn_Wk, L1_xattn_bk, L1_xattn_Wv, L1_xattn_bv, L1_xattn_Wo, L1_xattn_bo, L1_xattn_lambda_bias, L1_ffn_weight, L1_ffn_bias):
    import jax
    import jax.numpy as jnp

    def _L0_attn_ref(x, q, k, log_decay, norm_weight, o_w):
        import jax, jax.numpy as jnp
        import numpy as np
        H = 16
        EPS = 1e-06
        b, n, dm = x.shape
        dh = dm // H
        qh = q.reshape(H, dh)
        kh = k.reshape(H, dh)
        v = x.reshape(b, n, H, dh)
        lam = jax.nn.sigmoid(log_decay)

        def step(S, v_t):
            S = lam[None, :, None, None] * S + kh[None, :, :, None] * v_t[:, :, None, :]
            o_t = jnp.einsum('hd,bhdv->bhv', qh, S)
            return (S, o_t)
        S0 = jnp.zeros((b, H, dh, dh), dtype=x.dtype)
        _, o = jax.lax.scan(step, S0, jnp.moveaxis(v, 1, 0))
        o = jnp.moveaxis(o, 0, 1).reshape(b, n, dm)
        o = o * jax.lax.rsqrt(jnp.mean(o * o, axis=-1, keepdims=True) + EPS) * norm_weight
        return o @ o_w.T

    def _L0_xattn_ref(q, k, v, mask, Wq, bq, Wk, bk, Wv, bv, Wo, bo):
        import jax, jax.numpy as jnp
        import numpy as np
        D_MODEL = 256
        N_HEADS = 16
        D_K = D_MODEL // N_HEADS
        B, L = (2, 512)

        def _dense_bf16(x, W, b):
            return jnp.matmul(x.astype(jnp.bfloat16), W.astype(jnp.bfloat16)) + b.astype(jnp.bfloat16)

        def _attention(q, k, v, mask):
            Lq, Ls, dk = (q.shape[2], k.shape[2], q.shape[3])
            scale = 1.0 / np.sqrt(dk)
            scores = jnp.einsum('bhqd,bhkd->bhqk', q, k) * scale
            causal = jnp.tril(jnp.ones((Lq, Ls), bool))
            full_mask = causal[None, None] & (mask[:, None, None, :] > 0)
            scores = jnp.where(full_mask, scores, -jnp.inf)
            p = jax.nn.softmax(scores, axis=-1)
            return jnp.einsum('bhqk,bhkd->bhqd', p, v)
        query = _dense_bf16(q, Wq, bq).astype(jnp.float32)
        key_p = _dense_bf16(k, Wk, bk).astype(jnp.float32)
        val_p = _dense_bf16(v, Wv, bv).astype(jnp.float32)
        Bb, Lt, _ = query.shape
        Ls = key_p.shape[1]
        query = query.reshape(Bb, Lt, N_HEADS, D_K).transpose(0, 2, 1, 3)
        key_p = key_p.reshape(Bb, Ls, N_HEADS, D_K).transpose(0, 2, 1, 3)
        val_p = val_p.reshape(Bb, Ls, N_HEADS, D_K).transpose(0, 2, 1, 3)
        x = _attention(query, key_p, val_p, mask)
        x = x.transpose(0, 2, 1, 3).reshape(Bb, Lt, D_MODEL)
        out = _dense_bf16(x, Wo, bo)
        return out.astype(jnp.float32)

    def _L0_ffn_ref(x, gate_w, w1, b1, w2, b2):
        import jax, jax.numpy as jnp
        import numpy as np
        EMBED_DIM = 256
        HIDDEN_DIM = 1024
        NUM_EXPERTS = 8
        TOP_K = 2
        orig_shape = x.shape
        xt = x.reshape(-1, EMBED_DIM)
        logits = xt @ gate_w.T
        probs = jax.nn.softmax(logits, axis=-1)
        top_w, top_i = jax.lax.top_k(probs, TOP_K)
        top_w = top_w / (top_w.sum(axis=-1, keepdims=True) + 1e-09)
        h = jnp.einsum('td,ndh->tnh', xt, w1) + b1
        h = jax.nn.gelu(h, approximate=False)
        out_all = jnp.einsum('tnh,nhd->tnd', h, w2) + b2
        sel = jnp.take_along_axis(out_all, top_i[:, :, None], axis=1)
        out = (sel * top_w[:, :, None]).sum(axis=1)
        return out.reshape(orig_shape)

    def _L1_attn_ref(x, ln1_g, ln1_b, ln2_g, ln2_b, time_decay, time_first, time_mix_k, time_mix_v, time_mix_r, att_Wk, att_Wv, att_Wr, att_Wo, cm_k, cm_r, ffn_Wk, ffn_Wr, ffn_Wv):
        import jax, jax.numpy as jnp
        import numpy as np
        B, T, C = (8, 512, 256)
        NL, LID = (12, 1)
        H = 4 * C

        def _ln(x, g, b):
            m = x.mean(-1, keepdims=True)
            v = ((x - m) ** 2).mean(-1, keepdims=True)
            return (x - m) * jax.lax.rsqrt(v + 1e-05) * g + b

        def _shift(x):
            return jnp.pad(x, ((0, 0), (1, 0), (0, 0)))[:, :-1]

        def _wkv(time_decay, time_first, k, v):
            w = -jnp.exp(time_decay)
            kt = jnp.moveaxis(k, 1, 0)
            vt = jnp.moveaxis(v, 1, 0)
            Bb, Cc = (k.shape[0], k.shape[2])
            init = (jnp.zeros((Bb, Cc), k.dtype), jnp.zeros((Bb, Cc), k.dtype), jnp.full((Bb, Cc), -1e+38, k.dtype))

            def step(carry, kv_t):
                aa, bb, pp = carry
                kk, vv = kv_t
                ww = time_first + kk
                p = jnp.maximum(pp, ww)
                e1 = jnp.exp(pp - p)
                e2 = jnp.exp(ww - p)
                out = (e1 * aa + e2 * vv) / (e1 * bb + e2)
                ww2 = pp + w
                p2 = jnp.maximum(ww2, kk)
                e1b = jnp.exp(ww2 - p2)
                e2b = jnp.exp(kk - p2)
                return ((e1b * aa + e2b * vv, e1b * bb + e2b, p2), out)
            _, out = jax.lax.scan(step, init, (kt, vt))
            return jnp.moveaxis(out, 0, 1)
        xa = _ln(x, ln1_g, ln1_b)
        xx = _shift(xa)
        xk = xa * time_mix_k + xx * (1 - time_mix_k)
        xv = xa * time_mix_v + xx * (1 - time_mix_v)
        xr = xa * time_mix_r + xx * (1 - time_mix_r)
        k = jnp.einsum('btc,oc->bto', xk, att_Wk)
        v = jnp.einsum('btc,oc->bto', xv, att_Wv)
        r = jnp.einsum('btc,oc->bto', xr, att_Wr)
        rwkv = jax.nn.sigmoid(r) * _wkv(time_decay, time_first, k, v)
        x = x + jnp.einsum('bto,co->btc', rwkv, att_Wo)
        xc = _ln(x, ln2_g, ln2_b)
        xx2 = _shift(xc)
        xk2 = xc * cm_k + xx2 * (1 - cm_k)
        xr2 = xc * cm_r + xx2 * (1 - cm_r)
        kk = jnp.square(jax.nn.relu(jnp.einsum('btc,hc->bth', xk2, ffn_Wk)))
        kv = jnp.einsum('bth,ch->btc', kk, ffn_Wv)
        rkv = jax.nn.sigmoid(jnp.einsum('btc,oc->bto', xr2, ffn_Wr)) * kv
        return x + rkv

    def _L1_xattn_ref(query, key, value, bias_struct, Wq, bq, Wk, bk, Wv, bv, Wo, bo, lambda_bias):
        import jax, jax.numpy as jnp
        import numpy as np
        B, S, D, H = (2, 512, 256, 16)
        HD = D // H
        SCALE = HD ** (-0.5)

        def _split_heads(x):
            b, s, _ = x.shape
            return x.reshape(b, s, H, HD).transpose(0, 2, 1, 3)
        Q = _split_heads(query @ Wq.T + bq)
        K = _split_heads(key @ Wk.T + bk)
        V = _split_heads(value @ Wv.T + bv)
        scores = jnp.einsum('bhqd,bhkd->bhqk', Q, K) * SCALE
        scores = scores + lambda_bias * bias_struct[:, None, :, :]
        attn = jax.nn.softmax(scores, axis=-1)
        out = jnp.einsum('bhqk,bhkd->bhqd', attn, V)
        out = out.transpose(0, 2, 1, 3).reshape(query.shape[0], query.shape[1], D)
        return out @ Wo.T + bo

    def _L1_ffn_ref(x, weight, bias):
        import jax, jax.numpy as jnp
        import numpy as np
        FP8_MAX = 448.0
        SCALE = 1.0
        _FP8_DTYPE = getattr(jnp, 'float8_e4m3fn', jnp.float16)

        def quantize_e4m3(t, scale):
            return jnp.clip(t / scale, -FP8_MAX, FP8_MAX).astype(_FP8_DTYPE)
        B, N, C = x.shape
        x2d = x.reshape(B * N, C)
        x_mat = quantize_e4m3(x2d, SCALE).astype(jnp.float16)
        w_mat = quantize_e4m3(weight, SCALE).astype(jnp.float16)
        out2d = (x_mat @ w_mat.T).astype(jnp.float32) * (SCALE * SCALE)
        out2d = out2d + bias
        return out2d.reshape(B, N, -1)
    x = x + _L0_attn_ref(_layernorm(x, axis=-1), L0_attn_q, L0_attn_k, L0_attn_log_decay, L0_attn_norm_weight, L0_attn_o_w)
    x = x + _L0_xattn_ref(_layernorm(x, axis=-1), ctx_1024, ctx_1024, mask_BxS2_if1, L0_xattn_Wq, L0_xattn_bq, L0_xattn_Wk, L0_xattn_bk, L0_xattn_Wv, L0_xattn_bv, L0_xattn_Wo, L0_xattn_bo)
    x = x + _L0_ffn_ref(_layernorm(x, axis=-1), L0_ffn_gate_w, L0_ffn_w1, L0_ffn_b1, L0_ffn_w2, L0_ffn_b2)
    x = x + _L1_attn_ref(_layernorm(x, axis=-1), L1_attn_ln1_g, L1_attn_ln1_b, L1_attn_ln2_g, L1_attn_ln2_b, L1_attn_time_decay, L1_attn_time_first, L1_attn_time_mix_k, L1_attn_time_mix_v, L1_attn_time_mix_r, L1_attn_att_Wk, L1_attn_att_Wv, L1_attn_att_Wr, L1_attn_att_Wo, L1_attn_cm_k, L1_attn_cm_r, L1_attn_ffn_Wk, L1_attn_ffn_Wr, L1_attn_ffn_Wv)
    x = x + _L1_xattn_ref(_layernorm(x, axis=-1), ctx_1024, ctx_1024, fside_BxSxS2_0, L1_xattn_Wq, L1_xattn_bq, L1_xattn_Wk, L1_xattn_bk, L1_xattn_Wv, L1_xattn_bv, L1_xattn_Wo, L1_xattn_bo, L1_xattn_lambda_bias)
    x = x + _L1_ffn_ref(_layernorm(x, axis=-1), L1_ffn_weight, L1_ffn_bias)
    return x

_drawn_inputs = setup_inputs


def setup_inputs(seed=0):
    import zlib

    import numpy as np

    out = dict(_drawn_inputs(seed))
    spreads = {'L0_attn_norm_weight': (1.0, 0.2),
     'L0_xattn_bq': (0.0, 0.633),
     'L0_xattn_bk': (0.0, 2.0),
     'L0_xattn_bv': (0.0, 0.1),
     'L0_xattn_bo': (0.0, 0.1),
     'L0_ffn_b1': (0.0, 0.1),
     'L0_ffn_b2': (0.0, 0.1),
     'L1_attn_ln1_g': (1.0, 0.6),
     'L1_attn_ln1_b': (0.0, 0.8),
     'L1_attn_ln2_g': (1.0, 0.6),
     'L1_attn_ln2_b': (0.0, 0.8),
     'L1_xattn_bq': (0.0, 2.0),
     'L1_xattn_bk': (0.0, 2.0),
     'L1_xattn_bv': (0.0, 2.0),
     'L1_xattn_bo': (0.0, 2.0),
     'L1_ffn_bias': (0.0, 2.0)}
    factors = {'fside_BxSxS2_0': 190.488,
     'L0_xattn_Wq': 3.395,
     'L1_attn_time_decay': 7.125,
     'L1_attn_time_first': 8.0,
     'L1_attn_time_mix_k': 8.0,
     'L1_attn_time_mix_v': 8.0,
     'L1_attn_time_mix_r': 8.0,
     'L1_attn_att_Wk': 8.0,
     'L1_attn_att_Wv': 4.595,
     'L1_attn_att_Wr': 8.0,
     'L1_attn_att_Wo': 4.607,
     'L1_attn_cm_k': 7.469,
     'L1_attn_cm_r': 8.0,
     'L1_attn_ffn_Wk': 4.749,
     'L1_attn_ffn_Wr': 8.0,
     'L1_attn_ffn_Wv': 4.243,
     'L1_xattn_Wq': 64.0,
     'L1_xattn_Wk': 64.0,
     'L1_xattn_Wv': 21.464,
     'L1_xattn_Wo': 8.0,
     'L1_ffn_weight': 57.23}
    for name, (base, spread) in spreads.items():
        noise = np.random.default_rng([zlib.crc32(name.encode()), seed]).standard_normal(out[name].shape)
        drawn = base * np.exp(spread * noise) if base else spread * noise
        out[name] = jnp.asarray(drawn.astype(out[name].dtype))
    for name, factor in factors.items():
        out[name] = (out[name] * factor).astype(out[name].dtype)
    return out
```

```python
from contextlib import ExitStack

import concourse.bass as bass
from concourse import mybir

F32 = mybir.dt.float32
BF16 = mybir.dt.bfloat16
F16 = mybir.dt.float16
FP8 = mybir.dt.float8e4
I32 = mybir.dt.int32
U32 = mybir.dt.uint32
ALU = mybir.AluOpType
ACT = mybir.ActivationFunctionType
AX = mybir.AxisListType

P = 128
B = 16
S = 256
D = 256
H = 16
DH = D // H
NT = B * S // P
TB = S // P
DC = D // P
E = 8
HID = 1024
HC = HID // P
LN_EPS = 1e-5
HEAD = 1


class Chain:

    def __init__(self, eng, sem):
        self.eng, self.sem, self.n = eng, sem, 0

    def done(self, ins):
        self.n += 1
        return ins.then_inc(self.sem, 1)

    def wait(self):
        self.eng.wait_ge(self.sem, self.n)

    def close(self):
        self.wait()
        self.eng.sem_clear(self.sem)
        self.n = 0


def wait_alone(eng, stood, *waits):
    for sem, n in waits:
        eng.wait_ge(sem, n + HEAD)
    eng.sem_inc(stood, 1)


def make_identity(pool, ident, sem, dtype_one=1.0):
    pool.memset(ident, 0.0).then_inc(sem, 1)
    pool.wait_ge(sem, 1 + HEAD)
    pool.affine_select(out=ident, in_=ident, compare_op=ALU.not_equal, fill=1.0, base=0,
                       pattern=[[-1, P]], channel_multiplier=1).then_inc(sem, 1)


def transpose_blocks(pe, blocks, banks, ident, turned, freed):
    for g in range(0, len(blocks), 4):
        n = g // 4
        if n >= len(banks):
            pe.wait_ge(freed, n - len(banks) + 1 + HEAD)
        for j, block in enumerate(blocks[g:g + 4]):
            last = pe.transpose(banks[n % len(banks)][:, j * P:(j + 1) * P], block, ident)
        last.then_inc(turned, 1)


def evacuate_blocks(act, dests, banks, turned, freed):
    for n, dest in enumerate(dests):
        act.wait_ge(turned, n + 1 + HEAD)
        act.activation(dest, banks[n % len(banks)][:, 0:dest.shape[-1]], ACT.Copy).then_inc(freed, 1)


def layer_norm_stats(dve, chain, src, stats, aggr, measured):
    for t in range(TB):
        chain.done(dve.bn_stats(stats[:, t, :], src(t)))
    chain.wait()
    for t in range(TB):
        last = dve.bn_aggr(aggr[:, t, :], stats[:, t, :])
    last.then_inc(measured, 1)


def inverse_root(pool, out, in_, scale, add, minus_half, summed, ready, turn, stood):
    pool.tensor_scalar(out, in_, scale, add, ALU.mult, ALU.add).then_inc(summed, 1)
    wait_alone(pool, stood, (summed, turn + 1))
    pool.tensor_tensor(out, out, minus_half, ALU.pow).then_inc(ready, 1)


def layer_norm_apply(dve, src, out, aggr, rstd, normed):
    for t in range(TB):
        last = dve.tensor_scalar(out(t), src(t), aggr[:, t, 0:1], rstd[:, t:t + 1], ALU.subtract, ALU.mult)
    last.then_inc(normed, 1)


def sequences(eng):
    with eng.Fori(0, B // 2) as i:
        for s in range(2):
            yield 2 * i + s, s


def tile_of(X, b, t):
    return X[:, bass.ds(b * TB + t, 1), :].rearrange("p a d -> p (a d)")


OWN = ("chain_", "stood_", "loaded", "ctx_in", "raw_in", "zeroed", "scattered")


class Phase:

    def __init__(self, nc, name):
        self.nc, self.name, self.ctx, self.sems = nc, name, ExitStack(), []
        self.no_head = []

    def __enter__(self):
        self.ctx.__enter__()
        return self

    def __exit__(self, *e):
        self.ctx.__exit__(*e)
        self.nc.clear_and_free_semaphores(self.sems)

    def sb(self, name, shape, dt=F32):
        return self.ctx.enter_context(self.nc.sbuf_tensor(f"{self.name}_{name}", shape, dt))

    def ps(self, name, shape=(P, 512), dt=F32):
        return self.ctx.enter_context(self.nc.psum_tensor(f"{self.name}_{name}", list(shape), dt))

    def sem(self, name):
        self.sems.append(self.nc.alloc_semaphore(f"{self.name}_{name}"))
        return self.sems[-1]

    def own(self, name):
        sem = self.sem(name)
        self.no_head.append(sem)
        return sem

    def block(self):
        self.nc.all_engine_barrier()
        for sem in self.sems:
            if sem not in self.no_head:
                self.nc.sync.sem_inc(sem, HEAD)
        self.nc.all_engine_barrier()
        return self.ctx.enter_context(self.nc.Block())


def flat(ap):
    return ap.rearrange("p a b -> p (a b)")


def columns(vec):
    return vec.rearrange("(c p) -> p c", p=P)


def load_x(nc, x, X):
    x_v = x.rearrange("b (t p) d -> p (b t) d", p=P)
    with Phase(nc, "load") as ph:
        arrived = ph.own("arrived")
        block = ph.block()

        @block.sync
        def _(sp):
            for q in range(4):
                sp.dma_start(X[:, 8 * q:8 * q + 8, :], x_v[:, 8 * q:8 * q + 8, :]).then_inc(arrived, 16)
            sp.wait_ge(arrived, 64)


def store_x(nc, X, out):
    out_v = out.rearrange("b (t p) d -> p (b t) d", p=P)
    with Phase(nc, "store") as ph:
        stored = ph.own("stored")
        block = ph.block()

        @block.sync
        def _(sp):
            for q in range(4):
                sp.dma_start(out_v[:, 8 * q:8 * q + 8, :], X[:, 8 * q:8 * q + 8, :]).then_inc(stored, 16)
            sp.wait_ge(stored, 64)


def decay_attention(nc, ins, X):
    with Phase(nc, "dec") as ph:
        ident = ph.sb("ident", [P, P])
        groups = ph.sb("groups", [P, P])
        ones = ph.sb("ones", [P, 1])
        w_nat = ph.sb("w_nat", [P, DC, D])
        wt = ph.sb("wt", [P, DC, D])
        q_col = ph.sb("q_col", [P, DC])
        k_col = ph.sb("k_col", [P, DC])
        qk = ph.sb("qk", [P, DC])
        nw = ph.sb("nw", [P, DC])
        ld = ph.sb("ld", [P, DC])
        lam = ph.sb("lam", [P, DC])
        coef = ph.sb("coef", [P, DC])
        xn = ph.sb("xn", [P, 2, TB, D])
        stats = ph.sb("stats", [P, TB, 6])
        aggr = ph.sb("aggr", [P, TB, 2])
        rstd = ph.sb("rstd", [P, TB])
        v = ph.sb("v", [P, 2, DC, S])
        o = ph.sb("o", [P, 2, DC, S])
        osq = ph.sb("osq", [P, 2, DC, S])
        sum_sq = ph.sb("sum_sq", [P, TB])
        rms = ph.sb("rms", [P, TB])
        minus_half = ph.sb("minus_half", [P, TB])
        p_t = [ph.ps(f"p_t{i}") for i in range(2)]
        p_y = [ph.ps(f"p_y{i}") for i in range(2)]
        p_m = ph.ps("p_m")

        loaded = ph.own("loaded")
        ident_ready, groups_ready = ph.sem("ident_ready"), ph.sem("groups_ready")
        turned, freed = ph.sem("turned"), ph.sem("freed")
        qk_ready, coef_sum, consts = ph.sem("qk_ready"), ph.sem("coef_sum"), ph.sem("consts")
        wt_ready = ph.sem("wt_ready")
        normed, turned_x, v_ready = ph.sem("normed"), ph.sem("turned_x"), ph.sem("v_ready")
        scanned, squared, y_ready, added = ph.sem("scanned"), ph.sem("squared"), ph.sem("y_ready"), ph.sem("added")
        measured, rstd_ready = ph.sem("measured"), ph.sem("rstd_ready")
        var_eps, mean_eps = ph.sem("var_eps"), ph.sem("mean_eps")
        sum_sq_ready, rms_ready = ph.sem("sum_sq_ready"), ph.sem("rms_ready")
        stood_v, stood_p = ph.own("stood_v"), ph.own("stood_p")
        chain_v, chain_a = ph.own("chain_v"), ph.own("chain_a")
        block = ph.block()

        @block.sync
        def _(sp):
            sp.dma_start(w_nat[:, :, :], ins["L0_attn_o_w"].rearrange("(c p) d -> p c d", p=P)).then_inc(loaded, 16)
            with nc.allow_non_contiguous_dma(reason="vectors of 256 numbers"):
                for dst, name in ((q_col, "L0_attn_q"), (k_col, "L0_attn_k"), (nw, "L0_attn_norm_weight")):
                    sp.dma_start(dst[:, :], columns(ins[name])).then_inc(loaded, 16)
                decay = ins["L0_attn_log_decay"].rearrange("(c h) -> h c", c=DC)
                for h in range(P // DH):
                    sp.dma_start(ld[h * DH:(h + 1) * DH, :],
                                 decay[h:h + 1, :].broadcast_to([DH, DC])).then_inc(loaded, 16)

        n_loads = 4 + P // DH

        @block.gpsimd
        def _(pool):
            make_identity(pool, ident[:, :], ident_ready)
            pool.memset(ones[:, :], 1.0).then_inc(groups_ready, 1)
            pool.memset(groups[:, :], 1.0).then_inc(groups_ready, 1)
            pool.memset(minus_half[:, :], -0.5).then_inc(groups_ready, 1)
            pool.wait_ge(groups_ready, 3 + HEAD)
            g3 = groups[:, :].rearrange("p (h r) -> p h r", r=DH)
            pool.affine_select(out=g3, in_=g3, compare_op=ALU.is_ge, fill=0.0, base=0,
                               pattern=[[-DH, P // DH], [0, DH]], channel_multiplier=1).then_inc(groups_ready, 1)
            pool.wait_ge(groups_ready, 4 + HEAD)
            pool.affine_select(out=g3, in_=g3, compare_op=ALU.is_ge, fill=0.0, base=DH - 1,
                               pattern=[[DH, P // DH], [0, DH]], channel_multiplier=-1).then_inc(groups_ready, 1)

            for b, s in sequences(pool):
                wait_alone(pool, stood_p, (measured, b + 1))
                inverse_root(pool, rstd[:, :], aggr[:, :, 1], 1.0, LN_EPS, minus_half[:, :], var_eps, rstd_ready, b, stood_p)
                wait_alone(pool, stood_p, (sum_sq_ready, b + 1))
                inverse_root(pool, rms[:, :], sum_sq[:, :], 1.0 / D, 1e-6, minus_half[:, :], mean_eps, rms_ready, b, stood_p)

        @block.tensor
        def _(pe):
            pe.wait_ge(loaded, 16 * n_loads)
            pe.wait_ge(ident_ready, 2 + HEAD)
            for ct in range(DC):
                for ot in range(DC):
                    last = pe.transpose(p_t[0][:, (ct * DC + ot) * P:(ct * DC + ot + 1) * P],
                                        w_nat[:, ot, ct * P:(ct + 1) * P], ident[:, :])
            last.then_inc(turned, 1)
            pe.wait_ge(groups_ready, 5 + HEAD)
            pe.wait_ge(qk_ready, 1 + HEAD)
            pe.matmul(p_t[1][:, 0:DC], groups[:, :], qk[:, :], start=True, stop=True).then_inc(coef_sum, 1)
            pe.wait_ge(wt_ready, DC + HEAD)
            pe.wait_ge(consts, 1 + HEAD)
            for b, s in sequences(pe):
                pe.wait_ge(normed, b + 1 + HEAD)
                pe.wait_ge(v_ready, b + HEAD)
                for c in range(DC):
                    for t in range(TB):
                        last = pe.transpose(p_t[0][:, c * S + t * P:c * S + (t + 1) * P],
                                            xn[:, s, t, c * P:(c + 1) * P], ident[:, :])
                last.then_inc(turned_x, 1)
                pe.wait_ge(scanned, b + 1 + HEAD)
                pe.wait_ge(squared, b + 1 + HEAD)
                pe.wait_ge(added, b + HEAD)
                for t in range(TB):
                    for c in range(DC):
                        last = pe.matmul(p_m[:, t:t + 1], osq[:, s, c, t * P:(t + 1) * P], ones[:, :],
                                         start=(c == 0), stop=(c == DC - 1))
                for t in range(TB):
                    for c in range(DC):
                        last = pe.matmul(p_y[0][:, t * D:(t + 1) * D], o[:, s, c, t * P:(t + 1) * P],
                                         wt[:, c, :], start=(c == 0), stop=(c == DC - 1))
                last.then_inc(y_ready, 1)

        @block.scalar
        def _(act):
            act.wait_ge(loaded, 16 * n_loads)
            act.activation(lam[:, :], ld[:, :], ACT.Exp, scale=-1.0).then_inc(chain_a, 1)
            act.wait_ge(turned, 1 + HEAD)
            for c in range(DC):
                act.activation(wt[:, c, :], p_t[0][:, c * D:(c + 1) * D], ACT.Copy, scale=nw[:, c:c + 1]).then_inc(wt_ready, 1)
            act.wait_ge(consts, 1 + HEAD)
            for b, s in sequences(act):
                act.wait_ge(turned_x, b + 1 + HEAD)
                act.wait_ge(scanned, b + HEAD)
                for c in range(DC):
                    last = act.activation(v[:, s, c, :], p_t[0][:, c * S:(c + 1) * S], ACT.Copy, scale=coef[:, c:c + 1])
                last.then_inc(v_ready, 1)
                act.wait_ge(scanned, b + 1 + HEAD)
                act.wait_ge(y_ready, b + HEAD)
                act.activation(osq[:, s, :, :], o[:, s, :, :], ACT.Square).then_inc(squared, 1)

        @block.vector
        def _(dve):
            dve.wait_ge(loaded, 16 * n_loads)
            dve.tensor_tensor(qk[:, :], q_col[:, :], k_col[:, :], ALU.mult).then_inc(qk_ready, 1)
            dve.wait_ge(chain_a, 1)
            chain = Chain(dve, chain_v)
            chain.done(dve.tensor_scalar(lam[:, :], lam[:, :], 1.0, None, ALU.add))
            chain.wait()
            chain.done(dve.reciprocal(lam[:, :], lam[:, :]))
            dve.wait_ge(coef_sum, 1 + HEAD)
            dve.tensor_copy(coef[:, :], p_t[1][:, 0:DC]).then_inc(consts, 1)
            chain.close()
            for b, s in sequences(dve):
                layer_norm_stats(dve, chain, lambda t: tile_of(X, b, t), stats, aggr, measured)
                dve.wait_ge(rstd_ready, b + 1 + HEAD)
                layer_norm_apply(dve, lambda t: tile_of(X, b, t), lambda t: xn[:, s, t, :], aggr, rstd, normed)
                dve.wait_ge(v_ready, b + 1 + HEAD)
                dve.wait_ge(y_ready, b + HEAD)
                for c in range(DC):
                    last = dve.tensor_tensor_scan(o[:, s, c, :], lam[:, c:c + 1].broadcast_to([P, S]),
                                                  v[:, s, c, :], 0.0, ALU.mult, ALU.add)
                last.then_inc(scanned, 1)
                dve.wait_ge(y_ready, b + 1 + HEAD)
                dve.tensor_copy(sum_sq[:, :], p_m[:, 0:TB]).then_inc(sum_sq_ready, 1)
                dve.wait_ge(rms_ready, b + 1 + HEAD)
                for t in range(TB):
                    last = dve.scalar_tensor_tensor(tile_of(X, b, t), p_y[0][:, t * D:(t + 1) * D], rms[:, t:t + 1],
                                                    tile_of(X, b, t), ALU.mult, ALU.add)
                last.then_inc(added, 1)
                wait_alone(dve, stood_v, (added, b + 1))
                chain.close()


PAIRS = H // 2
UNITS = TB * PAIRS
OFF = 1e30
VW = DH + 1


def cross_attention(nc, ins, X, layer, causal):
    low = causal
    DT = BF16 if low else F32
    name = f"L{layer}_xattn_"
    with Phase(nc, f"xa{layer}") as ph:
        ident = ph.sb("ident", [P, P], F32)
        ident_d = ph.sb("ident_d", [P, P], DT) if low else ident
        w_nat = ph.sb("w_nat", [P, 4, DC, D])
        w = ph.sb("w", [P, 4, DC, D], DT)
        cols = ph.sb("cols", [P, 2, DC])
        cols_d = ph.sb("cols_d", [P, 2, DC])
        rows = ph.sb("rows", [P, 2, D])
        rows_d = ph.sb("rows_d", [P, 2, D], DT) if low else rows
        side = ph.sb("side", [P, 2, 4])
        parity = ph.sb("parity", [P, 2])
        q_bias = ph.sb("q_bias", [P, DC, 2])
        lam_b = ph.sb("lam_b", [P, 1])
        minus_half = ph.sb("minus_half", [P, TB])
        stats = ph.sb("stats", [P, TB, 6])
        aggr = ph.sb("aggr", [P, TB, 2])
        rstd = ph.sb("rstd", [P, TB])
        ctx = ph.sb("ctx", [P, 2, TB, D])
        ctx_d = ph.sb("ctx_d", [P, TB, D], DT) if low else None
        xn = ph.sb("xn", [P, TB, D], DT)
        xT = ph.sb("xT", [P, DC, S], DT)
        cT = ph.sb("cT", [P, DC, S], DT)
        raw = ph.sb("raw", [P, 2, S], I32) if causal else ph.sb("raw", [P, 2, TB, S])
        key_off = ph.sb("key_off", [P, 2, S]) if causal else None
        neg = ph.sb("neg", [P, 2, TB, S])
        q_r = ph.sb("q_r", [P, DC, S], DT) if low else None
        q_f = ph.sb("q_f", [P, DC, S], DT) if low else None
        k_r = ph.sb("k_r", [P, DC, S], DT) if low else None
        v_r = ph.sb("v_r", [P, TB, D], DT) if low else None
        v_f = ph.sb("v_f", [P, TB, D], DT) if low else None
        q = ph.sb("q", [P, 2, DC, S], DT)
        k = ph.sb("k", [P, DC, S], DT)
        v = ph.sb("v", [P, TB, H, VW])
        sc = ph.sb("sc", [P, 2, 2, S])
        nmax = ph.sb("nmax", [P, 2, 2])
        pr = ph.sb("pr", [P, 2, 2, S])
        prT = ph.sb("prT", [P, 2, 2, TB, P])
        inv = ph.sb("inv", [P, TB, H])
        o = ph.sb("o", [P, TB, D], DT)
        oT = ph.sb("oT", [P, DC, S], DT)
        y_r = ph.sb("y_r", [P, TB, D], DT) if low else None
        y_f = ph.sb("y_f", [P, TB, D], DT if low else F32)
        p_a = [ph.ps(f"p_a{i}") for i in range(2)]
        p_ad = [a[:, :].bitcast(BF16)[:, 0:512] if low else a for a in p_a]
        p_s = [ph.ps(f"p_s{i}") for i in range(2)]
        p_p = [ph.ps(f"p_p{i}") for i in range(2)]
        p_o = [ph.ps(f"p_o{i}") for i in range(2)]

        names = ("loaded_w loaded_c ctx_in raw_in ident_ready turned freed consts cast ones_set "
                 "measured var_eps rstd_ready normed turned_x x_ready c_ready projected qk_ready v_ready "
                 "off_ready neg_ready scored shifted exped p_turned p_copied_a p_copied_v pv o_ready turned_o oT_ready y_ready y_read added "
                 "chain_v chain_a chain_p rounded stood_v stood_p")
        sems = {n: ph.own(n) if n.startswith(OWN) else ph.sem(n) for n in names.split()}
        (loaded_w, loaded_c, ctx_in, raw_in, ident_ready, turned, freed, consts, cast, ones_set,
         measured, var_eps, rstd_ready, normed, turned_x, x_ready, c_ready, projected, qk_ready, v_ready,
         off_ready, neg_ready, scored, shifted, exped, p_turned, p_copied_a, p_copied_v, pv, o_ready, turned_o, oT_ready, y_ready, y_read, added,
         chain_v, chain_a, chain_p, rounded, stood_v, stood_p) = (sems[n] for n in names.split())
        block = ph.block()

        def keys(t):
            return (t + 1) * P if causal else S

        @block.sync
        def _(sp):
            for n, m in enumerate(("Wq", "Wk", "Wv", "Wo")):
                sp.dma_start(w_nat[:, n, :, :], ins[name + m].rearrange("(c p) d -> p c d", p=P)).then_inc(loaded_w, 16)
            with nc.allow_non_contiguous_dma(reason="vectors of 256 numbers"):
                for n, m in enumerate(("bq", "bk")):
                    sp.dma_start(cols[:, n, :], columns(ins[name + m])).then_inc(loaded_c, 16)
                for n, m in enumerate(("bv", "bo")):
                    sp.dma_start(rows[:, n, :], ins[name + m].partition_broadcast(P)).then_inc(loaded_c, 16)
                if not causal:
                    sp.dma_start(lam_b[:, :], ins["L1_xattn_lambda_bias"].partition_broadcast(P)).then_inc(loaded_c, 16)
            for b, s in sequences(sp):
                sp.wait_ge(c_ready, b + HEAD)
                sp.wait_ge(neg_ready, b + HEAD)
                sp.dma_start(ctx[:, s, :, :], ins["ctx_1024"][bass.ds(b, 1), :, :].rearrange("a (t p) d -> p (a t) d", p=P)).then_inc(ctx_in, 16)
                if causal:
                    sp.dma_start(raw[:, s, :], ins["mask_BxS2_if1"][bass.ds(b, 1), :].rearrange("a k -> (a k)").partition_broadcast(P)).then_inc(raw_in, 16)
                else:
                    sp.dma_start(raw[:, s, :, :], ins["fside_BxSxS2_0"][bass.ds(b, 1), :, :].rearrange("a (t p) k -> p (a t) k", p=P)).then_inc(raw_in, 16)

        n_cols = 4 if causal else 5

        @block.gpsimd
        def _(pool):
            make_identity(pool, ident[:, :], ident_ready)
            chain = Chain(pool, chain_p)
            pool.wait_ge(ident_ready, 2 + HEAD)
            if low:
                chain.done(pool.tensor_copy(ident_d[:, :], ident[:, :]))
            chain.done(pool.memset(minus_half[:, :], -0.5))
            chain.done(pool.memset(v[:, :, :, :], 1.0))
            chain.done(pool.memset(side[:, :, :], -1.0 / DH ** 0.5))
            chain.wait()
            for n in range(2):
                chain.done(pool.affine_select(out=side[:, n, :], in_=side[:, n, :], compare_op=ALU.is_ge, fill=0.0,
                                              base=-DH * n, pattern=[[-2 * DH, 4]], channel_multiplier=1))
            chain.wait()
            for n in range(2):
                chain.done(pool.affine_select(out=side[:, n, :], in_=side[:, n, :], compare_op=ALU.is_ge, fill=0.0,
                                              base=DH * n + DH - 1, pattern=[[2 * DH, 4]], channel_multiplier=-1))
            chain.wait()
            pool.sem_inc(ones_set, 1)
            for b, s in sequences(pool):
                wait_alone(pool, stood_p, (measured, b + 1))
                inverse_root(pool, rstd[:, :], aggr[:, :, 1], 1.0, LN_EPS, minus_half[:, :], var_eps, rstd_ready, b, stood_p)
                if low:
                    pool.wait_ge(ctx_in, 16 * b + 16)
                    pool.sem_inc(stood_p, 1)
                    wait_alone(pool, stood_p, (turned_x, b))
                    pool.tensor_copy(ctx_d[:, :, :], ctx[:, s, :, :]).then_inc(cast, 1)
                pool.wait_ge(raw_in, 16 * b + 16)
                pool.sem_inc(stood_p, 1)
                wait_alone(pool, stood_p, (pv, UNITS * b))
                if causal:
                    pool.tensor_scalar(key_off[:, s, :], raw[:, s, :], 0.0, OFF, ALU.is_le, ALU.mult).then_inc(off_ready, 1)
                    wait_alone(pool, stood_p, (off_ready, b + 1))
                    for t in range(TB):
                        last = pool.affine_select(out=neg[:, s, t, :], in_=key_off[:, s, :], compare_op=ALU.is_ge,
                                                  fill=OFF, base=t * P, pattern=[[-1, S]], channel_multiplier=1)
                    last.then_inc(neg_ready, 1)
                else:
                    pool.tensor_scalar(neg[:, s, :, :], raw[:, s, :, :], lam_b[:, 0:1], None, ALU.mult).then_inc(neg_ready, 1)

        def q_of(h, t):
            c, r = h // 8, 32 * (h % 8 // 2)
            return q[r:r + 32, h % 2, c, t * P:(t + 1) * P], k[r:r + 32, c, 0:keys(t)]

        def wait_copied(eng, b, m):
            eng.wait_ge(p_copied_a if m % 2 else p_copied_v, UNITS // 2 * b + (m // 2 + 1 if m >= 0 else 0) + HEAD)

        @block.tensor
        def _(pe):
            pe.wait_ge(ident_ready, 2 + HEAD)
            pe.wait_ge(ones_set, 1 + HEAD)
            if not low:
                pe.wait_ge(loaded_w, 64)
                blocks = [w_nat[:, n, ot, ct * P:(ct + 1) * P] for n in range(4) for ct in range(DC) for ot in range(DC)]
                transpose_blocks(pe, blocks, p_a, ident[:, :], turned, freed)
                pe.wait_ge(freed, 4 + HEAD)
            pe.wait_ge(consts, 1 + HEAD)
            for b, s in sequences(pe):
                pe.wait_ge(normed, b + 1 + HEAD)
                if low:
                    pe.wait_ge(cast, b + 1 + HEAD)
                else:
                    pe.wait_ge(ctx_in, 16 * b + 16)
                pe.wait_ge(added, b + HEAD)
                c_src = (lambda t, c: ctx_d[:, t, c * P:(c + 1) * P]) if low else (lambda t, c: ctx[:, s, t, c * P:(c + 1) * P])
                for c in range(DC):
                    for t in range(TB):
                        pe.transpose(p_ad[0][:, c * S + t * P:c * S + (t + 1) * P], xn[:, t, c * P:(c + 1) * P], ident_d[:, :])
                for c in range(DC):
                    for t in range(TB):
                        last = pe.transpose(p_ad[1][:, c * S + t * P:c * S + (t + 1) * P], c_src(t, c), ident_d[:, :])
                last.then_inc(turned_x, 1)
                pe.wait_ge(x_ready, b + 1 + HEAD)
                pe.wait_ge(c_ready, b + 1 + HEAD)
                for n, src in ((0, xT), (1, cT)):
                    for oc in range(DC):
                        for ic in range(DC):
                            last = pe.matmul(p_a[n][:, oc * S:(oc + 1) * S], w[:, n, ic, oc * P:(oc + 1) * P],
                                             src[:, ic, :], start=(ic == 0), stop=(ic == DC - 1))
                    last.then_inc(projected, 1)
                for t in range(TB):
                    for ic in range(DC):
                        last = pe.matmul(p_s[1][:, t * D:(t + 1) * D], cT[:, ic, t * P:(t + 1) * P], w[:, 2, ic, :],
                                         start=(ic == 0), stop=(ic == DC - 1))
                last.then_inc(projected, 1)
                pe.wait_ge(qk_ready, 2 * b + 2 + HEAD)
                for n in range(UNITS + 2):
                    if n < UNITS:
                        t, j = divmod(n, PAIRS)
                        if n == 1:
                            pe.wait_ge(v_ready, b + 1 + HEAD)
                        pe.wait_ge(shifted, UNITS * b + max(n - 1, 0) + HEAD)
                        for e in range(2):
                            lhs, rhs = q_of(2 * j + e, t)
                            last = pe.matmul(p_s[n % 2][:, e * S:e * S + keys(t)], lhs, rhs, start=True, stop=True)
                        last.then_inc(scored, 1)
                    if 1 <= n <= UNITS:
                        m = n - 1
                        t = m // PAIRS
                        pe.wait_ge(exped, UNITS * b + m + 1 + HEAD)
                        wait_copied(pe, b, m - 2)
                        for e in range(2):
                            for kt in range(keys(t) // P):
                                last = pe.transpose(p_p[m % 2][:, (e * TB + kt) * P:(e * TB + kt + 1) * P],
                                                    pr[:, m % 2, e, kt * P:(kt + 1) * P], ident[:, :])
                        last.then_inc(p_turned, 1)
                    if n >= 2:
                        m = n - 2
                        t, j = divmod(m, PAIRS)
                        wait_copied(pe, b, m)
                        if j == 0:
                            pe.wait_ge(o_ready, TB * b + max(t - 1, 0) + HEAD)
                        for e in range(2):
                            h = 2 * j + e
                            nk = keys(t) // P
                            for kt in range(nk):
                                last = pe.matmul(p_o[t][:, h * VW:(h + 1) * VW], prT[:, m % 2, e, kt, :],
                                                 v[:, kt, h, :], start=(kt == 0), stop=(kt == nk - 1))
                        last.then_inc(pv, 1)
                pe.wait_ge(o_ready, TB * b + TB + HEAD)
                for c in range(DC):
                    for t in range(TB):
                        last = pe.transpose(p_ad[0][:, c * S + t * P:c * S + (t + 1) * P], o[:, t, c * P:(c + 1) * P], ident_d[:, :])
                last.then_inc(turned_o, 1)
                pe.wait_ge(oT_ready, b + 1 + HEAD)
                for t in range(TB):
                    for ic in range(DC):
                        last = pe.matmul(p_a[1][:, t * D:(t + 1) * D], oT[:, ic, t * P:(t + 1) * P], w[:, 3, ic, :],
                                         start=(ic == 0), stop=(ic == DC - 1))
                last.then_inc(y_ready, 1)

        def turned_unit(b, m):
            nk = keys(m // PAIRS) // P
            return prT[:, m % 2, :, 0:nk, :], p_p[m % 2][:, :].rearrange("p (e k q) -> p e k q", e=2, k=TB)[:, :, 0:nk, :]

        @block.scalar
        def _(act):
            act.wait_ge(loaded_w, 64)
            if low:
                chain = Chain(act, chain_a)
                chain.done(act.activation(w[:, :, :, :], w_nat[:, :, :, :], ACT.Copy))
                chain.wait()
            else:
                evacuate_blocks(act, [w[:, n, :, :].rearrange("p c d -> p (c d)") for n in range(4)], p_a, turned, freed)
                act.wait_ge(freed, 4 + HEAD)
            act.wait_ge(consts, 1 + HEAD)
            for b, s in sequences(act):
                act.wait_ge(turned_x, b + 1 + HEAD)
                act.activation(xT[:, :, :].rearrange("p c n -> p (c n)"), p_ad[0][:, :], ACT.Copy).then_inc(x_ready, 1)
                act.wait_ge(projected, 3 * b + 1 + HEAD)
                if low:
                    act.activation(q_r[:, :, :].rearrange("p c n -> p (c n)"), p_a[0][:, :], ACT.Copy).then_inc(rounded, 1)
                    act.wait_ge(projected, 3 * b + 2 + HEAD)
                    act.activation(k_r[:, :, :].rearrange("p c n -> p (c n)"), p_a[1][:, :], ACT.Copy).then_inc(rounded, 1)
                    act.wait_ge(projected, 3 * b + 3 + HEAD)
                    act.activation(v_r[:, :, :].rearrange("p c n -> p (c n)"), p_s[1][:, :], ACT.Copy).then_inc(rounded, 1)
                else:
                    for e in range(2):
                        for c in range(DC):
                            last = act.activation(q[:, e, c, :], p_a[0][:, c * S:(c + 1) * S], ACT.Identity,
                                                  bias=q_bias[:, c, e:e + 1], scale=parity[:, e:e + 1])
                    last.then_inc(qk_ready, 1)
                for n in range(UNITS + 2):
                    if n < UNITS:
                        t = n // PAIRS
                        act.wait_ge(shifted, UNITS * b + n + 1 + HEAD)
                        act.wait_ge(p_turned, UNITS * b + max(n - 1, 0) + HEAD)
                        for e in range(2):
                            last = act.activation(pr[:, n % 2, e, 0:keys(t)], sc[:, n % 2, e, 0:keys(t)], ACT.Exp,
                                                  bias=nmax[:, n % 2, e:e + 1], scale=-1.0)
                        last.then_inc(exped, 1)
                    m = n - 1
                    if 0 <= m < UNITS and m % 2 == 1:
                        act.wait_ge(p_turned, UNITS * b + m + 1 + HEAD)
                        act.wait_ge(pv, UNITS * b + max(m - 1, 0) + HEAD)
                        act.activation(*turned_unit(b, m), ACT.Copy).then_inc(p_copied_a, 1)
                act.wait_ge(turned_o, b + 1 + HEAD)
                act.activation(oT[:, :, :].rearrange("p c n -> p (c n)"), p_ad[0][:, :], ACT.Copy).then_inc(oT_ready, 1)
                if low:
                    act.wait_ge(y_ready, b + 1 + HEAD)
                    act.activation(y_r[:, :, :].rearrange("p c n -> p (c n)"), p_a[1][:, :], ACT.Copy).then_inc(y_read, 1)

        @block.vector
        def _(dve):
            chain = Chain(dve, chain_v)
            dve.wait_ge(loaded_c, 16 * n_cols)
            dve.wait_ge(ones_set, 1 + HEAD)
            chain.done(dve.tensor_reduce(parity[:, :], side[:, :, :], AX.X, ALU.add))
            if low:
                chain.done(dve.tensor_copy(rows_d[:, :, :], rows[:, :, :]))
                chain.done(dve.tensor_copy(q_r[:, 0, 0:2 * DC], cols[:, :, :].rearrange("p a c -> p (a c)")))
                chain.wait()
                chain.done(dve.tensor_copy(cols_d[:, :, :].rearrange("p a c -> p (a c)"), q_r[:, 0, 0:2 * DC]))
            else:
                chain.wait()
                for e in range(2):
                    chain.done(dve.tensor_scalar(q_bias[:, :, e], cols[:, 0, :], parity[:, e:e + 1], None, ALU.mult))
                chain.done(dve.tensor_copy(cols_d[:, :, :], cols[:, :, :]))
                chain.done(dve.tensor_scalar(lam_b[:, :], lam_b[:, :], -1.0, None, ALU.mult))
            chain.wait()
            dve.sem_inc(consts, 1)
            chain.close()
            for b, s in sequences(dve):
                layer_norm_stats(dve, chain, lambda t: tile_of(X, b, t), stats, aggr, measured)
                dve.wait_ge(rstd_ready, b + 1 + HEAD)
                layer_norm_apply(dve, lambda t: tile_of(X, b, t), lambda t: xn[:, t, :], aggr, rstd, normed)
                dve.wait_ge(turned_x, b + 1 + HEAD)
                dve.tensor_copy(cT[:, :, :].rearrange("p c n -> p (c n)"), p_ad[1][:, :]).then_inc(c_ready, 1)
                if low:
                    dve.wait_ge(rounded, 3 * b + 1 + HEAD)
                    for c in range(DC):
                        chain.done(dve.tensor_scalar(q_f[:, c, :], q_r[:, c, :], cols_d[:, 0, c:c + 1], None, ALU.add))
                    chain.wait()
                    for e in range(2):
                        last = dve.tensor_scalar(q[:, e, :, :], q_f[:, :, :], parity[:, e:e + 1], None, ALU.mult)
                    last.then_inc(qk_ready, 1)
                    dve.wait_ge(rounded, 3 * b + 2 + HEAD)
                    for c in range(DC):
                        last = dve.tensor_scalar(k[:, c, :], k_r[:, c, :], cols_d[:, 1, c:c + 1], None, ALU.add)
                    last.then_inc(qk_ready, 1)
                    dve.wait_ge(rounded, 3 * b + 3 + HEAD)
                    for t in range(TB):
                        chain.done(dve.tensor_tensor(v_f[:, t, :], v_r[:, t, :], rows_d[:, 0, :], ALU.add))
                    chain.wait()
                    dve.tensor_copy(v[:, :, :, 0:DH], v_f[:, :, :].rearrange("p t (h r) -> p t h r", r=DH)).then_inc(v_ready, 1)
                else:
                    dve.wait_ge(projected, 3 * b + 2 + HEAD)
                    for c in range(DC):
                        last = dve.tensor_scalar(k[:, c, :], p_a[1][:, c * S:(c + 1) * S], cols_d[:, 1, c:c + 1], None, ALU.add)
                    last.then_inc(qk_ready, 1)
                    dve.wait_ge(projected, 3 * b + 3 + HEAD)
                    for t in range(TB):
                        last = dve.tensor_tensor(v[:, t, :, 0:DH], p_s[1][:, t * D:(t + 1) * D].rearrange("p (h r) -> p h r", r=DH),
                                                 rows[:, 0, :].rearrange("p (h r) -> p h r", r=DH), ALU.add)
                    last.then_inc(v_ready, 1)
                dve.wait_ge(neg_ready, b + 1 + HEAD)
                for n in range(UNITS + 3):
                    if n < UNITS:
                        t = n // PAIRS
                        wait_alone(dve, stood_v, (scored, UNITS * b + n + 1), (exped, UNITS * b + max(n - 1, 0)))
                        for e in range(2):
                            last = dve.tensor_tensor_reduce(
                                out=sc[:, n % 2, e, 0:keys(t)], in0=p_s[n % 2][:, e * S:e * S + keys(t)],
                                in1=neg[:, s, t, 0:keys(t)], scale=1.0, scalar=3e38, op0=ALU.add, op1=ALU.min,
                                accum_out=nmax[:, n % 2, e:e + 1])
                        last.then_inc(shifted, 1)
                    m = n - 2
                    if 0 <= m < UNITS and m % 2 == 0:
                        dve.wait_ge(p_turned, UNITS * b + m + 1 + HEAD)
                        dve.wait_ge(pv, UNITS * b + max(m - 1, 0) + HEAD)
                        dve.tensor_copy(*turned_unit(b, m)).then_inc(p_copied_v, 1)
                    m = n - 3
                    if 0 <= m and m % PAIRS == PAIRS - 1:
                        t = m // PAIRS
                        dve.wait_ge(pv, UNITS * b + m + 1 + HEAD)
                        heads = p_o[t][:, 0:H * VW].rearrange("p (h r) -> p h r", r=VW)
                        chain.done(dve.reciprocal(inv[:, t, :], heads[:, :, DH]))
                        chain.wait()
                        dve.tensor_tensor(o[:, t, :].rearrange("p (h r) -> p h r", r=DH), heads[:, :, 0:DH],
                                          inv[:, t, :].unsqueeze(2).broadcast_to([P, H, DH]), ALU.mult).then_inc(o_ready, 1)
                if low:
                    dve.wait_ge(y_read, b + 1 + HEAD)
                    for t in range(TB):
                        chain.done(dve.tensor_tensor(y_f[:, t, :], y_r[:, t, :], rows_d[:, 1, :], ALU.add))
                else:
                    dve.wait_ge(y_ready, b + 1 + HEAD)
                    for t in range(TB):
                        chain.done(dve.tensor_tensor(y_f[:, t, :], p_a[1][:, t * D:(t + 1) * D], rows[:, 1, :], ALU.add))
                chain.wait()
                for t in range(TB):
                    last = dve.tensor_tensor(tile_of(X, b, t), y_f[:, t, :], tile_of(X, b, t), ALU.add)
                last.then_inc(added, 1)
                wait_alone(dve, stood_v, (added, b + 1))
                chain.close()


G = 256
TG = G // P
NG = 2 * B * S // G + E - 1
RING = 3
GR = 8


def experts_ffn(nc, ins, X):
    rows_in = nc.dram_tensor("moe_rows_in", (NG * G, D), F32, kind="Internal").ap()
    rows_out = nc.dram_tensor("moe_rows_out", (NG * G, D), F32, kind="Internal").ap()
    with Phase(nc, "moe") as ph:
        ident = ph.sb("ident", [P, P])
        below = ph.sb("below", [P, P])
        ones = ph.sb("ones", [P, P])
        zeros = ph.sb("zeros", [P, D])
        minus_half = ph.sb("minus_half", [P, TB])
        gate = ph.sb("gate", [E, D])
        gateT = ph.sb("gateT", [P, DC, E])
        b1_nat = ph.sb("b1_nat", [E * HC, P])
        b1 = ph.sb("b1", [P, E * HC])
        b2 = ph.sb("b2", [P, E, D])
        stats = ph.sb("stats", [P, TB, 6])
        aggr = ph.sb("aggr", [P, TB, 2])
        rstd = ph.sb("rstd", [P, TB])
        XN = ph.sb("XN", [P, NT, D])
        XN_s = [ph.sb(f"XN_s{i}", [P, TB, D]) for i in range(2)]
        xT = ph.sb("xT", [P, DC, S])
        lg = ph.sb("lg", [P, NT, E])
        falling = ph.sb("falling", [P, E])
        ramp_i = ph.sb("ramp_i", [P, NG], I32)
        ramp = ph.sb("ramp", [P, NG])
        steps = ph.sb("steps", [P, B])
        best = ph.sb("best", [P, 2, NT])
        pick = ph.sb("pick", [P, 2, NT, E])
        cand = ph.sb("cand", [P, NT, E])
        cmax = ph.sb("cmax", [P, NT])
        lg2 = ph.sb("lg2", [P, NT, E])
        probs = ph.sb("probs", [P, NT, E])
        zsum = ph.sb("zsum", [P, NT])
        gap = ph.sb("gap", [P, NT])
        wsum = ph.sb("wsum", [P, NT])
        wt = ph.sb("wt", [P, 2, NT])
        both = ph.sb("both", [P, NT, E])
        before = ph.sb("before", [P, NT, E])
        total = ph.sb("total", [P, NT, E])
        upto = ph.sb("upto", [P, NT, E])
        over = ph.sb("over", [P, E, B])
        ngroups = ph.sb("ngroups", [P, E])
        gend = ph.sb("gend", [P, E])
        gstart = ph.sb("gstart", [P, E])
        passed = ph.sb("passed", [P, NG, E - 1])
        owner = ph.sb("owner", [P, NG])
        owner_i = ph.sb("owner_i", [P, NG], I32)
        place = ph.sb("place", [P, 2, NT])
        place_i = ph.sb("place_i", [P, 2, NT], U32)
        w1 = ph.sb("w1", [P, RING, DC, HID])
        w2 = ph.sb("w2", [P, RING, HC, D])
        gx = ph.sb("gx", [P, RING, TG, D])
        gT = ph.sb("gT", [P, DC, G])
        hT = ph.sb("hT", [P, HC, G])
        gy = ph.sb("gy", [P, RING, TG, D])
        got = ph.sb("got", [P, GR, D])
        p_t = ph.ps("p_t")
        p_c = ph.ps("p_c")
        p_h = [ph.ps(f"p_h{i}") for i in range(3)]
        p_y = ph.ps("p_y")
        names = ("loaded zeroed ident_ready set_up turned freed measured var_eps rstd_ready normed turned_x xT_ready logits lg_read "
                 "gap_ready exp_ready both_ready counted routed scattered gT_turned gT_ready hidden gelu_ready y_ready gy_ready stored "
                 "combined chain_v chain_p stood_v stood_p").split()
        s_ = {n: ph.own(n) if n.startswith(OWN) else ph.sem(n) for n in names}
        fed = [ph.own(f"fed{i}") for i in range(RING)]
        kept = [ph.sem(f"kept{i}") for i in range(RING)]
        gathered = [ph.own(f"gathered{i}") for i in range(GR)]
        block = ph.block()

        def groups(eng):
            with eng.Fori(0, NG // RING) as i:
                for r in range(RING):
                    yield i, RING * i + r, r

        def expert_of(eng, j):
            return eng.value_load(owner_i[0:1, bass.ds(j, 1)], min_val=0, max_val=E - 1)

        @block.sync
        def _(sp):
            sp.dma_start(gate[:, :], ins["L0_ffn_gate_w"]).then_inc(s_["loaded"], 16)
            sp.dma_start(b1_nat[:, :], ins["L0_ffn_b1"].rearrange("e (c p) -> (e c) p", p=P)).then_inc(s_["loaded"], 16)
            sp.dma_start(b2[:, :, :], ins["L0_ffn_b2"].partition_broadcast(P)).then_inc(s_["loaded"], 16)
            sp.wait_ge(s_["set_up"], 1 + HEAD)
            zero_src = zeros[:, :].unsqueeze(1).broadcast_to([P, NG * TG, D])
            sp.dma_start(rows_in.rearrange("(n p) d -> p n d", p=P), zero_src).then_inc(s_["zeroed"], 16)
            sp.wait_ge(s_["routed"], 1 + HEAD)
            sp.wait_ge(s_["scattered"], 16 * 2 * NT)
            for i, j, r in groups(sp):
                e = expert_of(sp, j)
                sp.wait_ge(s_["y_ready"], 3 * i + HEAD)
                sp.dma_start(gx[:, r, :, :], rows_in[bass.ds(j * G, G), :].rearrange("(t p) d -> p t d", p=P)).then_inc(fed[r], 16)
                sp.dma_start(w1[:, r, :, :], ins["L0_ffn_w1"][bass.ds(e, 1), :, :].rearrange("a (c p) h -> p (a c) h", p=P)).then_inc(fed[r], 16)
                sp.dma_start(w2[:, r, :, :], ins["L0_ffn_w2"][bass.ds(e, 1), :, :].rearrange("a (c p) d -> p (a c) d", p=P)).then_inc(fed[r], 16)

        @block.gpsimd
        def _(pool):
            make_identity(pool, ident[:, :], s_["ident_ready"])
            chain = Chain(pool, s_["chain_p"])
            chain.done(pool.memset(zeros[:, :], 0.0))
            chain.done(pool.memset(ones[:, :], 1.0))
            chain.done(pool.memset(minus_half[:, :], -0.5))
            chain.done(pool.iota(ramp_i[:, :], [[1, NG]], base=0, channel_multiplier=0))
            chain.wait()
            chain.done(pool.tensor_copy(ramp[:, :], ramp_i[:, :]))
            chain.done(pool.affine_select(out=below[:, :], in_=ones[:, :], compare_op=ALU.is_gt, fill=0.0, base=0,
                                          pattern=[[1, P]], channel_multiplier=-1))
            chain.wait()
            chain.done(pool.tensor_scalar(falling[:, :], ramp[:, 0:E], -1.0, float(E), ALU.mult, ALU.add))
            chain.done(pool.tensor_scalar(steps[:, :], ramp[:, 0:B], float(G), None, ALU.mult))
            chain.wait()
            pool.sem_inc(s_["set_up"], 1)
            for b, s in sequences(pool):
                wait_alone(pool, s_["stood_p"], (s_["measured"], b + 1))
                inverse_root(pool, rstd[:, :], aggr[:, :, 1], 1.0, LN_EPS, minus_half[:, :], s_["var_eps"], s_["rstd_ready"], b, s_["stood_p"])
            pool.wait_ge(s_["routed"], 1 + HEAD)
            pool.wait_ge(s_["zeroed"], 16)
            for t in range(NT):
                for k in range(2):
                    pool.indirect_dma_start(rows_in, bass.IndirectOffsetOnAxis(ap=place_i[:, k, t:t + 1], axis=0),
                                            XN[:, t, :], None).then_inc(s_["scattered"], 16)
            for r in range(RING):
                pool.wait_ge(kept[r], 16 * (NG // RING) + HEAD)
            for n in range(2 * NT):
                t, k = divmod(n, 2)
                if n >= GR:
                    pool.wait_ge(s_["combined"], n - GR + 1 + HEAD)
                pool.indirect_dma_start(got[:, n % GR, :], None, rows_out,
                                        bass.IndirectOffsetOnAxis(ap=place_i[:, k, t:t + 1], axis=0)).then_inc(gathered[n % GR], 16)

        @block.tensor
        def _(pe):
            pe.wait_ge(s_["loaded"], 48)
            pe.wait_ge(s_["ident_ready"], 2 + HEAD)
            for c in range(DC):
                pe.transpose(p_t[:, c * E:(c + 1) * E], gate[:, c * P:(c + 1) * P], ident[0:E, 0:E])
            pe.transpose(p_t[:, 2 * P:2 * P + E * HC], b1_nat[:, :], ident[0:E * HC, 0:E * HC]).then_inc(s_["turned"], 1)
            pe.wait_ge(s_["freed"], 1 + HEAD)
            for b, s in sequences(pe):
                pe.wait_ge(s_["normed"], b + 1 + HEAD)
                for c in range(DC):
                    for t in range(TB):
                        last = pe.transpose(p_t[:, c * S + t * P:c * S + (t + 1) * P], XN_s[s][:, t, c * P:(c + 1) * P], ident[:, :])
                last.then_inc(s_["turned_x"], 1)
                pe.wait_ge(s_["xT_ready"], b + 1 + HEAD)
                pe.wait_ge(s_["lg_read"], b + HEAD)
                for t in range(TB):
                    for ic in range(DC):
                        last = pe.matmul(p_c[:, t * E:(t + 1) * E], xT[:, ic, t * P:(t + 1) * P], gateT[:, ic, :],
                                         start=(ic == 0), stop=(ic == DC - 1))
                last.then_inc(s_["logits"], 1)
            pe.wait_ge(s_["both_ready"], 1 + HEAD)
            pe.wait_ge(s_["lg_read"], B + HEAD)
            both_v = both[:, :, :].rearrange("p t e -> p (t e)")
            pe.matmul(p_c[:, 0:NT * E], below[:, :], both_v, start=True, stop=True)
            pe.matmul(p_t[:, 0:NT * E], ones[:, :], both_v, start=True, stop=True).then_inc(s_["counted"], 1)
            pe.wait_ge(s_["routed"], 1 + HEAD)
            for i, j, r in groups(pe):
                pe.wait_ge(fed[r], 48 * i + 48)
                pe.wait_ge(s_["gT_ready"], j + HEAD)
                for c in range(DC):
                    for t in range(TG):
                        last = pe.transpose(p_t[:, c * G + t * P:c * G + (t + 1) * P], gx[:, r, t, c * P:(c + 1) * P], ident[:, :])
                last.then_inc(s_["gT_turned"], 1)
                pe.wait_ge(s_["gT_ready"], j + 1 + HEAD)
                for n in range(HC // 2):
                    pe.wait_ge(s_["gelu_ready"], HC // 2 * j + max(n - 2, 0) + HEAD)
                    for k in range(2):
                        for ic in range(DC):
                            last = pe.matmul(p_h[n % 3][:, k * G:(k + 1) * G], w1[:, r, ic, (2 * n + k) * P:(2 * n + k + 1) * P], gT[:, ic, :],
                                             start=(ic == 0), stop=(ic == DC - 1))
                    last.then_inc(s_["hidden"], 1)
                pe.wait_ge(s_["gy_ready"], j + HEAD)
                for t in range(TG):
                    for hc in range(HC):
                        if t == 0 and hc % 2 == 0:
                            pe.wait_ge(s_["gelu_ready"], HC // 2 * j + hc // 2 + 1 + HEAD)
                        last = pe.matmul(p_y[:, t * D:(t + 1) * D], hT[:, hc, t * P:(t + 1) * P], w2[:, r, hc, :],
                                         start=(hc == 0), stop=(hc == HC - 1))
                last.then_inc(s_["y_ready"], 1)

        @block.scalar
        def _(act):
            act.wait_ge(s_["turned"], 1 + HEAD)
            act.activation(gateT[:, :, :].rearrange("p c e -> p (c e)"), p_t[:, 0:DC * E], ACT.Copy)
            act.activation(b1[:, :], p_t[:, 2 * P:2 * P + E * HC], ACT.Copy).then_inc(s_["freed"], 1)
            for b, s in sequences(act):
                act.wait_ge(s_["turned_x"], b + 1 + HEAD)
                act.wait_ge(s_["logits"], b + HEAD)
                act.activation(flat(xT[:, :, :]), p_t[:, :], ACT.Copy).then_inc(s_["xT_ready"], 1)
            act.wait_ge(s_["gap_ready"], 1 + HEAD)
            act.activation(probs[:, :, :], probs[:, :, :], ACT.Exp)
            act.activation(gap[:, :], gap[:, :], ACT.Exp).then_inc(s_["exp_ready"], 1)
            act.wait_ge(s_["routed"], 1 + HEAD)
            for i, j, r in groups(act):
                e = expert_of(act, j)
                for n in range(HC // 2):
                    act.wait_ge(s_["hidden"], HC // 2 * j + n + 1 + HEAD)
                    if n == 0:
                        act.wait_ge(s_["y_ready"], j + HEAD)
                    for k in range(2):
                        last = act.activation(hT[:, 2 * n + k, :], p_h[n % 3][:, k * G:(k + 1) * G], ACT.Gelu,
                                              bias=b1[:, bass.ds(e * HC + 2 * n + k, 1)])
                    last.then_inc(s_["gelu_ready"], 1)
                act.wait_ge(s_["gy_ready"], j + 1 + HEAD)
                act.dma_start(rows_out[bass.ds(j * G, G), :].rearrange("(t p) d -> p t d", p=P), gy[:, r, :, :]).then_inc(kept[r], 16)

        @block.vector
        def _(dve):
            chain = Chain(dve, s_["chain_v"])

            def step(ins_):
                chain.done(ins_)
                chain.wait()

            dve.wait_ge(s_["set_up"], 1 + HEAD)
            for b, s in sequences(dve):
                layer_norm_stats(dve, chain, lambda t: tile_of(X, b, t), stats, aggr, s_["measured"])
                dve.wait_ge(s_["rstd_ready"], b + 1 + HEAD)
                dve.wait_ge(s_["turned_x"], b + HEAD)
                for t in range(TB):
                    chain.done(dve.tensor_scalar(XN_s[s][:, t, :], tile_of(X, b, t), aggr[:, t, 0:1], rstd[:, t:t + 1], ALU.subtract, ALU.mult))
                chain.wait()
                dve.tensor_copy(XN[:, bass.ds(TB * b, TB), :], XN_s[s][:, :, :]).then_inc(s_["normed"], 1)
                dve.wait_ge(s_["logits"], b + 1 + HEAD)
                dve.tensor_copy(lg[:, bass.ds(TB * b, TB), :], p_c[:, 0:TB * E].rearrange("p (t e) -> p t e", t=TB)).then_inc(s_["lg_read"], 1)
                wait_alone(dve, s_["stood_v"], (s_["normed"], b + 1), (s_["lg_read"], b + 1))
                chain.close()

            def by_tile(ap):
                return ap.unsqueeze(2).broadcast_to([P, NT, E])

            def by_expert(ap):
                return ap.unsqueeze(1).broadcast_to([P, NT, E])

            for k, src in ((0, lg), (1, lg2)):
                step(dve.tensor_reduce(best[:, k, :], src[:, :, :], AX.X, ALU.max))
                step(dve.tensor_tensor(cand[:, :, :], src[:, :, :], by_tile(best[:, k, :]), ALU.is_equal))
                step(dve.tensor_tensor(cand[:, :, :], cand[:, :, :], by_expert(falling[:, :]), ALU.mult))
                step(dve.tensor_reduce(cmax[:, :], cand[:, :, :], AX.X, ALU.max))
                step(dve.tensor_tensor(pick[:, k, :, :], cand[:, :, :], by_tile(cmax[:, :]), ALU.is_equal))
                if k == 0:
                    step(dve.scalar_tensor_tensor(flat(lg2[:, :, :]), flat(pick[:, 0, :, :]), -OFF, flat(lg[:, :, :]), ALU.mult, ALU.add))
            dve.tensor_tensor(both[:, :, :], pick[:, 0, :, :], pick[:, 1, :, :], ALU.add).then_inc(s_["both_ready"], 1)
            chain.done(dve.tensor_tensor(probs[:, :, :], lg[:, :, :], by_tile(best[:, 0, :]), ALU.subtract))
            chain.done(dve.tensor_tensor(gap[:, :], best[:, 1, :], best[:, 0, :], ALU.subtract))
            chain.wait()
            dve.sem_inc(s_["gap_ready"], 1)
            dve.wait_ge(s_["exp_ready"], 1 + HEAD)
            step(dve.tensor_reduce(zsum[:, :], probs[:, :, :], AX.X, ALU.add))
            step(dve.reciprocal(wt[:, 0, :], zsum[:, :]))
            step(dve.tensor_tensor(wt[:, 1, :], gap[:, :], wt[:, 0, :], ALU.mult))
            step(dve.tensor_tensor(wsum[:, :], wt[:, 0, :], wt[:, 1, :], ALU.add))
            step(dve.tensor_scalar(wsum[:, :], wsum[:, :], 1e-9, None, ALU.add))
            step(dve.reciprocal(wsum[:, :], wsum[:, :]))
            for k in range(2):
                chain.done(dve.tensor_tensor(wt[:, k, :], wt[:, k, :], wsum[:, :], ALU.mult))
            dve.wait_ge(s_["counted"], 1 + HEAD)
            step(dve.tensor_copy(total[:, :, :].rearrange("p t e -> p (t e)"), p_t[:, 0:NT * E]))
            for e in range(E):
                chain.done(dve.tensor_tensor_scan(upto[:, :, e], ones[:, 0:NT], total[:, :, e], 0.0, ALU.mult, ALU.add))
            chain.wait()
            step(dve.tensor_tensor(over[:, :, :], upto[:, NT - 1, :].unsqueeze(2).broadcast_to([P, E, B]),
                                   steps[:, :].unsqueeze(1).broadcast_to([P, E, B]), ALU.is_gt))
            step(dve.tensor_reduce(ngroups[:, :], over[:, :, :], AX.X, ALU.add))
            step(dve.tensor_tensor_scan(gend[:, :], ones[:, 0:E], ngroups[:, :], 0.0, ALU.mult, ALU.add))
            step(dve.tensor_tensor(gstart[:, :], gend[:, :], ngroups[:, :], ALU.subtract))
            step(dve.tensor_scalar(gstart[:, :], gstart[:, :], float(G), None, ALU.mult))
            step(dve.tensor_tensor(upto[:, :, :], upto[:, :, :], total[:, :, :], ALU.subtract))
            step(dve.tensor_tensor(before[:, :, :], p_c[:, 0:NT * E].rearrange("p (t e) -> p t e", e=E), upto[:, :, :], ALU.add))
            step(dve.tensor_tensor(before[:, :, :], before[:, :, :], by_expert(gstart[:, :]), ALU.add))
            for k in range(2):
                step(dve.tensor_tensor(cand[:, :, :], pick[:, k, :, :], before[:, :, :], ALU.mult))
                step(dve.tensor_reduce(place[:, k, :], cand[:, :, :], AX.X, ALU.add))
            step(dve.tensor_copy(place_i[:, :, :], place[:, :, :]))
            step(dve.tensor_tensor(passed[:, :, :], ramp[:, :].unsqueeze(2).broadcast_to([P, NG, E - 1]),
                                   gend[:, 0:E - 1].unsqueeze(1).broadcast_to([P, NG, E - 1]), ALU.is_ge))
            step(dve.tensor_reduce(owner[:, :], passed[:, :, :], AX.X, ALU.add))
            step(dve.tensor_copy(owner_i[:, :], owner[:, :]))
            dve.sem_inc(s_["routed"], 1)
            chain.close()
            for i, j, r in groups(dve):
                e = expert_of(dve, j)
                dve.wait_ge(s_["gT_turned"], j + 1 + HEAD)
                dve.tensor_copy(flat(gT[:, :, :]), p_t[:, :]).then_inc(s_["gT_ready"], 1)
                dve.wait_ge(s_["y_ready"], j + 1 + HEAD)
                dve.wait_ge(kept[r], 16 * i + HEAD)
                for t in range(TG):
                    last = dve.tensor_tensor(gy[:, r, t, :], p_y[:, t * D:(t + 1) * D], b2[:, bass.ds(e, 1), :].rearrange("p a d -> p (a d)"), ALU.add)
                last.then_inc(s_["gy_ready"], 1)
            for n in range(2 * NT):
                t, k = divmod(n, 2)
                dve.wait_ge(gathered[n % GR], 16 * (n // GR + 1))
                if k:
                    dve.wait_ge(s_["combined"], n + HEAD)
                dve.scalar_tensor_tensor(X[:, t, :], got[:, n % GR, :], wt[:, k, t:t + 1], X[:, t, :], ALU.mult, ALU.add).then_inc(s_["combined"], 1)
            dve.wait_ge(s_["combined"], 2 * NT + HEAD)


R_CAP = 85.0


def time_channel_mix(nc, ins, X):
    L = "L1_attn_"
    with Phase(nc, "mix") as ph:
        ident = ph.sb("ident", [P, P])
        minus_half = ph.sb("minus_half", [P, TB])
        w_nat = ph.sb("w_nat", [P, 5, DC, D])
        fk_nat = ph.sb("fk_nat", [P, HC, D])
        fv_nat = ph.sb("fv_nat", [P, DC, HID])
        w = ph.sb("w", [P, 5, DC, D])
        fk = ph.sb("fk", [P, DC, HID])
        fv = ph.sb("fv", [P, HC, D])
        vec_names = ("ln1_g", "ln1_b", "ln2_g", "ln2_b", "time_mix_k", "time_mix_v", "time_mix_r",
                     "cm_k", "cm_r", "time_decay", "time_first")
        vec = ph.sb("vec", [P, len(vec_names), DC])
        at = {n: i for i, n in enumerate(vec_names)}

        def col(n, c):
            return vec[:, at[n], c:c + 1]

        decay = ph.sb("decay", [P, DC])
        stats = ph.sb("stats", [P, TB, 6])
        aggr = ph.sb("aggr", [P, TB, 2])
        rstd = ph.sb("rstd", [P, TB])
        y = ph.sb("y", [P, TB, D])
        yn = ph.sb("yn", [P, TB, D])
        xa = ph.sb("xa", [P, DC, S + 1])
        dif = ph.sb("dif", [P, DC, S])
        mixed = ph.sb("mixed", [P, 3, DC, S])
        run = ph.sb("run", [P, DC, S + 1])
        num = ph.sb("num", [P, DC, S + 1])
        den = ph.sb("den", [P, DC, S + 1])
        vals = ph.sb("vals", [P, DC, S])
        top = ph.sb("top", [P, DC, S])
        fall = ph.sb("fall", [P, DC, S])
        gain = ph.sb("gain", [P, DC, S])
        gain_v = ph.sb("gain_v", [P, DC, S])
        e_old = ph.sb("e_old", [P, DC, S])
        e_new = ph.sb("e_new", [P, DC, S])
        e_r = ph.sb("e_r", [P, DC, S])
        a = ph.sb("a", [P, DC, S])
        a2 = ph.sb("a2", [P, DC, S])
        a3 = ph.sb("a3", [P, DC, S])
        mixed_out = ph.sb("mixed_out", [P, DC, S])
        hid = ph.sb("hid", [P, HC, S])
        hid_sq = ph.sb("hid_sq", [P, HC, S])
        e_r2 = ph.sb("e_r2", [P, TB, D])
        g = ph.sb("g", [P, TB, D])
        p_t = ph.ps("p_t")
        p_k, p_v, p_r = ph.ps("p_k"), ph.ps("p_v"), ph.ps("p_r")
        p_h = [ph.ps(f"p_h{i}") for i in range(2)]
        p_kv, p_y = ph.ps("p_kv"), ph.ps("p_y")
        banks = [p_t, p_k, p_v, p_r, p_h[0], p_h[1], p_kv, p_y]

        names = ("r_capped r2_capped loaded ident_ready set_up turned freed consts measured var_eps rstd_ready normed turned_x xa_ready "
                 "mixed_ready projected vals_ready run_ready d_fall d_gain top_ready d_old d_new fall_ready gain_ready old_ready new_ready "
                 "er_ready scans_ready part_a part_b part_c part_d out_ready att_ready mid_ready turned_m xc_ready mixed2_ready hidden relu_ready "
                 "squared r2_ready kv_ready er2_ready added chain_v chain_p stood_v stood_p stood_a").split()
        sems = {n: ph.own(n) if n.startswith(OWN) else ph.sem(n) for n in names}
        block = ph.block()
        s_ = sems
        n_blocks = (5 * 4 + 16 + 16) // 4

        @block.sync
        def _(sp):
            for n, m in enumerate(("att_Wk", "att_Wv", "att_Wr", "att_Wo", "ffn_Wr")):
                sp.dma_start(w_nat[:, n, :, :], ins[L + m].rearrange("(c p) d -> p c d", p=P)).then_inc(s_["loaded"], 16)
            sp.dma_start(fk_nat[:, :, :], ins[L + "ffn_Wk"].rearrange("(c p) d -> p c d", p=P)).then_inc(s_["loaded"], 16)
            sp.dma_start(fv_nat[:, :, :], ins[L + "ffn_Wv"].rearrange("(c p) d -> p c d", p=P)).then_inc(s_["loaded"], 16)
            with nc.allow_non_contiguous_dma(reason="vectors of 256 numbers"):
                for n, m in enumerate(vec_names):
                    sp.dma_start(vec[:, n, :], columns(ins[L + m])).then_inc(s_["loaded"], 16)

        n_loads = 7 + len(vec_names)

        @block.gpsimd
        def _(pool):
            make_identity(pool, ident[:, :], s_["ident_ready"])
            chain = Chain(pool, s_["chain_p"])
            chain.done(pool.memset(minus_half[:, :], -0.5))
            chain.done(pool.memset(xa[:, :, 0:1], 0.0))
            chain.done(pool.memset(run[:, :, 0:1], -1e38))
            chain.done(pool.memset(num[:, :, 0:1], 0.0))
            chain.done(pool.memset(den[:, :, 0:1], 0.0))
            chain.wait()
            pool.sem_inc(s_["set_up"], 1)
            chain.close()
            for b, s in sequences(pool):
                def root(k):
                    wait_alone(pool, s_["stood_p"], (s_["measured"], 3 * b + k + 1))
                    inverse_root(pool, rstd[:, :], aggr[:, :, 1], 1.0, LN_EPS, minus_half[:, :], s_["var_eps"], s_["rstd_ready"], 3 * b + k, s_["stood_p"])
                root(0)
                root(1)
                pool.wait_ge(s_["run_ready"], b + 1 + HEAD)
                pool.tensor_tensor(fall[:, :, :], run[:, :, 0:S], run[:, :, 1:S + 1], ALU.subtract).then_inc(s_["d_fall"], 1)
                pool.wait_ge(s_["top_ready"], b + 1 + HEAD)
                pool.tensor_tensor(e_old[:, :, :], run[:, :, 0:S], top[:, :, :], ALU.subtract).then_inc(s_["d_old"], 1)
                pool.wait_ge(s_["new_ready"], b + 1 + HEAD)
                pool.wait_ge(s_["vals_ready"], b + 1 + HEAD)
                pool.tensor_tensor(a[:, :, :], e_new[:, :, :], vals[:, :, :], ALU.mult).then_inc(s_["part_a"], 1)
                pool.wait_ge(s_["scans_ready"], b + 1 + HEAD)
                pool.wait_ge(s_["old_ready"], b + 1 + HEAD)
                pool.tensor_tensor(a2[:, :, :], e_old[:, :, :], num[:, :, 0:S], ALU.mult).then_inc(s_["part_b"], 1)
                pool.wait_ge(s_["part_b"], b + 1 + HEAD)
                pool.tensor_tensor(a[:, :, :], a[:, :, :], a2[:, :, :], ALU.add).then_inc(s_["part_c"], 1)
                root(2)
                for n in range(HC // 2):
                    pool.wait_ge(s_["relu_ready"], HC // 2 * b + n + 1 + HEAD)
                    pool.tensor_tensor(hid_sq[:, 2 * n:2 * n + 2, :], hid[:, 2 * n:2 * n + 2, :], hid[:, 2 * n:2 * n + 2, :], ALU.mult).then_inc(s_["squared"], 1)

        @block.tensor
        def _(pe):
            pe.wait_ge(s_["loaded"], 16 * n_loads)
            pe.wait_ge(s_["ident_ready"], 2 + HEAD)
            blocks = [w_nat[:, n, ot, ct * P:(ct + 1) * P] for n in range(5) for ct in range(DC) for ot in range(DC)]
            blocks += [fk_nat[:, ot, ct * P:(ct + 1) * P] for ct in range(DC) for ot in range(HC)]
            blocks += [fv_nat[:, ot, ct * P:(ct + 1) * P] for ct in range(HC) for ot in range(DC)]
            transpose_blocks(pe, blocks, banks, ident[:, :], s_["turned"], s_["freed"])
            pe.wait_ge(s_["freed"], n_blocks + HEAD)
            pe.wait_ge(s_["consts"], 1 + HEAD)

            def turn(src, done):
                for c in range(DC):
                    for t in range(TB):
                        last = pe.transpose(p_t[:, c * S + t * P:c * S + (t + 1) * P], src[:, t, c * P:(c + 1) * P], ident[:, :])
                last.then_inc(done, 1)

            for b, s in sequences(pe):
                pe.wait_ge(s_["normed"], 3 * b + 2 + HEAD)
                pe.wait_ge(s_["added"], b + HEAD)
                turn(yn, s_["turned_x"])
                for n, bank in enumerate((p_k, p_v, p_r)):
                    pe.wait_ge(s_["mixed_ready"], 3 * b + n + 1 + HEAD)
                    for oc in range(DC):
                        for ic in range(DC):
                            last = pe.matmul(bank[:, oc * S:(oc + 1) * S], w[:, n, ic, oc * P:(oc + 1) * P], mixed[:, n, ic, :],
                                             start=(ic == 0), stop=(ic == DC - 1))
                    last.then_inc(s_["projected"], 1)
                pe.wait_ge(s_["out_ready"], b + 1 + HEAD)
                for t in range(TB):
                    for ic in range(DC):
                        last = pe.matmul(p_y[:, t * D:(t + 1) * D], mixed_out[:, ic, t * P:(t + 1) * P], w[:, 3, ic, :],
                                         start=(ic == 0), stop=(ic == DC - 1))
                last.then_inc(s_["att_ready"], 1)
                pe.wait_ge(s_["normed"], 3 * b + 3 + HEAD)
                turn(yn, s_["turned_m"])
                pe.wait_ge(s_["mixed2_ready"], 2 * b + 1 + HEAD)
                for n in range(HC // 2):
                    pe.wait_ge(s_["relu_ready"], HC // 2 * b + max(n - 1, 0) + HEAD)
                    for k in range(2):
                        for ic in range(DC):
                            last = pe.matmul(p_h[n % 2][:, k * S:(k + 1) * S], fk[:, ic, (2 * n + k) * P:(2 * n + k + 1) * P], mixed[:, 0, ic, :],
                                             start=(ic == 0), stop=(ic == DC - 1))
                    last.then_inc(s_["hidden"], 1)
                pe.wait_ge(s_["mixed2_ready"], 2 * b + 2 + HEAD)
                for t in range(TB):
                    for ic in range(DC):
                        last = pe.matmul(p_y[:, t * D:(t + 1) * D], mixed[:, 1, ic, t * P:(t + 1) * P], w[:, 4, ic, :],
                                         start=(ic == 0), stop=(ic == DC - 1))
                last.then_inc(s_["r2_ready"], 1)
                pe.wait_ge(s_["squared"], HC // 2 * (b + 1) + HEAD)
                for t in range(TB):
                    for hc in range(HC):
                        last = pe.matmul(p_kv[:, t * D:(t + 1) * D], hid_sq[:, hc, t * P:(t + 1) * P], fv[:, hc, :],
                                         start=(hc == 0), stop=(hc == HC - 1))
                last.then_inc(s_["kv_ready"], 1)

        @block.scalar
        def _(act):
            act.wait_ge(s_["loaded"], 16 * n_loads)
            act.wait_ge(s_["set_up"], 1 + HEAD)
            dests = [flat(w[:, n, :, :]) for n in range(5)]
            dests += [fk[:, ct, g4 * 512:(g4 + 1) * 512] for ct in range(DC) for g4 in range(2)]
            dests += [flat(fv[:, 2 * g2:2 * g2 + 2, :]) for g2 in range(HC // 2)]
            evacuate_blocks(act, dests, banks, s_["turned"], s_["freed"])
            act.activation(decay[:, :], vec[:, at["time_decay"], :], ACT.Exp).then_inc(s_["freed"], 1)
            act.wait_ge(s_["consts"], 1 + HEAD)
            for b, s in sequences(act):
                act.wait_ge(s_["turned_x"], b + 1 + HEAD)
                for c in range(DC):
                    last = act.activation(xa[:, c, 1:S + 1], p_t[:, c * S:(c + 1) * S], ACT.Identity, scale=col("ln1_g", c), bias=col("ln1_b", c))
                last.then_inc(s_["xa_ready"], 1)
                act.wait_ge(s_["projected"], 3 * b + 2 + HEAD)
                act.activation(flat(vals[:, :, :]), p_v[:, :], ACT.Copy).then_inc(s_["vals_ready"], 1)
                act.wait_ge(s_["r_capped"], b + 1 + HEAD)
                act.activation(e_r[:, :, :], e_r[:, :, :], ACT.Exp, scale=-1.0).then_inc(s_["er_ready"], 1)
                act.wait_ge(s_["d_gain"], b + 1 + HEAD)
                act.activation(gain[:, :, :], gain[:, :, :], ACT.Exp).then_inc(s_["gain_ready"], 1)
                act.wait_ge(s_["d_fall"], b + 1 + HEAD)
                for c in range(DC):
                    last = act.activation(fall[:, c, :], fall[:, c, :], ACT.Exp, bias=decay[:, c:c + 1])
                last.then_inc(s_["fall_ready"], 1)
                act.wait_ge(s_["d_new"], b + 1 + HEAD)
                for c in range(DC):
                    last = act.activation(e_new[:, c, :], e_new[:, c, :], ACT.Exp, bias=col("time_first", c))
                last.then_inc(s_["new_ready"], 1)
                act.wait_ge(s_["d_old"], b + 1 + HEAD)
                act.activation(e_old[:, :, :], e_old[:, :, :], ACT.Exp).then_inc(s_["old_ready"], 1)
                act.wait_ge(s_["turned_m"], b + 1 + HEAD)
                for c in range(DC):
                    last = act.activation(xa[:, c, 1:S + 1], p_t[:, c * S:(c + 1) * S], ACT.Identity, scale=col("ln2_g", c), bias=col("ln2_b", c))
                last.then_inc(s_["xc_ready"], 1)
                for n in range(HC // 2):
                    act.wait_ge(s_["hidden"], HC // 2 * b + n + 1 + HEAD)
                    act.activation(flat(hid[:, 2 * n:2 * n + 2, :]), p_h[n % 2][:, :], ACT.Relu).then_inc(s_["relu_ready"], 1)
                act.wait_ge(s_["r2_capped"], b + 1 + HEAD)
                act.activation(e_r2[:, :, :], e_r2[:, :, :], ACT.Exp, scale=-1.0).then_inc(s_["er2_ready"], 1)

        @block.vector
        def _(dve):
            chain = Chain(dve, s_["chain_v"])
            dve.wait_ge(s_["freed"], n_blocks + 1 + HEAD)
            chain.done(dve.tensor_scalar(decay[:, :], decay[:, :], -1.0, None, ALU.mult))
            chain.wait()
            dve.sem_inc(s_["consts"], 1)
            chain.close()

            def norm(b, k, src, dst):
                layer_norm_stats(dve, chain, src, stats, aggr, s_["measured"])
                dve.wait_ge(s_["rstd_ready"], 3 * b + k + 1 + HEAD)
                layer_norm_apply(dve, src, lambda t: dst[:, t, :], aggr, rstd, s_["normed"])

            def mix(n, name, done):
                for c in range(DC):
                    last = dve.scalar_tensor_tensor(mixed[:, n, c, :], dif[:, c, :], col(name, c), xa[:, c, 0:S], ALU.mult, ALU.add)
                last.then_inc(done, 1)

            for b, s in sequences(dve):
                norm(b, 0, lambda t: tile_of(X, b, t), y)
                wait_alone(dve, s_["stood_v"], (s_["normed"], 3 * b + 1))
                norm(b, 1, lambda t: y[:, t, :], yn)
                dve.wait_ge(s_["xa_ready"], b + 1 + HEAD)
                chain.done(dve.tensor_tensor(dif[:, :, :], xa[:, :, 1:S + 1], xa[:, :, 0:S], ALU.subtract))
                chain.wait()
                for n, m in enumerate(("time_mix_k", "time_mix_v", "time_mix_r")):
                    mix(n, m, s_["mixed_ready"])
                dve.wait_ge(s_["projected"], 3 * b + 1 + HEAD)
                kk = p_k[:, :].rearrange("p (c n) -> p c n", c=DC)
                for c in range(DC):
                    last = dve.tensor_tensor_scan(run[:, c, 1:S + 1], decay[:, c:c + 1].broadcast_to([P, S]), kk[:, c, :], -1e38, ALU.add, ALU.max)
                last.then_inc(s_["run_ready"], 1)
                dve.wait_ge(s_["run_ready"], b + 1 + HEAD)
                dve.tensor_tensor(gain[:, :, :], kk, run[:, :, 1:S + 1], ALU.subtract).then_inc(s_["d_gain"], 1)
                for c in range(DC):
                    last = dve.scalar_tensor_tensor(top[:, c, :], kk[:, c, :], col("time_first", c), run[:, c, 0:S], ALU.add, ALU.max)
                last.then_inc(s_["top_ready"], 1)
                dve.wait_ge(s_["top_ready"], b + 1 + HEAD)
                dve.tensor_tensor(e_new[:, :, :], kk, top[:, :, :], ALU.subtract).then_inc(s_["d_new"], 1)
                dve.wait_ge(s_["projected"], 3 * b + 3 + HEAD)
                dve.tensor_scalar(flat(e_r[:, :, :]), p_r[:, :], -R_CAP, None, ALU.max).then_inc(s_["r_capped"], 1)
                dve.wait_ge(s_["gain_ready"], b + 1 + HEAD)
                dve.wait_ge(s_["vals_ready"], b + 1 + HEAD)
                chain.done(dve.tensor_tensor(gain_v[:, :, :], gain[:, :, :], vals[:, :, :], ALU.mult))
                dve.wait_ge(s_["fall_ready"], b + 1 + HEAD)
                for c in range(DC):
                    chain.done(dve.tensor_tensor_scan(den[:, c, 1:S + 1], fall[:, c, :], gain[:, c, :], 0.0, ALU.mult, ALU.add))
                chain.wait()
                for c in range(DC):
                    last = dve.tensor_tensor_scan(num[:, c, 1:S + 1], fall[:, c, :], gain_v[:, c, :], 0.0, ALU.mult, ALU.add)
                last.then_inc(s_["scans_ready"], 1)
                dve.wait_ge(s_["old_ready"], b + 1 + HEAD)
                dve.wait_ge(s_["new_ready"], b + 1 + HEAD)
                chain.done(dve.tensor_tensor(a3[:, :, :], e_old[:, :, :], den[:, :, 0:S], ALU.mult))
                chain.wait()
                chain.done(dve.tensor_tensor(a3[:, :, :], a3[:, :, :], e_new[:, :, :], ALU.add))
                dve.wait_ge(s_["er_ready"], b + 1 + HEAD)
                chain.wait()
                chain.done(dve.scalar_tensor_tensor(flat(a3[:, :, :]), flat(e_r[:, :, :]), 1.0, flat(a3[:, :, :]), ALU.add, ALU.mult))
                chain.wait()
                chain.done(dve.reciprocal(a3[:, :, :], a3[:, :, :]))
                chain.wait()
                dve.wait_ge(s_["part_c"], b + 1 + HEAD)
                dve.tensor_tensor(mixed_out[:, :, :], a[:, :, :], a3[:, :, :], ALU.mult).then_inc(s_["out_ready"], 1)
                dve.wait_ge(s_["att_ready"], b + 1 + HEAD)
                chain.done(dve.tensor_tensor(flat(y[:, :, :]), p_y[:, :], flat(y[:, :, :]), ALU.add))
                chain.wait()
                norm(b, 2, lambda t: y[:, t, :], yn)
                dve.wait_ge(s_["xc_ready"], b + 1 + HEAD)
                chain.done(dve.tensor_tensor(dif[:, :, :], xa[:, :, 1:S + 1], xa[:, :, 0:S], ALU.subtract))
                chain.wait()
                for n, m in enumerate(("cm_k", "cm_r")):
                    mix(n, m, s_["mixed2_ready"])
                dve.wait_ge(s_["r2_ready"], b + 1 + HEAD)
                dve.tensor_scalar(flat(e_r2[:, :, :]), p_y[:, :], -R_CAP, None, ALU.max).then_inc(s_["r2_capped"], 1)
                dve.wait_ge(s_["er2_ready"], b + 1 + HEAD)
                chain.done(dve.tensor_scalar(flat(g[:, :, :]), flat(e_r2[:, :, :]), 1.0, None, ALU.add))
                chain.wait()
                chain.done(dve.reciprocal(g[:, :, :], g[:, :, :]))
                chain.wait()
                dve.wait_ge(s_["kv_ready"], b + 1 + HEAD)
                chain.done(dve.tensor_tensor(flat(g[:, :, :]), p_kv[:, :], flat(g[:, :, :]), ALU.mult))
                chain.wait()
                chain.done(dve.tensor_tensor(g[:, :, :], g[:, :, :], y[:, :, :], ALU.add))
                chain.wait()
                for t in range(TB):
                    last = dve.tensor_tensor(tile_of(X, b, t), g[:, t, :], tile_of(X, b, t), ALU.add)
                last.then_inc(s_["added"], 1)
                wait_alone(dve, s_["stood_v"], (s_["added"], b + 1))
                chain.close()


def float8_ffn(nc, ins, X):
    FAR = 128.0
    with Phase(nc, "ffn") as ph:
        ident = ph.sb("ident", [P, P])
        ident_b = ph.sb("ident_b", [P, P], BF16)
        minus_half = ph.sb("minus_half", [P, TB])
        w_nat = ph.sb("w_nat", [P, DC, D])
        near8 = ph.sb("near8", [P, DC, D], FP8)
        far8 = ph.sb("far8", [P, DC, D], FP8)
        near = ph.sb("near", [P, DC, D])
        far = ph.sb("far", [P, DC, D])
        is_far = ph.sb("is_far", [P, DC, D])
        w_q = ph.sb("w_q", [P, DC, D], BF16)
        wt = ph.sb("wt", [P, DC, D], BF16)
        bias = ph.sb("bias", [P, D])
        stats = ph.sb("stats", [P, TB, 6])
        aggr = ph.sb("aggr", [P, TB, 2])
        rstd = ph.sb("rstd", [P, TB])
        xn = ph.sb("xn", [P, TB, D])
        x8 = ph.sb("x8", [P, TB, D], FP8)
        xq = ph.sb("xq", [P, 2, TB, D], BF16)
        xT = ph.sb("xT", [P, 2, DC, S], BF16)
        y16 = ph.sb("y16", [P, 2, TB, D], F16)
        y = ph.sb("y", [P, TB, D])
        p_t = [ph.ps(f"p_t{i}", (P, 1024), BF16) for i in range(2)]
        p_y = [ph.ps(f"p_y{i}") for i in range(2)]
        names = ("loaded ident_ready ident_b_ready w_ready w_turned wt_ready measured var_eps rstd_ready normed quantised turned_x xT_ready "
                 "y_ready y_read added chain_v stood_v stood_p").split()
        s_ = {n: ph.own(n) if n.startswith(OWN) else ph.sem(n) for n in names}
        block = ph.block()

        @block.sync
        def _(sp):
            sp.dma_start(w_nat[:, :, :], ins["L1_ffn_weight"].rearrange("(c p) d -> p c d", p=P)).then_inc(s_["loaded"], 16)
            sp.dma_start(bias[:, :], ins["L1_ffn_bias"].partition_broadcast(P)).then_inc(s_["loaded"], 16)

        @block.gpsimd
        def _(pool):
            make_identity(pool, ident[:, :], s_["ident_ready"])
            pool.memset(minus_half[:, :], -0.5).then_inc(s_["ident_b_ready"], 1)
            pool.wait_ge(s_["ident_ready"], 2 + HEAD)
            pool.tensor_copy(ident_b[:, :], ident[:, :]).then_inc(s_["ident_b_ready"], 1)
            pool.wait_ge(s_["ident_b_ready"], 2 + HEAD)
            for b, s in sequences(pool):
                wait_alone(pool, s_["stood_p"], (s_["measured"], b + 1))
                inverse_root(pool, rstd[:, :], aggr[:, :, 1], 1.0, LN_EPS, minus_half[:, :], s_["var_eps"], s_["rstd_ready"], b, s_["stood_p"])

        @block.tensor
        def _(pe):
            pe.wait_ge(s_["ident_b_ready"], 2 + HEAD)
            pe.wait_ge(s_["w_ready"], 1 + HEAD)
            for ct in range(DC):
                for ot in range(DC):
                    last = pe.transpose(p_t[0][:, (ct * DC + ot) * P:(ct * DC + ot + 1) * P], w_q[:, ot, ct * P:(ct + 1) * P], ident_b[:, :])
            last.then_inc(s_["w_turned"], 1)
            pe.wait_ge(s_["wt_ready"], 1 + HEAD)
            for b, s in sequences(pe):
                pe.wait_ge(s_["quantised"], b + 1 + HEAD)
                pe.wait_ge(s_["xT_ready"], b + HEAD)
                for c in range(DC):
                    for t in range(TB):
                        last = pe.transpose(p_t[s][:, c * S + t * P:c * S + (t + 1) * P], xq[:, s, t, c * P:(c + 1) * P], ident_b[:, :])
                last.then_inc(s_["turned_x"], 1)
                pe.wait_ge(s_["xT_ready"], b + 1 + HEAD)
                pe.wait_ge(s_["y_read"], b + HEAD)
                for t in range(TB):
                    for ic in range(DC):
                        last = pe.matmul(p_y[s][:, t * D:(t + 1) * D], xT[:, s, ic, t * P:(t + 1) * P], wt[:, ic, :],
                                         start=(ic == 0), stop=(ic == DC - 1))
                last.then_inc(s_["y_ready"], 1)

        @block.scalar
        def _(act):
            act.wait_ge(s_["w_turned"], 1 + HEAD)
            act.activation(flat(wt[:, :, :]), p_t[0][:, 0:512], ACT.Copy).then_inc(s_["wt_ready"], 1)
            for b, s in sequences(act):
                act.wait_ge(s_["turned_x"], b + 1 + HEAD)
                act.wait_ge(s_["y_ready"], b + HEAD)
                act.activation(flat(xT[:, s, :, :]), p_t[s][:, 0:512], ACT.Copy).then_inc(s_["xT_ready"], 1)
                act.wait_ge(s_["y_ready"], b + 1 + HEAD)
                act.wait_ge(s_["added"], b + HEAD)
                act.activation(flat(y16[:, s, :, :]), p_y[s][:, :], ACT.Copy).then_inc(s_["y_read"], 1)

        @block.vector
        def _(dve):
            chain = Chain(dve, s_["chain_v"])

            def step(ins_):
                chain.done(ins_)
                chain.wait()

            dve.wait_ge(s_["loaded"], 32)
            step(dve.tensor_scalar(w_nat[:, :, :], w_nat[:, :, :], 448.0, -448.0, ALU.min, ALU.max))
            step(dve.tensor_scalar(near[:, :, :], w_nat[:, :, :], FAR, -FAR, ALU.min, ALU.max))
            step(dve.tensor_copy(near8[:, :, :], near[:, :, :], saturate=False))
            step(dve.tensor_copy(near[:, :, :], near8[:, :, :]))
            step(dve.tensor_scalar(far[:, :, :], w_nat[:, :, :], 0.25, None, ALU.mult))
            step(dve.tensor_copy(far8[:, :, :], far[:, :, :], saturate=False))
            step(dve.tensor_copy(far[:, :, :], far8[:, :, :]))
            step(dve.tensor_tensor(is_far[:, :, :], w_nat[:, :, :], w_nat[:, :, :], ALU.mult))
            step(dve.tensor_scalar(is_far[:, :, :], is_far[:, :, :], FAR * FAR, None, ALU.is_gt))
            step(dve.scalar_tensor_tensor(flat(far[:, :, :]), flat(far[:, :, :]), 4.0, flat(near[:, :, :]), ALU.mult, ALU.subtract))
            step(dve.tensor_tensor(far[:, :, :], far[:, :, :], is_far[:, :, :], ALU.mult))
            step(dve.tensor_tensor(w_q[:, :, :], near[:, :, :], far[:, :, :], ALU.add))
            dve.sem_inc(s_["w_ready"], 1)
            chain.close()
            for b, s in sequences(dve):
                layer_norm_stats(dve, chain, lambda t: tile_of(X, b, t), stats, aggr, s_["measured"])
                dve.wait_ge(s_["rstd_ready"], b + 1 + HEAD)
                for t in range(TB):
                    chain.done(dve.tensor_scalar(xn[:, t, :], tile_of(X, b, t), aggr[:, t, 0:1], rstd[:, t:t + 1], ALU.subtract, ALU.mult))
                chain.wait()
                step(dve.tensor_copy(x8[:, :, :], xn[:, :, :], saturate=False))
                dve.tensor_copy(xq[:, s, :, :], x8[:, :, :]).then_inc(s_["quantised"], 1)
                dve.wait_ge(s_["y_read"], b + 1 + HEAD)
                for t in range(TB):
                    chain.done(dve.tensor_tensor(y[:, t, :], y16[:, s, t, :], bias[:, :], ALU.add))
                chain.wait()
                for t in range(TB):
                    last = dve.tensor_tensor(tile_of(X, b, t), y[:, t, :], tile_of(X, b, t), ALU.add)
                last.then_inc(s_["added"], 1)
                wait_alone(dve, s_["stood_v"], (s_["added"], b + 1))
                chain.close()


PHASES = [decay_attention, lambda nc, ins, X: cross_attention(nc, ins, X, 0, True), experts_ffn, time_channel_mix, lambda nc, ins, X: cross_attention(nc, ins, X, 1, False), float8_ffn]


def build(nc, ins, out, phases):
    with ExitStack() as ctx:
        X = ctx.enter_context(nc.sbuf_tensor("X", [P, NT, D], F32))
        load_x(nc, ins["x"], X)
        for n in phases:
            PHASES[n](nc, ins, X)
        store_x(nc, X, out)


_INS = [
    "x", "ctx_1024", "fside_BxSxS2_0", "mask_BxS2_if1",
    "L0_attn_q", "L0_attn_k", "L0_attn_log_decay", "L0_attn_norm_weight", "L0_attn_o_w",
    "L0_xattn_Wq", "L0_xattn_bq", "L0_xattn_Wk", "L0_xattn_bk", "L0_xattn_Wv", "L0_xattn_bv", "L0_xattn_Wo", "L0_xattn_bo",
    "L0_ffn_gate_w", "L0_ffn_w1", "L0_ffn_b1", "L0_ffn_w2", "L0_ffn_b2",
    "L1_attn_ln1_g", "L1_attn_ln1_b", "L1_attn_ln2_g", "L1_attn_ln2_b", "L1_attn_time_decay", "L1_attn_time_first",
    "L1_attn_time_mix_k", "L1_attn_time_mix_v", "L1_attn_time_mix_r",
    "L1_attn_att_Wk", "L1_attn_att_Wv", "L1_attn_att_Wr", "L1_attn_att_Wo", "L1_attn_cm_k", "L1_attn_cm_r",
    "L1_attn_ffn_Wk", "L1_attn_ffn_Wr", "L1_attn_ffn_Wv",
    "L1_xattn_Wq", "L1_xattn_bq", "L1_xattn_Wk", "L1_xattn_bk", "L1_xattn_Wv", "L1_xattn_bv", "L1_xattn_Wo", "L1_xattn_bo",
    "L1_xattn_lambda_bias", "L1_ffn_weight", "L1_ffn_bias",
]


def kernel(**inputs):
    import numpy as np
    import concourse.bacc as bacc
    from concourse.bass_utils import run_bass_kernel_spmd

    nc = bacc.Bacc("TRN2", target_bir_lowering=False, num_devices=1)
    arrays, ins = {}, {}
    for name in _INS:
        a = np.ascontiguousarray(inputs[name])
        a = a.reshape(a.shape or (1,))
        arrays[f"in_{name}_dram"] = a
        ins[name] = nc.dram_tensor(f"in_{name}_dram", a.shape, mybir.dt.from_np(a.dtype), kind="ExternalInput").ap()
    out = nc.dram_tensor("out_0_dram", (B, S, D), F32, kind="ExternalOutput").ap()
    build(nc, ins, out, range(len(PHASES)))
    r = run_bass_kernel_spmd(nc, [arrays], core_ids=[0])
    return r.results[0]["out_0_dram"]
```

```python
from contextlib import ExitStack

import concourse.bass as bass
from concourse import mybir

F32 = mybir.dt.float32
BF16 = mybir.dt.bfloat16
F16 = mybir.dt.float16
FP8 = mybir.dt.float8e4
I32 = mybir.dt.int32
U32 = mybir.dt.uint32
ALU = mybir.AluOpType
ACT = mybir.ActivationFunctionType
AX = mybir.AxisListType

P = 128
B = 16
S = 256
D = 256
H = 16
DH = D // H
NT = B * S // P
TB = S // P
DC = D // P
E = 8
HID = 1024
HC = HID // P
LN_EPS = 1e-5
HEAD = 1


class Chain:

    def __init__(self, eng, sem):
        self.eng, self.sem, self.n = eng, sem, 0

    def done(self, ins):
        self.n += 1
        return ins.then_inc(self.sem, 1)

    def wait(self):
        self.eng.wait_ge(self.sem, self.n)

    def close(self):
        self.wait()
        self.eng.sem_clear(self.sem)
        self.n = 0


def wait_alone(eng, stood, *waits):
    for sem, n in waits:
        eng.wait_ge(sem, n + HEAD)
    eng.sem_inc(stood, 1)


def make_identity(pool, ident, sem, dtype_one=1.0):
    pool.memset(ident, 0.0).then_inc(sem, 1)
    pool.wait_ge(sem, 1 + HEAD)
    pool.affine_select(out=ident, in_=ident, compare_op=ALU.not_equal, fill=1.0, base=0,
                       pattern=[[-1, P]], channel_multiplier=1).then_inc(sem, 1)


def transpose_blocks(pe, blocks, banks, ident, turned, freed):
    for g in range(0, len(blocks), 4):
        n = g // 4
        if n >= len(banks):
            pe.wait_ge(freed, n - len(banks) + 1 + HEAD)
        for j, block in enumerate(blocks[g:g + 4]):
            last = pe.transpose(banks[n % len(banks)][:, j * P:(j + 1) * P], block, ident)
        last.then_inc(turned, 1)


def evacuate_blocks(act, dests, banks, turned, freed):
    for n, dest in enumerate(dests):
        act.wait_ge(turned, n + 1 + HEAD)
        act.activation(dest, banks[n % len(banks)][:, 0:dest.shape[-1]], ACT.Copy).then_inc(freed, 1)


def layer_norm_stats(dve, chain, src, stats, aggr, measured):
    for t in range(TB):
        chain.done(dve.bn_stats(stats[:, t, :], src(t)))
    chain.wait()
    for t in range(TB):
        last = dve.bn_aggr(aggr[:, t, :], stats[:, t, :])
    last.then_inc(measured, 1)


def inverse_root(pool, out, in_, scale, add, minus_half, summed, ready, turn, stood):
    pool.tensor_scalar(out, in_, scale, add, ALU.mult, ALU.add).then_inc(summed, 1)
    wait_alone(pool, stood, (summed, turn + 1))
    pool.tensor_tensor(out, out, minus_half, ALU.pow).then_inc(ready, 1)


def layer_norm_apply(dve, src, out, aggr, rstd, normed):
    for t in range(TB):
        last = dve.tensor_scalar(out(t), src(t), aggr[:, t, 0:1], rstd[:, t:t + 1], ALU.subtract, ALU.mult)
    last.then_inc(normed, 1)


def sequences(eng):
    with eng.Fori(0, B // 2) as i:
        for s in range(2):
            yield 2 * i + s, s


def turns(eng, drain=False):
    yield 0, 0, 0
    with eng.Fori(0, B // 2 - 1) as i:
        yield 2 * i + 1, i, 1
        yield 2 * i + 2, i + 1, 0
    yield B - 1, B // 2 - 1, 1
    if drain:
        yield B, B // 2, 0


def tile_of(X, b, t):
    return X[:, bass.ds(b * TB + t, 1), :].rearrange("p a d -> p (a d)")


OWN = ("chain_", "stood_", "loaded", "ctx_in", "raw_in", "zeroed", "scattered")


class Phase:

    def __init__(self, nc, name):
        self.nc, self.name, self.ctx, self.sems = nc, name, ExitStack(), []
        self.no_head = []

    def __enter__(self):
        self.ctx.__enter__()
        return self

    def __exit__(self, *e):
        self.ctx.__exit__(*e)
        self.nc.clear_and_free_semaphores(self.sems)

    def sb(self, name, shape, dt=F32):
        return self.ctx.enter_context(self.nc.sbuf_tensor(f"{self.name}_{name}", shape, dt))

    def ps(self, name, shape=(P, 512), dt=F32):
        return self.ctx.enter_context(self.nc.psum_tensor(f"{self.name}_{name}", list(shape), dt))

    def sem(self, name):
        self.sems.append(self.nc.alloc_semaphore(f"{self.name}_{name}"))
        return self.sems[-1]

    def own(self, name):
        sem = self.sem(name)
        self.no_head.append(sem)
        return sem

    def block(self):
        self.nc.all_engine_barrier()
        for sem in self.sems:
            if sem not in self.no_head:
                self.nc.sync.sem_inc(sem, HEAD)
        self.nc.all_engine_barrier()
        return self.ctx.enter_context(self.nc.Block())


def flat(ap):
    return ap.rearrange("p a b -> p (a b)")


def columns(vec):
    return vec.rearrange("(c p) -> p c", p=P)


def load_x(nc, x, X):
    x_v = x.rearrange("b (t p) d -> p (b t) d", p=P)
    with Phase(nc, "load") as ph:
        arrived = ph.own("arrived")
        block = ph.block()

        @block.sync
        def _(sp):
            for q in range(4):
                sp.dma_start(X[:, 8 * q:8 * q + 8, :], x_v[:, 8 * q:8 * q + 8, :]).then_inc(arrived, 16)
            sp.wait_ge(arrived, 64)


def store_x(nc, X, out):
    out_v = out.rearrange("b (t p) d -> p (b t) d", p=P)
    with Phase(nc, "store") as ph:
        stored = ph.own("stored")
        block = ph.block()

        @block.sync
        def _(sp):
            for q in range(4):
                sp.dma_start(out_v[:, 8 * q:8 * q + 8, :], X[:, 8 * q:8 * q + 8, :]).then_inc(stored, 16)
            sp.wait_ge(stored, 64)


def decay_attention(nc, ins, X):
    with Phase(nc, "dec") as ph:
        ident = ph.sb("ident", [P, P])
        groups = ph.sb("groups", [P, P])
        ones = ph.sb("ones", [P, 1])
        w_nat = ph.sb("w_nat", [P, DC, D])
        wt = ph.sb("wt", [P, DC, D])
        q_col = ph.sb("q_col", [P, DC])
        k_col = ph.sb("k_col", [P, DC])
        qk = ph.sb("qk", [P, DC])
        nw = ph.sb("nw", [P, DC])
        ld = ph.sb("ld", [P, DC])
        lam = ph.sb("lam", [P, DC])
        coef = ph.sb("coef", [P, DC])
        xn = ph.sb("xn", [P, 2, TB, D])
        stats = ph.sb("stats", [P, TB, 6])
        aggr = ph.sb("aggr", [P, TB, 2])
        rstd = ph.sb("rstd", [P, TB])
        v = ph.sb("v", [P, 2, DC, S])
        o = ph.sb("o", [P, 2, DC, S])
        osq = ph.sb("osq", [P, 2, DC, S])
        sum_sq = ph.sb("sum_sq", [P, TB])
        rms = ph.sb("rms", [P, TB])
        minus_half = ph.sb("minus_half", [P, TB])
        p_t = [ph.ps(f"p_t{i}") for i in range(2)]
        p_y = [ph.ps(f"p_y{i}") for i in range(2)]
        p_m = ph.ps("p_m")

        loaded = ph.own("loaded")
        ident_ready, groups_ready = ph.sem("ident_ready"), ph.sem("groups_ready")
        turned, freed = ph.sem("turned"), ph.sem("freed")
        qk_ready, coef_sum, consts = ph.sem("qk_ready"), ph.sem("coef_sum"), ph.sem("consts")
        wt_ready = ph.sem("wt_ready")
        normed, turned_x, v_ready = ph.sem("normed"), ph.sem("turned_x"), ph.sem("v_ready")
        scanned, squared, y_ready, added = ph.sem("scanned"), ph.sem("squared"), ph.sem("y_ready"), ph.sem("added")
        measured, rstd_ready = ph.sem("measured"), ph.sem("rstd_ready")
        var_eps, mean_eps = ph.sem("var_eps"), ph.sem("mean_eps")
        sum_sq_ready, rms_ready = ph.sem("sum_sq_ready"), ph.sem("rms_ready")
        stood_v, stood_p = ph.own("stood_v"), ph.own("stood_p")
        chain_v, chain_a = ph.own("chain_v"), ph.own("chain_a")
        block = ph.block()

        @block.sync
        def _(sp):
            sp.dma_start(w_nat[:, :, :], ins["L0_attn_o_w"].rearrange("(c p) d -> p c d", p=P)).then_inc(loaded, 16)
            with nc.allow_non_contiguous_dma(reason="vectors of 256 numbers"):
                for dst, name in ((q_col, "L0_attn_q"), (k_col, "L0_attn_k"), (nw, "L0_attn_norm_weight")):
                    sp.dma_start(dst[:, :], columns(ins[name])).then_inc(loaded, 16)
                decay = ins["L0_attn_log_decay"].rearrange("(c h) -> h c", c=DC)
                for h in range(P // DH):
                    sp.dma_start(ld[h * DH:(h + 1) * DH, :],
                                 decay[h:h + 1, :].broadcast_to([DH, DC])).then_inc(loaded, 16)

        n_loads = 4 + P // DH

        @block.gpsimd
        def _(pool):
            make_identity(pool, ident[:, :], ident_ready)
            pool.memset(ones[:, :], 1.0).then_inc(groups_ready, 1)
            pool.memset(groups[:, :], 1.0).then_inc(groups_ready, 1)
            pool.memset(minus_half[:, :], -0.5).then_inc(groups_ready, 1)
            pool.wait_ge(groups_ready, 3 + HEAD)
            g3 = groups[:, :].rearrange("p (h r) -> p h r", r=DH)
            pool.affine_select(out=g3, in_=g3, compare_op=ALU.is_ge, fill=0.0, base=0,
                               pattern=[[-DH, P // DH], [0, DH]], channel_multiplier=1).then_inc(groups_ready, 1)
            pool.wait_ge(groups_ready, 4 + HEAD)
            pool.affine_select(out=g3, in_=g3, compare_op=ALU.is_ge, fill=0.0, base=DH - 1,
                               pattern=[[DH, P // DH], [0, DH]], channel_multiplier=-1).then_inc(groups_ready, 1)

            for b, s in sequences(pool):
                wait_alone(pool, stood_p, (measured, b + 1))
                inverse_root(pool, rstd[:, :], aggr[:, :, 1], 1.0, LN_EPS, minus_half[:, :], var_eps, rstd_ready, b, stood_p)
                wait_alone(pool, stood_p, (sum_sq_ready, b + 1))
                inverse_root(pool, rms[:, :], sum_sq[:, :], 1.0 / D, 1e-6, minus_half[:, :], mean_eps, rms_ready, b, stood_p)

        @block.tensor
        def _(pe):
            pe.wait_ge(loaded, 16 * n_loads)
            pe.wait_ge(ident_ready, 2 + HEAD)
            for ct in range(DC):
                for ot in range(DC):
                    last = pe.transpose(p_t[0][:, (ct * DC + ot) * P:(ct * DC + ot + 1) * P],
                                        w_nat[:, ot, ct * P:(ct + 1) * P], ident[:, :])
            last.then_inc(turned, 1)
            pe.wait_ge(groups_ready, 5 + HEAD)
            pe.wait_ge(qk_ready, 1 + HEAD)
            pe.matmul(p_t[1][:, 0:DC], groups[:, :], qk[:, :], start=True, stop=True).then_inc(coef_sum, 1)
            pe.wait_ge(wt_ready, DC + HEAD)
            pe.wait_ge(consts, 1 + HEAD)
            for b, s in sequences(pe):
                pe.wait_ge(normed, b + 1 + HEAD)
                pe.wait_ge(v_ready, b + HEAD)
                for c in range(DC):
                    for t in range(TB):
                        last = pe.transpose(p_t[0][:, c * S + t * P:c * S + (t + 1) * P],
                                            xn[:, s, t, c * P:(c + 1) * P], ident[:, :])
                last.then_inc(turned_x, 1)
                pe.wait_ge(scanned, b + 1 + HEAD)
                pe.wait_ge(squared, b + 1 + HEAD)
                pe.wait_ge(added, b + HEAD)
                for t in range(TB):
                    for c in range(DC):
                        last = pe.matmul(p_m[:, t:t + 1], osq[:, s, c, t * P:(t + 1) * P], ones[:, :],
                                         start=(c == 0), stop=(c == DC - 1))
                for t in range(TB):
                    for c in range(DC):
                        last = pe.matmul(p_y[0][:, t * D:(t + 1) * D], o[:, s, c, t * P:(t + 1) * P],
                                         wt[:, c, :], start=(c == 0), stop=(c == DC - 1))
                last.then_inc(y_ready, 1)

        @block.scalar
        def _(act):
            act.wait_ge(loaded, 16 * n_loads)
            act.activation(lam[:, :], ld[:, :], ACT.Exp, scale=-1.0).then_inc(chain_a, 1)
            act.wait_ge(turned, 1 + HEAD)
            for c in range(DC):
                act.activation(wt[:, c, :], p_t[0][:, c * D:(c + 1) * D], ACT.Copy, scale=nw[:, c:c + 1]).then_inc(wt_ready, 1)
            act.wait_ge(consts, 1 + HEAD)
            for b, s in sequences(act):
                act.wait_ge(turned_x, b + 1 + HEAD)
                act.wait_ge(scanned, b + HEAD)
                for c in range(DC):
                    last = act.activation(v[:, s, c, :], p_t[0][:, c * S:(c + 1) * S], ACT.Copy, scale=coef[:, c:c + 1])
                last.then_inc(v_ready, 1)
                act.wait_ge(scanned, b + 1 + HEAD)
                act.wait_ge(y_ready, b + HEAD)
                act.activation(osq[:, s, :, :], o[:, s, :, :], ACT.Square).then_inc(squared, 1)

        @block.vector
        def _(dve):
            dve.wait_ge(loaded, 16 * n_loads)
            dve.tensor_tensor(qk[:, :], q_col[:, :], k_col[:, :], ALU.mult).then_inc(qk_ready, 1)
            dve.wait_ge(chain_a, 1)
            chain = Chain(dve, chain_v)
            chain.done(dve.tensor_scalar(lam[:, :], lam[:, :], 1.0, None, ALU.add))
            chain.wait()
            chain.done(dve.reciprocal(lam[:, :], lam[:, :]))
            dve.wait_ge(coef_sum, 1 + HEAD)
            dve.tensor_copy(coef[:, :], p_t[1][:, 0:DC]).then_inc(consts, 1)
            chain.close()
            for b, s in sequences(dve):
                layer_norm_stats(dve, chain, lambda t: tile_of(X, b, t), stats, aggr, measured)
                dve.wait_ge(rstd_ready, b + 1 + HEAD)
                layer_norm_apply(dve, lambda t: tile_of(X, b, t), lambda t: xn[:, s, t, :], aggr, rstd, normed)
                dve.wait_ge(v_ready, b + 1 + HEAD)
                dve.wait_ge(y_ready, b + HEAD)
                for c in range(DC):
                    last = dve.tensor_tensor_scan(o[:, s, c, :], lam[:, c:c + 1].broadcast_to([P, S]),
                                                  v[:, s, c, :], 0.0, ALU.mult, ALU.add)
                last.then_inc(scanned, 1)
                dve.wait_ge(y_ready, b + 1 + HEAD)
                dve.tensor_copy(sum_sq[:, :], p_m[:, 0:TB]).then_inc(sum_sq_ready, 1)
                dve.wait_ge(rms_ready, b + 1 + HEAD)
                for t in range(TB):
                    last = dve.scalar_tensor_tensor(tile_of(X, b, t), p_y[0][:, t * D:(t + 1) * D], rms[:, t:t + 1],
                                                    tile_of(X, b, t), ALU.mult, ALU.add)
                last.then_inc(added, 1)
                wait_alone(dve, stood_v, (added, b + 1))
                chain.close()


PAIRS = H // 2
UNITS = TB * PAIRS
RB = 4
OFF = 1e30
VW = DH + 1


def cross_attention(nc, ins, X, layer, causal):
    low = causal
    DT = BF16 if low else F32
    name = f"L{layer}_xattn_"
    with Phase(nc, f"xa{layer}") as ph:
        ident = ph.sb("ident", [P, P], F32)
        ident_d = ph.sb("ident_d", [P, P], DT) if low else ident
        w_nat = ph.sb("w_nat", [P, 4, DC, D])
        w = ph.sb("w", [P, 4, DC, D], DT)
        cols = ph.sb("cols", [P, 2, DC])
        cols_d = ph.sb("cols_d", [P, 2, DC])
        rows = ph.sb("rows", [P, 2, D])
        rows_d = ph.sb("rows_d", [P, 2, D], DT) if low else rows
        side = ph.sb("side", [P, 2, 4])
        parity = ph.sb("parity", [P, 2])
        q_bias = ph.sb("q_bias", [P, DC, 2])
        lam_b = ph.sb("lam_b", [P, 1])
        minus_half = ph.sb("minus_half", [P, TB])
        stats = ph.sb("stats", [P, TB, 6])
        aggr = ph.sb("aggr", [P, TB, 2])
        rstd = ph.sb("rstd", [P, TB])
        ctx = ph.sb("ctx", [P, 2, TB, D])
        ctx_d = ph.sb("ctx_d", [P, TB, D], DT) if low else None
        xn = ph.sb("xn", [P, TB, D], DT)
        xT = ph.sb("xT", [P, DC, S], DT)
        cT = ph.sb("cT", [P, DC, S], DT)
        raw = ph.sb("raw", [P, 2, S], I32) if causal else ph.sb("raw", [P, 2, TB, S])
        key_off = ph.sb("key_off", [P, 2, S]) if causal else None
        neg = ph.sb("neg", [P, 2, TB, S])
        q_r = ph.sb("q_r", [P, DC, S], DT) if low else None
        q_f = ph.sb("q_f", [P, DC, S], DT) if low else None
        k_r = ph.sb("k_r", [P, DC, S], DT) if low else None
        v_r = ph.sb("v_r", [P, TB, D], DT) if low else None
        v_f = ph.sb("v_f", [P, TB, D], DT) if low else None
        q = ph.sb("q", [P, 2, 2, DC, S], DT)
        k = ph.sb("k", [P, 2, DC, S], DT)
        v = ph.sb("v", [P, 2, TB, H, VW])
        sc = ph.sb("sc", [P, RB, 2, S])
        nmax = ph.sb("nmax", [P, RB, 2])
        pr = ph.sb("pr", [P, RB, 2, S])
        prT = ph.sb("prT", [P, RB, 2, TB, P])
        inv = ph.sb("inv", [P, TB, H])
        o = ph.sb("o", [P, TB, D], DT)
        oT = ph.sb("oT", [P, DC, S], DT)
        y_r = ph.sb("y_r", [P, TB, D], DT) if low else None
        y_f = ph.sb("y_f", [P, TB, D], DT if low else F32)
        p_a = [ph.ps(f"p_a{i}") for i in range(2)]
        p_ad = [a[:, :].bitcast(BF16)[:, 0:512] if low else a for a in p_a]
        p_s = [ph.ps(f"p_s{i}") for i in range(2)]
        p_p = [ph.ps(f"p_p{i}") for i in range(2)]
        p_o = [ph.ps(f"p_o{i}") for i in range(2)]

        names = ("loaded_w loaded_c ident_ready turned freed consts cast ones_set "
                 "measured var_eps rstd_ready normed turned_x x_ready c_ready k_proj k_read q_proj q_read v_proj v_read "
                 "q_ready k_ready v_ready off_ready neg_ready scored shifted exped p_turned p_copied_a p_copied_v pv "
                 "o_ready turned_o oT_ready y_ready y_read added chain_v chain_a chain_p stood_v stood_p").split()
        (loaded_w, loaded_c, ident_ready, turned, freed, consts, cast, ones_set,
         measured, var_eps, rstd_ready, normed, turned_x, x_ready, c_ready, k_proj, k_read, q_proj, q_read, v_proj, v_read,
         q_ready, k_ready, v_ready, off_ready, neg_ready, scored, shifted, exped, p_turned, p_copied_a, p_copied_v, pv,
         o_ready, turned_o, oT_ready, y_ready, y_read, added, chain_v, chain_a, chain_p, stood_v, stood_p) = (
            ph.own(n) if n.startswith(OWN) else ph.sem(n) for n in names)
        if not low:
            k_read, q_read, v_read = k_ready, q_ready, v_ready
        ctx_in = [ph.own(f"ctx_in{s}") for s in range(2)]
        raw_in = [ph.own(f"raw_in{s}") for s in range(2)]
        block = ph.block()

        TURN, SUM = 2, 4
        AT_NORM, AT_X, AT_O, AT_K, AT_Y, AT_Q, AT_V = 1, 4, 6, 7, 8, 10, 12

        def keys(t):
            return (t + 1) * P if causal else S

        def live(b, m):
            return m >= 0 or not at(b, 0)

        def at(b, n):
            return isinstance(b, int) and b == n

        def has_before(b):
            return not at(b, 0)

        def has_next(b):
            return not isinstance(b, int) or b < B - 1

        @block.sync
        def _(sp):
            def load(b, h, s):
                sp.dma_start(ctx[:, s, :, :], ins["ctx_1024"][bass.ds(b, 1), :, :].rearrange("a (t p) d -> p (a t) d", p=P)).then_inc(ctx_in[s], 16)
                if causal:
                    sp.dma_start(raw[:, s, :], ins["mask_BxS2_if1"][bass.ds(b, 1), :].rearrange("a k -> (a k)").partition_broadcast(P)).then_inc(raw_in[s], 16)
                else:
                    sp.dma_start(raw[:, s, :, :], ins["fside_BxSxS2_0"][bass.ds(b, 1), :, :].rearrange("a (t p) k -> p (a t) k", p=P)).then_inc(raw_in[s], 16)

            load(0, 0, 0)
            for n, m in enumerate(("Wq", "Wk", "Wv", "Wo")):
                sp.dma_start(w_nat[:, n, :, :], ins[name + m].rearrange("(c p) d -> p c d", p=P)).then_inc(loaded_w, 16)
            with nc.allow_non_contiguous_dma(reason="vectors of 256 numbers"):
                for n, m in enumerate(("bq", "bk")):
                    sp.dma_start(cols[:, n, :], columns(ins[name + m])).then_inc(loaded_c, 16)
                for n, m in enumerate(("bv", "bo")):
                    sp.dma_start(rows[:, n, :], ins[name + m].partition_broadcast(P)).then_inc(loaded_c, 16)
                if not causal:
                    sp.dma_start(lam_b[:, :], ins["L1_xattn_lambda_bias"].partition_broadcast(P)).then_inc(loaded_c, 16)
            for b, h, s in turns(sp):
                if has_next(b):
                    if has_before(b):
                        sp.wait_ge(cast if low else turned_x, b + HEAD)
                        sp.wait_ge(neg_ready, b + HEAD)
                    load(b + 1, h + s, 1 - s)

        n_cols = 4 if causal else 5

        @block.gpsimd
        def _(pool):
            make_identity(pool, ident[:, :], ident_ready)
            chain = Chain(pool, chain_p)
            pool.wait_ge(ident_ready, 2 + HEAD)
            if low:
                chain.done(pool.tensor_copy(ident_d[:, :], ident[:, :]))
            chain.done(pool.memset(minus_half[:, :], -0.5))
            chain.done(pool.memset(v[:, :, :, :, :], 1.0))
            chain.done(pool.memset(side[:, :, :], -1.0 / DH ** 0.5))
            chain.wait()
            for n in range(2):
                chain.done(pool.affine_select(out=side[:, n, :], in_=side[:, n, :], compare_op=ALU.is_ge, fill=0.0,
                                              base=-DH * n, pattern=[[-2 * DH, 4]], channel_multiplier=1))
            chain.wait()
            for n in range(2):
                chain.done(pool.affine_select(out=side[:, n, :], in_=side[:, n, :], compare_op=ALU.is_ge, fill=0.0,
                                              base=DH * n + DH - 1, pattern=[[2 * DH, 4]], channel_multiplier=-1))
            chain.wait()
            pool.sem_inc(ones_set, 1)

            def prepare(b, h, s):
                if low:
                    pool.wait_ge(ctx_in[s], 16 * h + 16)
                    wait_alone(pool, stood_p, (turned_x, b))
                    pool.tensor_copy(ctx_d[:, :, :], ctx[:, s, :, :]).then_inc(cast, 1)
                wait_alone(pool, stood_p, (measured, b + 1))
                inverse_root(pool, rstd[:, :], aggr[:, :, 1], 1.0, LN_EPS, minus_half[:, :], var_eps, rstd_ready, b, stood_p)
                pool.wait_ge(raw_in[s], 16 * h + 16)
                if not isinstance(b, int) or b >= 2:
                    pool.wait_ge(shifted, UNITS * (b - 1) + HEAD)
                pool.sem_inc(stood_p, 1)
                if causal:
                    pool.tensor_scalar(key_off[:, s, :], raw[:, s, :], 0.0, OFF, ALU.is_le, ALU.mult).then_inc(off_ready, 1)
                    wait_alone(pool, stood_p, (off_ready, b + 1))
                    for t in range(TB):
                        last = pool.affine_select(out=neg[:, s, t, :], in_=key_off[:, s, :], compare_op=ALU.is_ge,
                                                  fill=OFF, base=t * P, pattern=[[-1, S]], channel_multiplier=1)
                    last.then_inc(neg_ready, 1)
                else:
                    pool.tensor_scalar(neg[:, s, :, :], raw[:, s, :, :], lam_b[:, 0:1], None, ALU.mult).then_inc(neg_ready, 1)

            if not causal:
                pool.wait_ge(consts, 1 + HEAD)
            prepare(0, 0, 0)
            for b, h, s in turns(pool):
                if has_next(b):
                    prepare(b + 1, h + s, 1 - s)

        def copied(m):
            return (p_copied_a, (m + 1) // 2) if m % 2 else (p_copied_v, m // 2 + 1)

        @block.tensor
        def _(pe):
            def turn(bank, tiles, done):
                for c in range(DC):
                    for t in range(TB):
                        last = pe.transpose(bank[:, c * S + t * P:c * S + (t + 1) * P], tiles(t)[:, c * P:(c + 1) * P], ident_d[:, :])
                if done is not None:
                    last.then_inc(done, 1)

            def project(bank, n, src, done):
                for oc in range(DC):
                    for ic in range(DC):
                        last = pe.matmul(bank[:, oc * S:(oc + 1) * S], w[:, n, ic, oc * P:(oc + 1) * P],
                                         src[:, ic, :], start=(ic == 0), stop=(ic == DC - 1))
                last.then_inc(done, 1)

            def project_rows(bank, src, n, done):
                for t in range(TB):
                    for ic in range(DC):
                        last = pe.matmul(bank[:, t * D:(t + 1) * D], src[:, ic, t * P:(t + 1) * P], w[:, n, ic, :],
                                         start=(ic == 0), stop=(ic == DC - 1))
                last.then_inc(done, 1)

            def turn_inputs(b, h, s):
                pe.wait_ge(normed, b + 1 + HEAD)
                if low:
                    pe.wait_ge(cast, b + 1 + HEAD)
                else:
                    pe.wait_ge(ctx_in[s], 16 * h + 16)
                if not at(b, 0):
                    pe.wait_ge(v_read, b + HEAD)
                    pe.wait_ge(q_read, b + HEAD)
                turn(p_ad[0], lambda t: xn[:, t, :], None)
                turn(p_ad[1], lambda t: ctx_d[:, t, :] if low else ctx[:, s, t, :], turned_x)

            def project_keys(b):
                pe.wait_ge(c_ready, b + 1 + HEAD)
                project(p_a[1], 1, cT, k_proj)

            def project_queries(b):
                pe.wait_ge(x_ready, b + 1 + HEAD)
                pe.wait_ge(k_read, b + 1 + HEAD)
                project(p_a[1], 0, xT, q_proj)

            def project_values(b):
                if not at(b, 0) and not at(b, 1):
                    pe.wait_ge(y_read, b - 1 + HEAD)
                project_rows(p_a[0], cT, 2, v_proj)

            def scores(b, s, n):
                t, j = divmod(n, PAIRS)
                if n == 0:
                    pe.wait_ge(q_ready, b + 1 + HEAD)
                    pe.wait_ge(k_ready, b + 1 + HEAD)
                if live(b, n - 2):
                    pe.wait_ge(shifted, UNITS * b + n - 1 + HEAD)
                for e in range(2):
                    h = 2 * j + e
                    c, r = h // 8, 32 * (h % 8 // 2)
                    last = pe.matmul(p_s[n % 2][:, e * S:e * S + keys(t)], q[r:r + 32, s, e, c, t * P:(t + 1) * P],
                                     k[r:r + 32, s, c, 0:keys(t)], start=True, stop=True)
                last.then_inc(scored, 1)

            def turn_unit(b, m):
                t = m % UNITS // PAIRS
                pe.wait_ge(exped, UNITS * b + m + 1 + HEAD)
                if live(b, m - 2):
                    former, count = copied(m - 2)
                    pe.wait_ge(former, UNITS // 2 * b + count + HEAD)
                for e in range(2):
                    for kt in range(keys(t) // P):
                        last = pe.transpose(p_p[m % 2][:, (e * TB + kt) * P:(e * TB + kt + 1) * P],
                                            pr[:, m % RB, e, kt * P:(kt + 1) * P], ident[:, :])
                last.then_inc(p_turned, 1)

            def sum_unit(b, s, m):
                t, j = divmod(m % UNITS, PAIRS)
                nk = keys(t) // P
                own, count = copied(m)
                pe.wait_ge(own, UNITS // 2 * b + count + HEAD)
                if j == 0:
                    if t == 0:
                        pe.wait_ge(v_ready, b + 1 + HEAD)
                    if not at(b, 0):
                        pe.wait_ge(o_ready, TB * (b - 1) + t + 1 + HEAD)
                for e in range(2):
                    h = 2 * j + e
                    for kt in range(nk):
                        last = pe.matmul(p_o[t][:, h * VW:(h + 1) * VW], prT[:, m % RB, e, kt, :],
                                         v[:, s, kt, h, :], start=(kt == 0), stop=(kt == nk - 1))
                last.then_inc(pv, 1)

            pe.wait_ge(ident_ready, 2 + HEAD)
            pe.wait_ge(ones_set, 1 + HEAD)
            if not low:
                pe.wait_ge(loaded_w, 64)
                blocks = [w_nat[:, n, ot, ct * P:(ct + 1) * P] for n in range(4) for ct in range(DC) for ot in range(DC)]
                transpose_blocks(pe, blocks, p_a, ident[:, :], turned, freed)
            pe.wait_ge(freed, (1 if low else 4) + HEAD)
            pe.wait_ge(consts, 1 + HEAD)
            turn_inputs(0, 0, 0)
            project_keys(0)
            project_queries(0)
            project_values(0)
            for b, h, s in turns(pe, drain=True):
                for n in range(UNITS):
                    if at(b, B) and n > AT_Y:
                        break
                    if not at(b, B):
                        scores(b, s, n)
                    if live(b, n - TURN) and (not at(b, B) or n < TURN):
                        turn_unit(b, n - TURN)
                    if live(b, n - SUM) and (not at(b, B) or n < SUM):
                        sum_unit(b, s if n >= SUM else 1 - s, n - SUM)
                    if n == AT_X and has_next(b):
                        turn_inputs(b + 1, h + s, 1 - s)
                    if n == AT_O and has_before(b):
                        pe.wait_ge(o_ready, TB * b + HEAD)
                        if has_next(b):
                            pe.wait_ge(x_ready, b + 2 + HEAD)
                        turn(p_ad[0], lambda t: o[:, t, :], turned_o)
                    if n == AT_K and has_next(b):
                        project_keys(b + 1)
                    if n == AT_Y and has_before(b):
                        pe.wait_ge(oT_ready, b + HEAD)
                        project_rows(p_a[0], oT, 3, y_ready)
                    if n == AT_Q and has_next(b):
                        project_queries(b + 1)
                    if n == AT_V and has_next(b):
                        project_values(b + 1)

        def turned_unit(m):
            nk = keys(m % UNITS // PAIRS) // P
            return prT[:, m % RB, :, 0:nk, :], p_p[m % 2][:, :].rearrange("p (e k q) -> p e k q", e=2, k=TB)[:, :, 0:nk, :]

        @block.scalar
        def _(act):
            def read_x(b):
                act.wait_ge(turned_x, b + 1 + HEAD)
                if not at(b, 0):
                    act.wait_ge(q_proj, b + HEAD)
                act.activation(flat(xT[:, :, :]), p_ad[0][:, :], ACT.Copy).then_inc(x_ready, 1)

            def read_keys(b):
                act.wait_ge(k_proj, b + 1 + HEAD)
                if not at(b, 0):
                    act.wait_ge(k_ready, b + HEAD)
                act.activation(flat(k_r[:, :, :]), p_a[1][:, :], ACT.Copy).then_inc(k_read, 1)

            def read_queries(b, s):
                act.wait_ge(q_proj, b + 1 + HEAD)
                if low:
                    if not at(b, 0):
                        act.wait_ge(q_ready, b + HEAD)
                    act.activation(flat(q_r[:, :, :]), p_a[1][:, :], ACT.Copy).then_inc(q_read, 1)
                else:
                    if not at(b, 0):
                        act.wait_ge(scored, UNITS * (b - 1) + HEAD)
                    for e in range(2):
                        for c in range(DC):
                            last = act.activation(q[:, s, e, c, :], p_a[1][:, c * S:(c + 1) * S], ACT.Identity,
                                                  bias=q_bias[:, c, e:e + 1], scale=parity[:, e:e + 1])
                    last.then_inc(q_ready, 1)

            def read_values(b):
                act.wait_ge(v_proj, b + 1 + HEAD)
                if not at(b, 0):
                    act.wait_ge(v_ready, b + HEAD)
                act.activation(flat(v_r[:, :, :]), p_a[0][:, :], ACT.Copy).then_inc(v_read, 1)

            act.wait_ge(loaded_w, 64)
            if low:
                act.activation(w[:, :, :, :], w_nat[:, :, :, :], ACT.Copy).then_inc(freed, 1)
            else:
                evacuate_blocks(act, [flat(w[:, n, :, :]) for n in range(4)], p_a, turned, freed)
            act.wait_ge(consts, 1 + HEAD)
            read_x(0)
            if low:
                read_keys(0)
            read_queries(0, 0)
            if low:
                read_values(0)
            for b, h, s in turns(act, drain=True):
                for n in range(UNITS):
                    if at(b, B) and n > AT_Y:
                        break
                    if not at(b, B):
                        t = n // PAIRS
                        act.wait_ge(shifted, UNITS * b + n + 1 + HEAD)
                        if live(b, n - RB):
                            act.wait_ge(p_turned, UNITS * b + n - RB + 1 + HEAD)
                        for e in range(2):
                            last = act.activation(pr[:, n % RB, e, 0:keys(t)], sc[:, n % RB, e, 0:keys(t)], ACT.Exp,
                                                  bias=nmax[:, n % RB, e:e + 1], scale=-1.0)
                        last.then_inc(exped, 1)
                    m = n - TURN
                    if m % 2 == 1 and live(b, m) and (not at(b, B) or n < TURN):
                        act.wait_ge(p_turned, UNITS * b + m + 1 + HEAD)
                        if live(b, m - RB):
                            act.wait_ge(pv, UNITS * b + m - RB + 1 + HEAD)
                        act.activation(*turned_unit(m), ACT.Copy).then_inc(p_copied_a, 1)
                    if n == AT_X and has_next(b):
                        read_x(b + 1)
                    if n == AT_O and has_before(b):
                        act.wait_ge(turned_o, b + HEAD)
                        if not at(b, 1):
                            act.wait_ge(y_ready, b - 1 + HEAD)
                        act.activation(flat(oT[:, :, :]), p_ad[0][:, :], ACT.Copy).then_inc(oT_ready, 1)
                    if n == AT_K and has_next(b) and low:
                        read_keys(b + 1)
                    if n == AT_Y and has_before(b) and low:
                        act.wait_ge(y_ready, b + HEAD)
                        if not at(b, 1):
                            act.wait_ge(added, b - 1 + HEAD)
                        act.activation(flat(y_r[:, :, :]), p_a[0][:, :], ACT.Copy).then_inc(y_read, 1)
                    if n == AT_Q and has_next(b):
                        read_queries(b + 1, 1 - s)
                    if n == AT_V and has_next(b) and low:
                        read_values(b + 1)

        @block.vector
        def _(dve):
            chain = Chain(dve, chain_v)

            def measure(b):
                layer_norm_stats(dve, chain, lambda t: tile_of(X, b, t), stats, aggr, measured)

            def norm(b):
                dve.wait_ge(rstd_ready, b + 1 + HEAD)
                if not at(b, 0):
                    dve.wait_ge(turned_x, b + HEAD)
                layer_norm_apply(dve, lambda t: tile_of(X, b, t), lambda t: xn[:, t, :], aggr, rstd, normed)

            def read_context(b):
                dve.wait_ge(turned_x, b + 1 + HEAD)
                if not at(b, 0):
                    dve.wait_ge(v_proj, b + HEAD)
                dve.tensor_copy(flat(cT[:, :, :]), p_ad[1][:, :]).then_inc(c_ready, 1)

            def finish_keys(b, s):
                dve.wait_ge(k_read if low else k_proj, b + 1 + HEAD)
                if not at(b, 0):
                    dve.wait_ge(scored, UNITS * (b - 1) + HEAD)
                for c in range(DC):
                    last = dve.tensor_scalar(k[:, s, c, :], k_r[:, c, :] if low else p_a[1][:, c * S:(c + 1) * S],
                                             cols_d[:, 1, c:c + 1], None, ALU.add)
                    if c < DC - 1:
                        chain.done(last)
                last.then_inc(k_ready, 1)

            def finish_queries(b, s):
                dve.wait_ge(q_read, b + 1 + HEAD)
                if not at(b, 0):
                    dve.wait_ge(scored, UNITS * (b - 1) + HEAD)
                for c in range(DC):
                    chain.done(dve.tensor_scalar(q_f[:, c, :], q_r[:, c, :], cols_d[:, 0, c:c + 1], None, ALU.add))
                chain.wait()
                for e in range(2):
                    last = dve.tensor_scalar(q[:, s, e, :, :], q_f[:, :, :], parity[:, e:e + 1], None, ALU.mult)
                last.then_inc(q_ready, 1)

            def finish_values(b, s):
                if low:
                    dve.wait_ge(v_read, b + 1 + HEAD)
                    for t in range(TB):
                        chain.done(dve.tensor_tensor(v_f[:, t, :], v_r[:, t, :], rows_d[:, 0, :], ALU.add))
                    chain.wait()
                    dve.tensor_copy(v[:, s, :, :, 0:DH], v_f[:, :, :].rearrange("p t (h r) -> p t h r", r=DH)).then_inc(v_ready, 1)
                else:
                    dve.wait_ge(v_proj, b + 1 + HEAD)
                    if not at(b, 0):
                        dve.wait_ge(pv, UNITS * (b - 1) + HEAD)
                    for t in range(TB):
                        last = dve.tensor_tensor(v[:, s, t, :, 0:DH], p_a[0][:, t * D:(t + 1) * D].rearrange("p (h r) -> p h r", r=DH),
                                                 rows[:, 0, :].rearrange("p (h r) -> p h r", r=DH), ALU.add)
                    last.then_inc(v_ready, 1)

            dve.wait_ge(loaded_c, 16 * n_cols)
            dve.wait_ge(ones_set, 1 + HEAD)
            chain.done(dve.tensor_reduce(parity[:, :], side[:, :, :], AX.X, ALU.add))
            if low:
                chain.done(dve.tensor_copy(rows_d[:, :, :], rows[:, :, :]))
                chain.done(dve.tensor_copy(q_r[:, 0, 0:2 * DC], flat(cols[:, :, :])))
                chain.wait()
                chain.done(dve.tensor_copy(flat(cols_d[:, :, :]), q_r[:, 0, 0:2 * DC]))
            else:
                chain.wait()
                for e in range(2):
                    chain.done(dve.tensor_scalar(q_bias[:, :, e], cols[:, 0, :], parity[:, e:e + 1], None, ALU.mult))
                chain.done(dve.tensor_copy(cols_d[:, :, :], cols[:, :, :]))
                chain.done(dve.tensor_scalar(lam_b[:, :], lam_b[:, :], -1.0, None, ALU.mult))
            chain.wait()
            dve.sem_inc(consts, 1)
            measure(0)
            norm(0)
            read_context(0)
            finish_keys(0, 0)
            if low:
                finish_queries(0, 0)
            finish_values(0, 0)
            chain.close()
            for b, h, s in turns(dve, drain=True):
                for n in range(UNITS):
                    if at(b, B) and n > AT_Y + 1:
                        break
                    if not at(b, B):
                        t = n // PAIRS
                        if n == 0:
                            dve.wait_ge(neg_ready, b + 1 + HEAD)
                            dve.sem_inc(stood_v, 1)
                        if live(b, n - RB):
                            wait_alone(dve, stood_v, (scored, UNITS * b + n + 1), (exped, UNITS * b + n - RB + 1))
                        else:
                            dve.wait_ge(scored, UNITS * b + n + 1 + HEAD)
                        for e in range(2):
                            last = dve.tensor_tensor_reduce(
                                out=sc[:, n % RB, e, 0:keys(t)], in0=p_s[n % 2][:, e * S:e * S + keys(t)],
                                in1=neg[:, s, t, 0:keys(t)], scale=1.0, scalar=3e38, op0=ALU.add, op1=ALU.min,
                                accum_out=nmax[:, n % RB, e:e + 1])
                        last.then_inc(shifted, 1)
                    m = n - TURN
                    if m % 2 == 0 and live(b, m) and (not at(b, B) or n < TURN):
                        dve.wait_ge(p_turned, UNITS * b + m + 1 + HEAD)
                        if live(b, m - RB):
                            dve.wait_ge(pv, UNITS * b + m - RB + 1 + HEAD)
                        dve.tensor_copy(*turned_unit(m)).then_inc(p_copied_v, 1)
                    m = n - SUM
                    if m % PAIRS == 0 and live(b, m - 1) and (not at(b, B) or n == SUM):
                        t = (m - 1) % UNITS // PAIRS
                        dve.wait_ge(pv, UNITS * b + m + HEAD)
                        heads = p_o[t][:, 0:H * VW].rearrange("p (h r) -> p h r", r=VW)
                        chain.done(dve.reciprocal(inv[:, t, :], heads[:, :, DH]))
                        chain.wait()
                        if m > 0 and not at(b, 0) and not at(b, 1):
                            dve.wait_ge(turned_o, b - 1 + HEAD)
                        dve.tensor_tensor(o[:, t, :].rearrange("p (h r) -> p h r", r=DH), heads[:, :, 0:DH],
                                          inv[:, t, :].unsqueeze(2).broadcast_to([P, H, DH]), ALU.mult).then_inc(o_ready, 1)
                    if n == AT_NORM and has_next(b):
                        measure(b + 1)
                    if n == AT_NORM + 1 and has_next(b):
                        norm(b + 1)
                    if n == AT_X and has_next(b):
                        read_context(b + 1)
                    if n == AT_K + 1 and has_next(b):
                        finish_keys(b + 1, 1 - s)
                    if n == AT_Y + 1 and has_before(b):
                        dve.wait_ge(y_read if low else y_ready, b + HEAD)
                        y_src = flat(y_r[:, :, :]) if low else p_a[0][:, :]
                        for t in range(TB):
                            chain.done(dve.tensor_tensor(y_f[:, t, :], y_src[:, t * D:(t + 1) * D], rows_d[:, 1, :], ALU.add))
                        chain.wait()
                        if not low:
                            dve.sem_inc(y_read, 1)
                        for t in range(TB):
                            last = dve.tensor_tensor(tile_of(X, b - 1, t), y_f[:, t, :], tile_of(X, b - 1, t), ALU.add)
                            if t < TB - 1:
                                chain.done(last)
                        last.then_inc(added, 1)
                    if n == AT_Q + 1 and has_next(b) and low:
                        finish_queries(b + 1, 1 - s)
                    if n == AT_V + 1 and has_next(b):
                        finish_values(b + 1, 1 - s)
                chain.close()
            dve.wait_ge(added, B + HEAD)


G = 256
TG = G // P
NG = 2 * B * S // G + E - 1
RING = 3
GR = 8


def experts_ffn(nc, ins, X):
    rows_in = nc.dram_tensor("moe_rows_in", (NG * G, D), F32, kind="Internal").ap()
    rows_out = nc.dram_tensor("moe_rows_out", (NG * G, D), F32, kind="Internal").ap()
    with Phase(nc, "moe") as ph:
        ident = ph.sb("ident", [P, P])
        below = ph.sb("below", [P, P])
        ones = ph.sb("ones", [P, P])
        zeros = ph.sb("zeros", [P, D])
        minus_half = ph.sb("minus_half", [P, TB])
        gate = ph.sb("gate", [E, D])
        gateT = ph.sb("gateT", [P, DC, E])
        b1_nat = ph.sb("b1_nat", [E * HC, P])
        b1 = ph.sb("b1", [P, E * HC])
        b2 = ph.sb("b2", [P, E, D])
        stats = ph.sb("stats", [P, TB, 6])
        aggr = ph.sb("aggr", [P, TB, 2])
        rstd = ph.sb("rstd", [P, TB])
        XN = ph.sb("XN", [P, NT, D])
        XN_s = [ph.sb(f"XN_s{i}", [P, TB, D]) for i in range(2)]
        xT = ph.sb("xT", [P, DC, S])
        lg = ph.sb("lg", [P, NT, E])
        falling = ph.sb("falling", [P, E])
        ramp_i = ph.sb("ramp_i", [P, NG], I32)
        ramp = ph.sb("ramp", [P, NG])
        steps = ph.sb("steps", [P, B])
        best = ph.sb("best", [P, 2, NT])
        pick = ph.sb("pick", [P, 2, NT, E])
        cand = ph.sb("cand", [P, NT, E])
        cmax = ph.sb("cmax", [P, NT])
        lg2 = ph.sb("lg2", [P, NT, E])
        probs = ph.sb("probs", [P, NT, E])
        zsum = ph.sb("zsum", [P, NT])
        gap = ph.sb("gap", [P, NT])
        wsum = ph.sb("wsum", [P, NT])
        wt = ph.sb("wt", [P, 2, NT])
        both = ph.sb("both", [P, NT, E])
        before = ph.sb("before", [P, NT, E])
        total = ph.sb("total", [P, NT, E])
        upto = ph.sb("upto", [P, NT, E])
        over = ph.sb("over", [P, E, B])
        ngroups = ph.sb("ngroups", [P, E])
        gend = ph.sb("gend", [P, E])
        gstart = ph.sb("gstart", [P, E])
        passed = ph.sb("passed", [P, NG, E - 1])
        owner = ph.sb("owner", [P, NG])
        owner_i = ph.sb("owner_i", [P, NG], I32)
        place = ph.sb("place", [P, 2, NT])
        place_i = ph.sb("place_i", [P, 2, NT], U32)
        w1 = ph.sb("w1", [P, RING, DC, HID])
        w2 = ph.sb("w2", [P, RING, HC, D])
        gx = ph.sb("gx", [P, RING, TG, D])
        gT = ph.sb("gT", [P, DC, G])
        hT = ph.sb("hT", [P, HC, G])
        gy = ph.sb("gy", [P, RING, TG, D])
        got = ph.sb("got", [P, GR, D])
        p_t = ph.ps("p_t")
        p_c = ph.ps("p_c")
        p_h = [ph.ps(f"p_h{i}") for i in range(3)]
        p_y = ph.ps("p_y")
        names = ("loaded zeroed ident_ready set_up turned freed measured var_eps rstd_ready normed turned_x xT_ready logits lg_read "
                 "gap_ready exp_ready both_ready counted routed scattered gT_turned gT_ready hidden gelu_ready y_ready gy_ready stored "
                 "combined chain_v chain_p stood_v stood_p").split()
        s_ = {n: ph.own(n) if n.startswith(OWN) else ph.sem(n) for n in names}
        fed = [ph.own(f"fed{i}") for i in range(RING)]
        kept = [ph.sem(f"kept{i}") for i in range(RING)]
        gathered = [ph.own(f"gathered{i}") for i in range(GR)]
        block = ph.block()

        def groups(eng):
            with eng.Fori(0, NG // RING) as i:
                for r in range(RING):
                    yield i, RING * i + r, r

        def expert_of(eng, j):
            return eng.value_load(owner_i[0:1, bass.ds(j, 1)], min_val=0, max_val=E - 1)

        @block.sync
        def _(sp):
            sp.dma_start(gate[:, :], ins["L0_ffn_gate_w"]).then_inc(s_["loaded"], 16)
            sp.dma_start(b1_nat[:, :], ins["L0_ffn_b1"].rearrange("e (c p) -> (e c) p", p=P)).then_inc(s_["loaded"], 16)
            sp.dma_start(b2[:, :, :], ins["L0_ffn_b2"].partition_broadcast(P)).then_inc(s_["loaded"], 16)
            sp.wait_ge(s_["set_up"], 1 + HEAD)
            zero_src = zeros[:, :].unsqueeze(1).broadcast_to([P, NG * TG, D])
            sp.dma_start(rows_in.rearrange("(n p) d -> p n d", p=P), zero_src).then_inc(s_["zeroed"], 16)
            sp.wait_ge(s_["routed"], 1 + HEAD)
            sp.wait_ge(s_["scattered"], 16 * 2 * NT)
            for i, j, r in groups(sp):
                e = expert_of(sp, j)
                sp.wait_ge(s_["y_ready"], 3 * i + HEAD)
                sp.dma_start(gx[:, r, :, :], rows_in[bass.ds(j * G, G), :].rearrange("(t p) d -> p t d", p=P)).then_inc(fed[r], 16)
                sp.dma_start(w1[:, r, :, :], ins["L0_ffn_w1"][bass.ds(e, 1), :, :].rearrange("a (c p) h -> p (a c) h", p=P)).then_inc(fed[r], 16)
                sp.dma_start(w2[:, r, :, :], ins["L0_ffn_w2"][bass.ds(e, 1), :, :].rearrange("a (c p) d -> p (a c) d", p=P)).then_inc(fed[r], 16)

        @block.gpsimd
        def _(pool):
            make_identity(pool, ident[:, :], s_["ident_ready"])
            chain = Chain(pool, s_["chain_p"])
            chain.done(pool.memset(zeros[:, :], 0.0))
            chain.done(pool.memset(ones[:, :], 1.0))
            chain.done(pool.memset(minus_half[:, :], -0.5))
            chain.done(pool.iota(ramp_i[:, :], [[1, NG]], base=0, channel_multiplier=0))
            chain.wait()
            chain.done(pool.tensor_copy(ramp[:, :], ramp_i[:, :]))
            chain.done(pool.affine_select(out=below[:, :], in_=ones[:, :], compare_op=ALU.is_gt, fill=0.0, base=0,
                                          pattern=[[1, P]], channel_multiplier=-1))
            chain.wait()
            chain.done(pool.tensor_scalar(falling[:, :], ramp[:, 0:E], -1.0, float(E), ALU.mult, ALU.add))
            chain.done(pool.tensor_scalar(steps[:, :], ramp[:, 0:B], float(G), None, ALU.mult))
            chain.wait()
            pool.sem_inc(s_["set_up"], 1)
            for b, s in sequences(pool):
                wait_alone(pool, s_["stood_p"], (s_["measured"], b + 1))
                inverse_root(pool, rstd[:, :], aggr[:, :, 1], 1.0, LN_EPS, minus_half[:, :], s_["var_eps"], s_["rstd_ready"], b, s_["stood_p"])
            pool.wait_ge(s_["routed"], 1 + HEAD)
            pool.wait_ge(s_["zeroed"], 16)
            for t in range(NT):
                for k in range(2):
                    pool.indirect_dma_start(rows_in, bass.IndirectOffsetOnAxis(ap=place_i[:, k, t:t + 1], axis=0),
                                            XN[:, t, :], None).then_inc(s_["scattered"], 16)
            for r in range(RING):
                pool.wait_ge(kept[r], 16 * (NG // RING) + HEAD)
            for n in range(2 * NT):
                t, k = divmod(n, 2)
                if n >= GR:
                    pool.wait_ge(s_["combined"], n - GR + 1 + HEAD)
                pool.indirect_dma_start(got[:, n % GR, :], None, rows_out,
                                        bass.IndirectOffsetOnAxis(ap=place_i[:, k, t:t + 1], axis=0)).then_inc(gathered[n % GR], 16)

        @block.tensor
        def _(pe):
            pe.wait_ge(s_["loaded"], 48)
            pe.wait_ge(s_["ident_ready"], 2 + HEAD)
            for c in range(DC):
                pe.transpose(p_t[:, c * E:(c + 1) * E], gate[:, c * P:(c + 1) * P], ident[0:E, 0:E])
            pe.transpose(p_t[:, 2 * P:2 * P + E * HC], b1_nat[:, :], ident[0:E * HC, 0:E * HC]).then_inc(s_["turned"], 1)
            pe.wait_ge(s_["freed"], 1 + HEAD)
            for b, s in sequences(pe):
                pe.wait_ge(s_["normed"], b + 1 + HEAD)
                for c in range(DC):
                    for t in range(TB):
                        last = pe.transpose(p_t[:, c * S + t * P:c * S + (t + 1) * P], XN_s[s][:, t, c * P:(c + 1) * P], ident[:, :])
                last.then_inc(s_["turned_x"], 1)
                pe.wait_ge(s_["xT_ready"], b + 1 + HEAD)
                pe.wait_ge(s_["lg_read"], b + HEAD)
                for t in range(TB):
                    for ic in range(DC):
                        last = pe.matmul(p_c[:, t * E:(t + 1) * E], xT[:, ic, t * P:(t + 1) * P], gateT[:, ic, :],
                                         start=(ic == 0), stop=(ic == DC - 1))
                last.then_inc(s_["logits"], 1)
            pe.wait_ge(s_["both_ready"], 1 + HEAD)
            pe.wait_ge(s_["lg_read"], B + HEAD)
            both_v = both[:, :, :].rearrange("p t e -> p (t e)")
            pe.matmul(p_c[:, 0:NT * E], below[:, :], both_v, start=True, stop=True)
            pe.matmul(p_t[:, 0:NT * E], ones[:, :], both_v, start=True, stop=True).then_inc(s_["counted"], 1)
            pe.wait_ge(s_["routed"], 1 + HEAD)
            for i, j, r in groups(pe):
                pe.wait_ge(fed[r], 48 * i + 48)
                pe.wait_ge(s_["gT_ready"], j + HEAD)
                for c in range(DC):
                    for t in range(TG):
                        last = pe.transpose(p_t[:, c * G + t * P:c * G + (t + 1) * P], gx[:, r, t, c * P:(c + 1) * P], ident[:, :])
                last.then_inc(s_["gT_turned"], 1)
                pe.wait_ge(s_["gT_ready"], j + 1 + HEAD)
                for n in range(HC // 2):
                    pe.wait_ge(s_["gelu_ready"], HC // 2 * j + max(n - 2, 0) + HEAD)
                    for k in range(2):
                        for ic in range(DC):
                            last = pe.matmul(p_h[n % 3][:, k * G:(k + 1) * G], w1[:, r, ic, (2 * n + k) * P:(2 * n + k + 1) * P], gT[:, ic, :],
                                             start=(ic == 0), stop=(ic == DC - 1))
                    last.then_inc(s_["hidden"], 1)
                pe.wait_ge(s_["gy_ready"], j + HEAD)
                for t in range(TG):
                    for hc in range(HC):
                        if t == 0 and hc % 2 == 0:
                            pe.wait_ge(s_["gelu_ready"], HC // 2 * j + hc // 2 + 1 + HEAD)
                        last = pe.matmul(p_y[:, t * D:(t + 1) * D], hT[:, hc, t * P:(t + 1) * P], w2[:, r, hc, :],
                                         start=(hc == 0), stop=(hc == HC - 1))
                last.then_inc(s_["y_ready"], 1)

        @block.scalar
        def _(act):
            act.wait_ge(s_["turned"], 1 + HEAD)
            act.activation(gateT[:, :, :].rearrange("p c e -> p (c e)"), p_t[:, 0:DC * E], ACT.Copy)
            act.activation(b1[:, :], p_t[:, 2 * P:2 * P + E * HC], ACT.Copy).then_inc(s_["freed"], 1)
            for b, s in sequences(act):
                act.wait_ge(s_["turned_x"], b + 1 + HEAD)
                act.wait_ge(s_["logits"], b + HEAD)
                act.activation(flat(xT[:, :, :]), p_t[:, :], ACT.Copy).then_inc(s_["xT_ready"], 1)
            act.wait_ge(s_["gap_ready"], 1 + HEAD)
            act.activation(probs[:, :, :], probs[:, :, :], ACT.Exp)
            act.activation(gap[:, :], gap[:, :], ACT.Exp).then_inc(s_["exp_ready"], 1)
            act.wait_ge(s_["routed"], 1 + HEAD)
            for i, j, r in groups(act):
                e = expert_of(act, j)
                for n in range(HC // 2):
                    act.wait_ge(s_["hidden"], HC // 2 * j + n + 1 + HEAD)
                    if n == 0:
                        act.wait_ge(s_["y_ready"], j + HEAD)
                    for k in range(2):
                        last = act.activation(hT[:, 2 * n + k, :], p_h[n % 3][:, k * G:(k + 1) * G], ACT.Gelu,
                                              bias=b1[:, bass.ds(e * HC + 2 * n + k, 1)])
                    last.then_inc(s_["gelu_ready"], 1)
                act.wait_ge(s_["gy_ready"], j + 1 + HEAD)
                act.dma_start(rows_out[bass.ds(j * G, G), :].rearrange("(t p) d -> p t d", p=P), gy[:, r, :, :]).then_inc(kept[r], 16)

        @block.vector
        def _(dve):
            chain = Chain(dve, s_["chain_v"])

            def step(ins_):
                chain.done(ins_)
                chain.wait()

            dve.wait_ge(s_["set_up"], 1 + HEAD)
            for b, s in sequences(dve):
                layer_norm_stats(dve, chain, lambda t: tile_of(X, b, t), stats, aggr, s_["measured"])
                dve.wait_ge(s_["rstd_ready"], b + 1 + HEAD)
                dve.wait_ge(s_["turned_x"], b + HEAD)
                for t in range(TB):
                    chain.done(dve.tensor_scalar(XN_s[s][:, t, :], tile_of(X, b, t), aggr[:, t, 0:1], rstd[:, t:t + 1], ALU.subtract, ALU.mult))
                chain.wait()
                dve.tensor_copy(XN[:, bass.ds(TB * b, TB), :], XN_s[s][:, :, :]).then_inc(s_["normed"], 1)
                dve.wait_ge(s_["logits"], b + 1 + HEAD)
                dve.tensor_copy(lg[:, bass.ds(TB * b, TB), :], p_c[:, 0:TB * E].rearrange("p (t e) -> p t e", t=TB)).then_inc(s_["lg_read"], 1)
                wait_alone(dve, s_["stood_v"], (s_["normed"], b + 1), (s_["lg_read"], b + 1))
                chain.close()

            def by_tile(ap):
                return ap.unsqueeze(2).broadcast_to([P, NT, E])

            def by_expert(ap):
                return ap.unsqueeze(1).broadcast_to([P, NT, E])

            for k, src in ((0, lg), (1, lg2)):
                step(dve.tensor_reduce(best[:, k, :], src[:, :, :], AX.X, ALU.max))
                step(dve.tensor_tensor(cand[:, :, :], src[:, :, :], by_tile(best[:, k, :]), ALU.is_equal))
                step(dve.tensor_tensor(cand[:, :, :], cand[:, :, :], by_expert(falling[:, :]), ALU.mult))
                step(dve.tensor_reduce(cmax[:, :], cand[:, :, :], AX.X, ALU.max))
                step(dve.tensor_tensor(pick[:, k, :, :], cand[:, :, :], by_tile(cmax[:, :]), ALU.is_equal))
                if k == 0:
                    step(dve.scalar_tensor_tensor(flat(lg2[:, :, :]), flat(pick[:, 0, :, :]), -OFF, flat(lg[:, :, :]), ALU.mult, ALU.add))
            dve.tensor_tensor(both[:, :, :], pick[:, 0, :, :], pick[:, 1, :, :], ALU.add).then_inc(s_["both_ready"], 1)
            chain.done(dve.tensor_tensor(probs[:, :, :], lg[:, :, :], by_tile(best[:, 0, :]), ALU.subtract))
            chain.done(dve.tensor_tensor(gap[:, :], best[:, 1, :], best[:, 0, :], ALU.subtract))
            chain.wait()
            dve.sem_inc(s_["gap_ready"], 1)
            dve.wait_ge(s_["exp_ready"], 1 + HEAD)
            step(dve.tensor_reduce(zsum[:, :], probs[:, :, :], AX.X, ALU.add))
            step(dve.reciprocal(wt[:, 0, :], zsum[:, :]))
            step(dve.tensor_tensor(wt[:, 1, :], gap[:, :], wt[:, 0, :], ALU.mult))
            step(dve.tensor_tensor(wsum[:, :], wt[:, 0, :], wt[:, 1, :], ALU.add))
            step(dve.tensor_scalar(wsum[:, :], wsum[:, :], 1e-9, None, ALU.add))
            step(dve.reciprocal(wsum[:, :], wsum[:, :]))
            for k in range(2):
                chain.done(dve.tensor_tensor(wt[:, k, :], wt[:, k, :], wsum[:, :], ALU.mult))
            dve.wait_ge(s_["counted"], 1 + HEAD)
            step(dve.tensor_copy(total[:, :, :].rearrange("p t e -> p (t e)"), p_t[:, 0:NT * E]))
            for e in range(E):
                chain.done(dve.tensor_tensor_scan(upto[:, :, e], ones[:, 0:NT], total[:, :, e], 0.0, ALU.mult, ALU.add))
            chain.wait()
            step(dve.tensor_tensor(over[:, :, :], upto[:, NT - 1, :].unsqueeze(2).broadcast_to([P, E, B]),
                                   steps[:, :].unsqueeze(1).broadcast_to([P, E, B]), ALU.is_gt))
            step(dve.tensor_reduce(ngroups[:, :], over[:, :, :], AX.X, ALU.add))
            step(dve.tensor_tensor_scan(gend[:, :], ones[:, 0:E], ngroups[:, :], 0.0, ALU.mult, ALU.add))
            step(dve.tensor_tensor(gstart[:, :], gend[:, :], ngroups[:, :], ALU.subtract))
            step(dve.tensor_scalar(gstart[:, :], gstart[:, :], float(G), None, ALU.mult))
            step(dve.tensor_tensor(upto[:, :, :], upto[:, :, :], total[:, :, :], ALU.subtract))
            step(dve.tensor_tensor(before[:, :, :], p_c[:, 0:NT * E].rearrange("p (t e) -> p t e", e=E), upto[:, :, :], ALU.add))
            step(dve.tensor_tensor(before[:, :, :], before[:, :, :], by_expert(gstart[:, :]), ALU.add))
            for k in range(2):
                step(dve.tensor_tensor(cand[:, :, :], pick[:, k, :, :], before[:, :, :], ALU.mult))
                step(dve.tensor_reduce(place[:, k, :], cand[:, :, :], AX.X, ALU.add))
            step(dve.tensor_copy(place_i[:, :, :], place[:, :, :]))
            step(dve.tensor_tensor(passed[:, :, :], ramp[:, :].unsqueeze(2).broadcast_to([P, NG, E - 1]),
                                   gend[:, 0:E - 1].unsqueeze(1).broadcast_to([P, NG, E - 1]), ALU.is_ge))
            step(dve.tensor_reduce(owner[:, :], passed[:, :, :], AX.X, ALU.add))
            step(dve.tensor_copy(owner_i[:, :], owner[:, :]))
            dve.sem_inc(s_["routed"], 1)
            chain.close()
            for i, j, r in groups(dve):
                e = expert_of(dve, j)
                dve.wait_ge(s_["gT_turned"], j + 1 + HEAD)
                dve.tensor_copy(flat(gT[:, :, :]), p_t[:, :]).then_inc(s_["gT_ready"], 1)
                dve.wait_ge(s_["y_ready"], j + 1 + HEAD)
                dve.wait_ge(kept[r], 16 * i + HEAD)
                for t in range(TG):
                    last = dve.tensor_tensor(gy[:, r, t, :], p_y[:, t * D:(t + 1) * D], b2[:, bass.ds(e, 1), :].rearrange("p a d -> p (a d)"), ALU.add)
                last.then_inc(s_["gy_ready"], 1)
            for n in range(2 * NT):
                t, k = divmod(n, 2)
                dve.wait_ge(gathered[n % GR], 16 * (n // GR + 1))
                if k:
                    dve.wait_ge(s_["combined"], n + HEAD)
                dve.scalar_tensor_tensor(X[:, t, :], got[:, n % GR, :], wt[:, k, t:t + 1], X[:, t, :], ALU.mult, ALU.add).then_inc(s_["combined"], 1)
            dve.wait_ge(s_["combined"], 2 * NT + HEAD)


R_CAP = 85.0


def time_channel_mix(nc, ins, X):
    L = "L1_attn_"
    with Phase(nc, "mix") as ph:
        ident = ph.sb("ident", [P, P])
        minus_half = ph.sb("minus_half", [P, TB])
        w_nat = ph.sb("w_nat", [P, 5, DC, D])
        fk_nat = ph.sb("fk_nat", [P, HC, D])
        fv_nat = ph.sb("fv_nat", [P, DC, HID])
        w = ph.sb("w", [P, 5, DC, D])
        fk = ph.sb("fk", [P, DC, HID])
        fv = ph.sb("fv", [P, HC, D])
        vec_names = ("ln1_g", "ln1_b", "ln2_g", "ln2_b", "time_mix_k", "time_mix_v", "time_mix_r",
                     "cm_k", "cm_r", "time_decay", "time_first")
        vec = ph.sb("vec", [P, len(vec_names), DC])
        at = {n: i for i, n in enumerate(vec_names)}

        def col(n, c):
            return vec[:, at[n], c:c + 1]

        decay = ph.sb("decay", [P, DC])
        stats = ph.sb("stats", [P, TB, 6])
        aggr = ph.sb("aggr", [P, TB, 2])
        rstd = ph.sb("rstd", [P, TB])
        y = ph.sb("y", [P, TB, D])
        yn = ph.sb("yn", [P, TB, D])
        xa = ph.sb("xa", [P, DC, S + 1])
        dif = ph.sb("dif", [P, DC, S])
        mixed = ph.sb("mixed", [P, 3, DC, S])
        run = ph.sb("run", [P, DC, S + 1])
        num = ph.sb("num", [P, DC, S + 1])
        den = ph.sb("den", [P, DC, S + 1])
        vals = ph.sb("vals", [P, DC, S])
        top = ph.sb("top", [P, DC, S])
        fall = ph.sb("fall", [P, DC, S])
        gain = ph.sb("gain", [P, DC, S])
        gain_v = ph.sb("gain_v", [P, DC, S])
        e_old = ph.sb("e_old", [P, DC, S])
        e_new = ph.sb("e_new", [P, DC, S])
        e_r = ph.sb("e_r", [P, DC, S])
        a = ph.sb("a", [P, DC, S])
        a2 = ph.sb("a2", [P, DC, S])
        a3 = ph.sb("a3", [P, DC, S])
        mixed_out = ph.sb("mixed_out", [P, DC, S])
        hid = ph.sb("hid", [P, HC, S])
        hid_sq = ph.sb("hid_sq", [P, HC, S])
        e_r2 = ph.sb("e_r2", [P, TB, D])
        g = ph.sb("g", [P, TB, D])
        p_t = ph.ps("p_t")
        p_k, p_v, p_r = ph.ps("p_k"), ph.ps("p_v"), ph.ps("p_r")
        p_h = [ph.ps(f"p_h{i}") for i in range(2)]
        p_kv, p_y = ph.ps("p_kv"), ph.ps("p_y")
        banks = [p_t, p_k, p_v, p_r, p_h[0], p_h[1], p_kv, p_y]

        names = ("r_capped r2_capped loaded ident_ready set_up turned freed consts measured var_eps rstd_ready normed turned_x xa_ready "
                 "mixed_ready projected vals_ready run_ready d_fall d_gain top_ready d_old d_new fall_ready gain_ready old_ready new_ready "
                 "er_ready scans_ready part_a part_b part_c part_d out_ready att_ready mid_ready turned_m xc_ready mixed2_ready hidden relu_ready "
                 "squared r2_ready kv_ready er2_ready added chain_v chain_p stood_v stood_p stood_a").split()
        sems = {n: ph.own(n) if n.startswith(OWN) else ph.sem(n) for n in names}
        block = ph.block()
        s_ = sems
        n_blocks = (5 * 4 + 16 + 16) // 4

        @block.sync
        def _(sp):
            for n, m in enumerate(("att_Wk", "att_Wv", "att_Wr", "att_Wo", "ffn_Wr")):
                sp.dma_start(w_nat[:, n, :, :], ins[L + m].rearrange("(c p) d -> p c d", p=P)).then_inc(s_["loaded"], 16)
            sp.dma_start(fk_nat[:, :, :], ins[L + "ffn_Wk"].rearrange("(c p) d -> p c d", p=P)).then_inc(s_["loaded"], 16)
            sp.dma_start(fv_nat[:, :, :], ins[L + "ffn_Wv"].rearrange("(c p) d -> p c d", p=P)).then_inc(s_["loaded"], 16)
            with nc.allow_non_contiguous_dma(reason="vectors of 256 numbers"):
                for n, m in enumerate(vec_names):
                    sp.dma_start(vec[:, n, :], columns(ins[L + m])).then_inc(s_["loaded"], 16)

        n_loads = 7 + len(vec_names)

        @block.gpsimd
        def _(pool):
            make_identity(pool, ident[:, :], s_["ident_ready"])
            chain = Chain(pool, s_["chain_p"])
            chain.done(pool.memset(minus_half[:, :], -0.5))
            chain.done(pool.memset(xa[:, :, 0:1], 0.0))
            chain.done(pool.memset(run[:, :, 0:1], -1e38))
            chain.done(pool.memset(num[:, :, 0:1], 0.0))
            chain.done(pool.memset(den[:, :, 0:1], 0.0))
            chain.wait()
            pool.sem_inc(s_["set_up"], 1)
            chain.close()
            for b, s in sequences(pool):
                def root(k):
                    wait_alone(pool, s_["stood_p"], (s_["measured"], 3 * b + k + 1))
                    inverse_root(pool, rstd[:, :], aggr[:, :, 1], 1.0, LN_EPS, minus_half[:, :], s_["var_eps"], s_["rstd_ready"], 3 * b + k, s_["stood_p"])
                root(0)
                root(1)
                pool.wait_ge(s_["run_ready"], b + 1 + HEAD)
                pool.tensor_tensor(fall[:, :, :], run[:, :, 0:S], run[:, :, 1:S + 1], ALU.subtract).then_inc(s_["d_fall"], 1)
                pool.wait_ge(s_["top_ready"], b + 1 + HEAD)
                pool.tensor_tensor(e_old[:, :, :], run[:, :, 0:S], top[:, :, :], ALU.subtract).then_inc(s_["d_old"], 1)
                pool.wait_ge(s_["new_ready"], b + 1 + HEAD)
                pool.wait_ge(s_["vals_ready"], b + 1 + HEAD)
                pool.tensor_tensor(a[:, :, :], e_new[:, :, :], vals[:, :, :], ALU.mult).then_inc(s_["part_a"], 1)
                pool.wait_ge(s_["scans_ready"], b + 1 + HEAD)
                pool.wait_ge(s_["old_ready"], b + 1 + HEAD)
                pool.tensor_tensor(a2[:, :, :], e_old[:, :, :], num[:, :, 0:S], ALU.mult).then_inc(s_["part_b"], 1)
                pool.wait_ge(s_["part_b"], b + 1 + HEAD)
                pool.tensor_tensor(a[:, :, :], a[:, :, :], a2[:, :, :], ALU.add).then_inc(s_["part_c"], 1)
                root(2)
                for n in range(HC // 2):
                    pool.wait_ge(s_["relu_ready"], HC // 2 * b + n + 1 + HEAD)
                    pool.tensor_tensor(hid_sq[:, 2 * n:2 * n + 2, :], hid[:, 2 * n:2 * n + 2, :], hid[:, 2 * n:2 * n + 2, :], ALU.mult).then_inc(s_["squared"], 1)

        @block.tensor
        def _(pe):
            pe.wait_ge(s_["loaded"], 16 * n_loads)
            pe.wait_ge(s_["ident_ready"], 2 + HEAD)
            blocks = [w_nat[:, n, ot, ct * P:(ct + 1) * P] for n in range(5) for ct in range(DC) for ot in range(DC)]
            blocks += [fk_nat[:, ot, ct * P:(ct + 1) * P] for ct in range(DC) for ot in range(HC)]
            blocks += [fv_nat[:, ot, ct * P:(ct + 1) * P] for ct in range(HC) for ot in range(DC)]
            transpose_blocks(pe, blocks, banks, ident[:, :], s_["turned"], s_["freed"])
            pe.wait_ge(s_["freed"], n_blocks + HEAD)
            pe.wait_ge(s_["consts"], 1 + HEAD)

            def turn(src, done):
                for c in range(DC):
                    for t in range(TB):
                        last = pe.transpose(p_t[:, c * S + t * P:c * S + (t + 1) * P], src[:, t, c * P:(c + 1) * P], ident[:, :])
                last.then_inc(done, 1)

            for b, s in sequences(pe):
                pe.wait_ge(s_["normed"], 3 * b + 2 + HEAD)
                pe.wait_ge(s_["added"], b + HEAD)
                turn(yn, s_["turned_x"])
                for n, bank in enumerate((p_k, p_v, p_r)):
                    pe.wait_ge(s_["mixed_ready"], 3 * b + n + 1 + HEAD)
                    for oc in range(DC):
                        for ic in range(DC):
                            last = pe.matmul(bank[:, oc * S:(oc + 1) * S], w[:, n, ic, oc * P:(oc + 1) * P], mixed[:, n, ic, :],
                                             start=(ic == 0), stop=(ic == DC - 1))
                    last.then_inc(s_["projected"], 1)
                pe.wait_ge(s_["out_ready"], b + 1 + HEAD)
                for t in range(TB):
                    for ic in range(DC):
                        last = pe.matmul(p_y[:, t * D:(t + 1) * D], mixed_out[:, ic, t * P:(t + 1) * P], w[:, 3, ic, :],
                                         start=(ic == 0), stop=(ic == DC - 1))
                last.then_inc(s_["att_ready"], 1)
                pe.wait_ge(s_["normed"], 3 * b + 3 + HEAD)
                turn(yn, s_["turned_m"])
                pe.wait_ge(s_["mixed2_ready"], 2 * b + 1 + HEAD)
                for n in range(HC // 2):
                    pe.wait_ge(s_["relu_ready"], HC // 2 * b + max(n - 1, 0) + HEAD)
                    for k in range(2):
                        for ic in range(DC):
                            last = pe.matmul(p_h[n % 2][:, k * S:(k + 1) * S], fk[:, ic, (2 * n + k) * P:(2 * n + k + 1) * P], mixed[:, 0, ic, :],
                                             start=(ic == 0), stop=(ic == DC - 1))
                    last.then_inc(s_["hidden"], 1)
                pe.wait_ge(s_["mixed2_ready"], 2 * b + 2 + HEAD)
                for t in range(TB):
                    for ic in range(DC):
                        last = pe.matmul(p_y[:, t * D:(t + 1) * D], mixed[:, 1, ic, t * P:(t + 1) * P], w[:, 4, ic, :],
                                         start=(ic == 0), stop=(ic == DC - 1))
                last.then_inc(s_["r2_ready"], 1)
                pe.wait_ge(s_["squared"], HC // 2 * (b + 1) + HEAD)
                for t in range(TB):
                    for hc in range(HC):
                        last = pe.matmul(p_kv[:, t * D:(t + 1) * D], hid_sq[:, hc, t * P:(t + 1) * P], fv[:, hc, :],
                                         start=(hc == 0), stop=(hc == HC - 1))
                last.then_inc(s_["kv_ready"], 1)

        @block.scalar
        def _(act):
            act.wait_ge(s_["loaded"], 16 * n_loads)
            act.wait_ge(s_["set_up"], 1 + HEAD)
            dests = [flat(w[:, n, :, :]) for n in range(5)]
            dests += [fk[:, ct, g4 * 512:(g4 + 1) * 512] for ct in range(DC) for g4 in range(2)]
            dests += [flat(fv[:, 2 * g2:2 * g2 + 2, :]) for g2 in range(HC // 2)]
            evacuate_blocks(act, dests, banks, s_["turned"], s_["freed"])
            act.activation(decay[:, :], vec[:, at["time_decay"], :], ACT.Exp).then_inc(s_["freed"], 1)
            act.wait_ge(s_["consts"], 1 + HEAD)
            for b, s in sequences(act):
                act.wait_ge(s_["turned_x"], b + 1 + HEAD)
                for c in range(DC):
                    last = act.activation(xa[:, c, 1:S + 1], p_t[:, c * S:(c + 1) * S], ACT.Identity, scale=col("ln1_g", c), bias=col("ln1_b", c))
                last.then_inc(s_["xa_ready"], 1)
                act.wait_ge(s_["projected"], 3 * b + 2 + HEAD)
                act.activation(flat(vals[:, :, :]), p_v[:, :], ACT.Copy).then_inc(s_["vals_ready"], 1)
                act.wait_ge(s_["r_capped"], b + 1 + HEAD)
                act.activation(e_r[:, :, :], e_r[:, :, :], ACT.Exp, scale=-1.0).then_inc(s_["er_ready"], 1)
                act.wait_ge(s_["d_gain"], b + 1 + HEAD)
                act.activation(gain[:, :, :], gain[:, :, :], ACT.Exp).then_inc(s_["gain_ready"], 1)
                act.wait_ge(s_["d_fall"], b + 1 + HEAD)
                for c in range(DC):
                    last = act.activation(fall[:, c, :], fall[:, c, :], ACT.Exp, bias=decay[:, c:c + 1])
                last.then_inc(s_["fall_ready"], 1)
                act.wait_ge(s_["d_new"], b + 1 + HEAD)
                for c in range(DC):
                    last = act.activation(e_new[:, c, :], e_new[:, c, :], ACT.Exp, bias=col("time_first", c))
                last.then_inc(s_["new_ready"], 1)
                act.wait_ge(s_["d_old"], b + 1 + HEAD)
                act.activation(e_old[:, :, :], e_old[:, :, :], ACT.Exp).then_inc(s_["old_ready"], 1)
                act.wait_ge(s_["turned_m"], b + 1 + HEAD)
                for c in range(DC):
                    last = act.activation(xa[:, c, 1:S + 1], p_t[:, c * S:(c + 1) * S], ACT.Identity, scale=col("ln2_g", c), bias=col("ln2_b", c))
                last.then_inc(s_["xc_ready"], 1)
                for n in range(HC // 2):
                    act.wait_ge(s_["hidden"], HC // 2 * b + n + 1 + HEAD)
                    act.activation(flat(hid[:, 2 * n:2 * n + 2, :]), p_h[n % 2][:, :], ACT.Relu).then_inc(s_["relu_ready"], 1)
                act.wait_ge(s_["r2_capped"], b + 1 + HEAD)
                act.activation(e_r2[:, :, :], e_r2[:, :, :], ACT.Exp, scale=-1.0).then_inc(s_["er2_ready"], 1)

        @block.vector
        def _(dve):
            chain = Chain(dve, s_["chain_v"])
            dve.wait_ge(s_["freed"], n_blocks + 1 + HEAD)
            chain.done(dve.tensor_scalar(decay[:, :], decay[:, :], -1.0, None, ALU.mult))
            chain.wait()
            dve.sem_inc(s_["consts"], 1)
            chain.close()

            def norm(b, k, src, dst):
                layer_norm_stats(dve, chain, src, stats, aggr, s_["measured"])
                dve.wait_ge(s_["rstd_ready"], 3 * b + k + 1 + HEAD)
                layer_norm_apply(dve, src, lambda t: dst[:, t, :], aggr, rstd, s_["normed"])

            def mix(n, name, done):
                for c in range(DC):
                    last = dve.scalar_tensor_tensor(mixed[:, n, c, :], dif[:, c, :], col(name, c), xa[:, c, 0:S], ALU.mult, ALU.add)
                last.then_inc(done, 1)

            for b, s in sequences(dve):
                norm(b, 0, lambda t: tile_of(X, b, t), y)
                wait_alone(dve, s_["stood_v"], (s_["normed"], 3 * b + 1))
                norm(b, 1, lambda t: y[:, t, :], yn)
                dve.wait_ge(s_["xa_ready"], b + 1 + HEAD)
                chain.done(dve.tensor_tensor(dif[:, :, :], xa[:, :, 1:S + 1], xa[:, :, 0:S], ALU.subtract))
                chain.wait()
                for n, m in enumerate(("time_mix_k", "time_mix_v", "time_mix_r")):
                    mix(n, m, s_["mixed_ready"])
                dve.wait_ge(s_["projected"], 3 * b + 1 + HEAD)
                kk = p_k[:, :].rearrange("p (c n) -> p c n", c=DC)
                for c in range(DC):
                    last = dve.tensor_tensor_scan(run[:, c, 1:S + 1], decay[:, c:c + 1].broadcast_to([P, S]), kk[:, c, :], -1e38, ALU.add, ALU.max)
                last.then_inc(s_["run_ready"], 1)
                dve.wait_ge(s_["run_ready"], b + 1 + HEAD)
                dve.tensor_tensor(gain[:, :, :], kk, run[:, :, 1:S + 1], ALU.subtract).then_inc(s_["d_gain"], 1)
                for c in range(DC):
                    last = dve.scalar_tensor_tensor(top[:, c, :], kk[:, c, :], col("time_first", c), run[:, c, 0:S], ALU.add, ALU.max)
                last.then_inc(s_["top_ready"], 1)
                dve.wait_ge(s_["top_ready"], b + 1 + HEAD)
                dve.tensor_tensor(e_new[:, :, :], kk, top[:, :, :], ALU.subtract).then_inc(s_["d_new"], 1)
                dve.wait_ge(s_["projected"], 3 * b + 3 + HEAD)
                dve.tensor_scalar(flat(e_r[:, :, :]), p_r[:, :], -R_CAP, None, ALU.max).then_inc(s_["r_capped"], 1)
                dve.wait_ge(s_["gain_ready"], b + 1 + HEAD)
                dve.wait_ge(s_["vals_ready"], b + 1 + HEAD)
                chain.done(dve.tensor_tensor(gain_v[:, :, :], gain[:, :, :], vals[:, :, :], ALU.mult))
                dve.wait_ge(s_["fall_ready"], b + 1 + HEAD)
                for c in range(DC):
                    chain.done(dve.tensor_tensor_scan(den[:, c, 1:S + 1], fall[:, c, :], gain[:, c, :], 0.0, ALU.mult, ALU.add))
                chain.wait()
                for c in range(DC):
                    last = dve.tensor_tensor_scan(num[:, c, 1:S + 1], fall[:, c, :], gain_v[:, c, :], 0.0, ALU.mult, ALU.add)
                last.then_inc(s_["scans_ready"], 1)
                dve.wait_ge(s_["old_ready"], b + 1 + HEAD)
                dve.wait_ge(s_["new_ready"], b + 1 + HEAD)
                chain.done(dve.tensor_tensor(a3[:, :, :], e_old[:, :, :], den[:, :, 0:S], ALU.mult))
                chain.wait()
                chain.done(dve.tensor_tensor(a3[:, :, :], a3[:, :, :], e_new[:, :, :], ALU.add))
                dve.wait_ge(s_["er_ready"], b + 1 + HEAD)
                chain.wait()
                chain.done(dve.scalar_tensor_tensor(flat(a3[:, :, :]), flat(e_r[:, :, :]), 1.0, flat(a3[:, :, :]), ALU.add, ALU.mult))
                chain.wait()
                chain.done(dve.reciprocal(a3[:, :, :], a3[:, :, :]))
                chain.wait()
                dve.wait_ge(s_["part_c"], b + 1 + HEAD)
                dve.tensor_tensor(mixed_out[:, :, :], a[:, :, :], a3[:, :, :], ALU.mult).then_inc(s_["out_ready"], 1)
                dve.wait_ge(s_["att_ready"], b + 1 + HEAD)
                chain.done(dve.tensor_tensor(flat(y[:, :, :]), p_y[:, :], flat(y[:, :, :]), ALU.add))
                chain.wait()
                norm(b, 2, lambda t: y[:, t, :], yn)
                dve.wait_ge(s_["xc_ready"], b + 1 + HEAD)
                chain.done(dve.tensor_tensor(dif[:, :, :], xa[:, :, 1:S + 1], xa[:, :, 0:S], ALU.subtract))
                chain.wait()
                for n, m in enumerate(("cm_k", "cm_r")):
                    mix(n, m, s_["mixed2_ready"])
                dve.wait_ge(s_["r2_ready"], b + 1 + HEAD)
                dve.tensor_scalar(flat(e_r2[:, :, :]), p_y[:, :], -R_CAP, None, ALU.max).then_inc(s_["r2_capped"], 1)
                dve.wait_ge(s_["er2_ready"], b + 1 + HEAD)
                chain.done(dve.tensor_scalar(flat(g[:, :, :]), flat(e_r2[:, :, :]), 1.0, None, ALU.add))
                chain.wait()
                chain.done(dve.reciprocal(g[:, :, :], g[:, :, :]))
                chain.wait()
                dve.wait_ge(s_["kv_ready"], b + 1 + HEAD)
                chain.done(dve.tensor_tensor(flat(g[:, :, :]), p_kv[:, :], flat(g[:, :, :]), ALU.mult))
                chain.wait()
                chain.done(dve.tensor_tensor(g[:, :, :], g[:, :, :], y[:, :, :], ALU.add))
                chain.wait()
                for t in range(TB):
                    last = dve.tensor_tensor(tile_of(X, b, t), g[:, t, :], tile_of(X, b, t), ALU.add)
                last.then_inc(s_["added"], 1)
                wait_alone(dve, s_["stood_v"], (s_["added"], b + 1))
                chain.close()


def float8_ffn(nc, ins, X):
    FAR = 128.0
    with Phase(nc, "ffn") as ph:
        ident = ph.sb("ident", [P, P])
        ident_b = ph.sb("ident_b", [P, P], BF16)
        minus_half = ph.sb("minus_half", [P, TB])
        w_nat = ph.sb("w_nat", [P, DC, D])
        near8 = ph.sb("near8", [P, DC, D], FP8)
        far8 = ph.sb("far8", [P, DC, D], FP8)
        near = ph.sb("near", [P, DC, D])
        far = ph.sb("far", [P, DC, D])
        is_far = ph.sb("is_far", [P, DC, D])
        w_q = ph.sb("w_q", [P, DC, D], BF16)
        wt = ph.sb("wt", [P, DC, D], BF16)
        bias = ph.sb("bias", [P, D])
        stats = ph.sb("stats", [P, TB, 6])
        aggr = ph.sb("aggr", [P, TB, 2])
        rstd = ph.sb("rstd", [P, TB])
        xn = ph.sb("xn", [P, TB, D])
        x8 = ph.sb("x8", [P, TB, D], FP8)
        xq = ph.sb("xq", [P, 2, TB, D], BF16)
        xT = ph.sb("xT", [P, 2, DC, S], BF16)
        y16 = ph.sb("y16", [P, 2, TB, D], F16)
        y = ph.sb("y", [P, TB, D])
        p_t = [ph.ps(f"p_t{i}", (P, 1024), BF16) for i in range(2)]
        p_y = [ph.ps(f"p_y{i}") for i in range(2)]
        names = ("loaded ident_ready ident_b_ready w_ready w_turned wt_ready measured var_eps rstd_ready normed quantised turned_x xT_ready "
                 "y_ready y_read added chain_v stood_v stood_p").split()
        s_ = {n: ph.own(n) if n.startswith(OWN) else ph.sem(n) for n in names}
        block = ph.block()

        @block.sync
        def _(sp):
            sp.dma_start(w_nat[:, :, :], ins["L1_ffn_weight"].rearrange("(c p) d -> p c d", p=P)).then_inc(s_["loaded"], 16)
            sp.dma_start(bias[:, :], ins["L1_ffn_bias"].partition_broadcast(P)).then_inc(s_["loaded"], 16)

        @block.gpsimd
        def _(pool):
            make_identity(pool, ident[:, :], s_["ident_ready"])
            pool.memset(minus_half[:, :], -0.5).then_inc(s_["ident_b_ready"], 1)
            pool.wait_ge(s_["ident_ready"], 2 + HEAD)
            pool.tensor_copy(ident_b[:, :], ident[:, :]).then_inc(s_["ident_b_ready"], 1)
            pool.wait_ge(s_["ident_b_ready"], 2 + HEAD)
            for b, s in sequences(pool):
                wait_alone(pool, s_["stood_p"], (s_["measured"], b + 1))
                inverse_root(pool, rstd[:, :], aggr[:, :, 1], 1.0, LN_EPS, minus_half[:, :], s_["var_eps"], s_["rstd_ready"], b, s_["stood_p"])

        @block.tensor
        def _(pe):
            pe.wait_ge(s_["ident_b_ready"], 2 + HEAD)
            pe.wait_ge(s_["w_ready"], 1 + HEAD)
            for ct in range(DC):
                for ot in range(DC):
                    last = pe.transpose(p_t[0][:, (ct * DC + ot) * P:(ct * DC + ot + 1) * P], w_q[:, ot, ct * P:(ct + 1) * P], ident_b[:, :])
            last.then_inc(s_["w_turned"], 1)
            pe.wait_ge(s_["wt_ready"], 1 + HEAD)
            for b, s in sequences(pe):
                pe.wait_ge(s_["quantised"], b + 1 + HEAD)
                pe.wait_ge(s_["xT_ready"], b + HEAD)
                for c in range(DC):
                    for t in range(TB):
                        last = pe.transpose(p_t[s][:, c * S + t * P:c * S + (t + 1) * P], xq[:, s, t, c * P:(c + 1) * P], ident_b[:, :])
                last.then_inc(s_["turned_x"], 1)
                pe.wait_ge(s_["xT_ready"], b + 1 + HEAD)
                pe.wait_ge(s_["y_read"], b + HEAD)
                for t in range(TB):
                    for ic in range(DC):
                        last = pe.matmul(p_y[s][:, t * D:(t + 1) * D], xT[:, s, ic, t * P:(t + 1) * P], wt[:, ic, :],
                                         start=(ic == 0), stop=(ic == DC - 1))
                last.then_inc(s_["y_ready"], 1)

        @block.scalar
        def _(act):
            act.wait_ge(s_["w_turned"], 1 + HEAD)
            act.activation(flat(wt[:, :, :]), p_t[0][:, 0:512], ACT.Copy).then_inc(s_["wt_ready"], 1)
            for b, s in sequences(act):
                act.wait_ge(s_["turned_x"], b + 1 + HEAD)
                act.wait_ge(s_["y_ready"], b + HEAD)
                act.activation(flat(xT[:, s, :, :]), p_t[s][:, 0:512], ACT.Copy).then_inc(s_["xT_ready"], 1)
                act.wait_ge(s_["y_ready"], b + 1 + HEAD)
                act.wait_ge(s_["added"], b + HEAD)
                act.activation(flat(y16[:, s, :, :]), p_y[s][:, :], ACT.Copy).then_inc(s_["y_read"], 1)

        @block.vector
        def _(dve):
            chain = Chain(dve, s_["chain_v"])

            def step(ins_):
                chain.done(ins_)
                chain.wait()

            dve.wait_ge(s_["loaded"], 32)
            step(dve.tensor_scalar(w_nat[:, :, :], w_nat[:, :, :], 448.0, -448.0, ALU.min, ALU.max))
            step(dve.tensor_scalar(near[:, :, :], w_nat[:, :, :], FAR, -FAR, ALU.min, ALU.max))
            step(dve.tensor_copy(near8[:, :, :], near[:, :, :], saturate=False))
            step(dve.tensor_copy(near[:, :, :], near8[:, :, :]))
            step(dve.tensor_scalar(far[:, :, :], w_nat[:, :, :], 0.25, None, ALU.mult))
            step(dve.tensor_copy(far8[:, :, :], far[:, :, :], saturate=False))
            step(dve.tensor_copy(far[:, :, :], far8[:, :, :]))
            step(dve.tensor_tensor(is_far[:, :, :], w_nat[:, :, :], w_nat[:, :, :], ALU.mult))
            step(dve.tensor_scalar(is_far[:, :, :], is_far[:, :, :], FAR * FAR, None, ALU.is_gt))
            step(dve.scalar_tensor_tensor(flat(far[:, :, :]), flat(far[:, :, :]), 4.0, flat(near[:, :, :]), ALU.mult, ALU.subtract))
            step(dve.tensor_tensor(far[:, :, :], far[:, :, :], is_far[:, :, :], ALU.mult))
            step(dve.tensor_tensor(w_q[:, :, :], near[:, :, :], far[:, :, :], ALU.add))
            dve.sem_inc(s_["w_ready"], 1)
            chain.close()
            for b, s in sequences(dve):
                layer_norm_stats(dve, chain, lambda t: tile_of(X, b, t), stats, aggr, s_["measured"])
                dve.wait_ge(s_["rstd_ready"], b + 1 + HEAD)
                for t in range(TB):
                    chain.done(dve.tensor_scalar(xn[:, t, :], tile_of(X, b, t), aggr[:, t, 0:1], rstd[:, t:t + 1], ALU.subtract, ALU.mult))
                chain.wait()
                step(dve.tensor_copy(x8[:, :, :], xn[:, :, :], saturate=False))
                dve.tensor_copy(xq[:, s, :, :], x8[:, :, :]).then_inc(s_["quantised"], 1)
                dve.wait_ge(s_["y_read"], b + 1 + HEAD)
                for t in range(TB):
                    chain.done(dve.tensor_tensor(y[:, t, :], y16[:, s, t, :], bias[:, :], ALU.add))
                chain.wait()
                for t in range(TB):
                    last = dve.tensor_tensor(tile_of(X, b, t), y[:, t, :], tile_of(X, b, t), ALU.add)
                last.then_inc(s_["added"], 1)
                wait_alone(dve, s_["stood_v"], (s_["added"], b + 1))
                chain.close()


PHASES = [decay_attention, lambda nc, ins, X: cross_attention(nc, ins, X, 0, True), experts_ffn, time_channel_mix, lambda nc, ins, X: cross_attention(nc, ins, X, 1, False), float8_ffn]


def build(nc, ins, out, phases):
    with ExitStack() as ctx:
        X = ctx.enter_context(nc.sbuf_tensor("X", [P, NT, D], F32))
        load_x(nc, ins["x"], X)
        for n in phases:
            PHASES[n](nc, ins, X)
        store_x(nc, X, out)


_INS = [
    "x", "ctx_1024", "fside_BxSxS2_0", "mask_BxS2_if1",
    "L0_attn_q", "L0_attn_k", "L0_attn_log_decay", "L0_attn_norm_weight", "L0_attn_o_w",
    "L0_xattn_Wq", "L0_xattn_bq", "L0_xattn_Wk", "L0_xattn_bk", "L0_xattn_Wv", "L0_xattn_bv", "L0_xattn_Wo", "L0_xattn_bo",
    "L0_ffn_gate_w", "L0_ffn_w1", "L0_ffn_b1", "L0_ffn_w2", "L0_ffn_b2",
    "L1_attn_ln1_g", "L1_attn_ln1_b", "L1_attn_ln2_g", "L1_attn_ln2_b", "L1_attn_time_decay", "L1_attn_time_first",
    "L1_attn_time_mix_k", "L1_attn_time_mix_v", "L1_attn_time_mix_r",
    "L1_attn_att_Wk", "L1_attn_att_Wv", "L1_attn_att_Wr", "L1_attn_att_Wo", "L1_attn_cm_k", "L1_attn_cm_r",
    "L1_attn_ffn_Wk", "L1_attn_ffn_Wr", "L1_attn_ffn_Wv",
    "L1_xattn_Wq", "L1_xattn_bq", "L1_xattn_Wk", "L1_xattn_bk", "L1_xattn_Wv", "L1_xattn_bv", "L1_xattn_Wo", "L1_xattn_bo",
    "L1_xattn_lambda_bias", "L1_ffn_weight", "L1_ffn_bias",
]


def kernel(**inputs):
    import numpy as np
    import concourse.bacc as bacc
    from concourse.bass_utils import run_bass_kernel_spmd

    nc = bacc.Bacc("TRN2", target_bir_lowering=False, num_devices=1)
    arrays, ins = {}, {}
    for name in _INS:
        a = np.ascontiguousarray(inputs[name])
        a = a.reshape(a.shape or (1,))
        arrays[f"in_{name}_dram"] = a
        ins[name] = nc.dram_tensor(f"in_{name}_dram", a.shape, mybir.dt.from_np(a.dtype), kind="ExternalInput").ap()
    out = nc.dram_tensor("out_0_dram", (B, S, D), F32, kind="ExternalOutput").ap()
    build(nc, ins, out, range(len(PHASES)))
    r = run_bass_kernel_spmd(nc, [arrays], core_ids=[0])
    return r.results[0]["out_0_dram"]
```

```python
from contextlib import ExitStack

import concourse.bass as bass
from concourse import mybir

F32 = mybir.dt.float32
BF16 = mybir.dt.bfloat16
F16 = mybir.dt.float16
FP8 = mybir.dt.float8e4
I32 = mybir.dt.int32
U32 = mybir.dt.uint32
ALU = mybir.AluOpType
ACT = mybir.ActivationFunctionType
AX = mybir.AxisListType

P = 128
B = 16
S = 256
D = 256
H = 16
DH = D // H
NT = B * S // P
TB = S // P
DC = D // P
E = 8
HID = 1024
HC = HID // P
LN_EPS = 1e-5
HEAD = 1


class Chain:

    def __init__(self, eng, sem):
        self.eng, self.sem, self.n = eng, sem, 0

    def done(self, ins):
        self.n += 1
        return ins.then_inc(self.sem, 1)

    def wait(self):
        self.eng.wait_ge(self.sem, self.n)

    def close(self):
        self.wait()
        self.eng.sem_clear(self.sem)
        self.n = 0


def wait_alone(eng, stood, *waits):
    for sem, n in waits:
        eng.wait_ge(sem, n + HEAD)
    eng.sem_inc(stood, 1)


def make_identity(pool, ident, sem, dtype_one=1.0):
    pool.memset(ident, 0.0).then_inc(sem, 1)
    pool.wait_ge(sem, 1 + HEAD)
    pool.affine_select(out=ident, in_=ident, compare_op=ALU.not_equal, fill=1.0, base=0,
                       pattern=[[-1, P]], channel_multiplier=1).then_inc(sem, 1)


def transpose_blocks(pe, blocks, banks, ident, turned, freed):
    for g in range(0, len(blocks), 4):
        n = g // 4
        if n >= len(banks):
            pe.wait_ge(freed, n - len(banks) + 1 + HEAD)
        for j, block in enumerate(blocks[g:g + 4]):
            last = pe.transpose(banks[n % len(banks)][:, j * P:(j + 1) * P], block, ident)
        last.then_inc(turned, 1)


def evacuate_blocks(act, dests, banks, turned, freed):
    for n, dest in enumerate(dests):
        act.wait_ge(turned, n + 1 + HEAD)
        act.activation(dest, banks[n % len(banks)][:, 0:dest.shape[-1]], ACT.Copy).then_inc(freed, 1)


def layer_norm_stats(dve, chain, src, stats, aggr, measured):
    for t in range(TB):
        chain.done(dve.bn_stats(stats[:, t, :], src(t)))
    chain.wait()
    for t in range(TB):
        last = dve.bn_aggr(aggr[:, t, :], stats[:, t, :])
    last.then_inc(measured, 1)


def inverse_root(pool, out, in_, scale, add, minus_half, summed, ready, turn, stood):
    pool.tensor_scalar(out, in_, scale, add, ALU.mult, ALU.add).then_inc(summed, 1)
    wait_alone(pool, stood, (summed, turn + 1))
    pool.tensor_tensor(out, out, minus_half, ALU.pow).then_inc(ready, 1)


def layer_norm_apply(dve, src, out, aggr, rstd, normed):
    for t in range(TB):
        last = dve.tensor_scalar(out(t), src(t), aggr[:, t, 0:1], rstd[:, t:t + 1], ALU.subtract, ALU.mult)
    last.then_inc(normed, 1)


def sequences(eng):
    with eng.Fori(0, B // 2) as i:
        for s in range(2):
            yield 2 * i + s, s


def turns(eng, drain=False, ahead=1):
    after = 1 if ahead == 1 else 3
    yield 0, 0, 0
    with eng.Fori(0, (B - 1 - after) // 2) as i:
        yield 2 * i + 1, i, 1
        yield 2 * i + 2, i + 1, 0
    for b in range(B - after, B + drain):
        yield b, b // 2, b % 2


def first(b):
    return isinstance(b, int) and b == 0


def has_next(b, ahead=1):
    return not isinstance(b, int) or b + ahead < B


def tile_of(X, b, t):
    return X[:, bass.ds(b * TB + t, 1), :].rearrange("p a d -> p (a d)")


OWN = ("chain_", "stood_", "loaded", "ctx_in", "raw_in", "zeroed", "scattered", "stored")


class Phase:

    def __init__(self, nc, name):
        self.nc, self.name, self.ctx, self.sems = nc, name, ExitStack(), []
        self.no_head = []

    def __enter__(self):
        self.ctx.__enter__()
        return self

    def __exit__(self, *e):
        self.ctx.__exit__(*e)
        self.nc.clear_and_free_semaphores(self.sems)

    def sb(self, name, shape, dt=F32):
        return self.ctx.enter_context(self.nc.sbuf_tensor(f"{self.name}_{name}", shape, dt))

    def ps(self, name, shape=(P, 512), dt=F32):
        return self.ctx.enter_context(self.nc.psum_tensor(f"{self.name}_{name}", list(shape), dt))

    def sem(self, name):
        self.sems.append(self.nc.alloc_semaphore(f"{self.name}_{name}"))
        return self.sems[-1]

    def own(self, name):
        sem = self.sem(name)
        self.no_head.append(sem)
        return sem

    def block(self):
        self.nc.all_engine_barrier()
        for sem in self.sems:
            if sem not in self.no_head:
                self.nc.sync.sem_inc(sem, HEAD)
        self.nc.all_engine_barrier()
        return self.ctx.enter_context(self.nc.Block())


def flat(ap):
    return ap.rearrange("p a b -> p (a b)")


def columns(vec):
    return vec.rearrange("(c p) -> p c", p=P)


def decay_attention(nc, ins, X, x):
    with Phase(nc, "dec") as ph:
        ident = ph.sb("ident", [P, P])
        groups = ph.sb("groups", [P, P])
        ones = ph.sb("ones", [P, 1])
        w_nat = ph.sb("w_nat", [P, DC, D])
        wt = ph.sb("wt", [P, DC, D])
        q_col = ph.sb("q_col", [P, DC])
        k_col = ph.sb("k_col", [P, DC])
        qk = ph.sb("qk", [P, DC])
        nw = ph.sb("nw", [P, DC])
        ld = ph.sb("ld", [P, DC])
        lam = ph.sb("lam", [P, DC])
        coef = ph.sb("coef", [P, DC])
        xn = ph.sb("xn", [P, 2, TB, D])
        stats = ph.sb("stats", [P, TB, 6])
        aggr = ph.sb("aggr", [P, TB, 2])
        rstd = ph.sb("rstd", [P, TB])
        v = ph.sb("v", [P, 2, DC, S])
        o = ph.sb("o", [P, 2, DC, S])
        osq = ph.sb("osq", [P, 2, DC, S])
        sum_sq = ph.sb("sum_sq", [P, TB])
        rms = ph.sb("rms", [P, TB])
        minus_half = ph.sb("minus_half", [P, TB])
        p_t = [ph.ps(f"p_t{i}") for i in range(2)]
        p_y = [ph.ps(f"p_y{i}") for i in range(2)]
        p_m = [ph.ps(f"p_m{i}") for i in range(2)]

        loaded = ph.own("loaded")
        x_in = [ph.own(f"loaded_x{q}") for q in range(4)]
        ident_ready, groups_ready = ph.sem("ident_ready"), ph.sem("groups_ready")
        turned, freed = ph.sem("turned"), ph.sem("freed")
        qk_ready, coef_sum, consts = ph.sem("qk_ready"), ph.sem("coef_sum"), ph.sem("consts")
        wt_ready = ph.sem("wt_ready")
        normed, turned_x, v_ready = ph.sem("normed"), ph.sem("turned_x"), ph.sem("v_ready")
        scanned, squared, y_ready, added = ph.sem("scanned"), ph.sem("squared"), ph.sem("y_ready"), ph.sem("added")
        measured, rstd_ready = ph.sem("measured"), ph.sem("rstd_ready")
        var_eps, mean_eps = ph.sem("var_eps"), ph.sem("mean_eps")
        sum_sq_ready, rms_ready = ph.sem("sum_sq_ready"), ph.sem("rms_ready")
        stood_p = ph.own("stood_p")
        chain_v, chain_a = ph.own("chain_v"), ph.own("chain_a")
        block = ph.block()

        @block.sync
        def _(sp):
            x_v = x.rearrange("b (t p) d -> p (b t) d", p=P)
            for q in range(4):
                sp.dma_start(X[:, 8 * q:8 * q + 8, :], x_v[:, 8 * q:8 * q + 8, :]).then_inc(x_in[q], 16)
            sp.dma_start(w_nat[:, :, :], ins["L0_attn_o_w"].rearrange("(c p) d -> p c d", p=P)).then_inc(loaded, 16)
            with nc.allow_non_contiguous_dma(reason="vectors of 256 numbers"):
                for dst, name in ((q_col, "L0_attn_q"), (k_col, "L0_attn_k"), (nw, "L0_attn_norm_weight")):
                    sp.dma_start(dst[:, :], columns(ins[name])).then_inc(loaded, 16)
                decay = ins["L0_attn_log_decay"].rearrange("(c h) -> h c", c=DC)
                for h in range(P // DH):
                    sp.dma_start(ld[h * DH:(h + 1) * DH, :],
                                 decay[h:h + 1, :].broadcast_to([DH, DC])).then_inc(loaded, 16)

        n_loads = 4 + P // DH

        @block.gpsimd
        def _(pool):
            make_identity(pool, ident[:, :], ident_ready)
            pool.memset(ones[:, :], 1.0).then_inc(groups_ready, 1)
            pool.memset(groups[:, :], 1.0).then_inc(groups_ready, 1)
            pool.memset(minus_half[:, :], -0.5).then_inc(groups_ready, 1)
            pool.wait_ge(groups_ready, 3 + HEAD)
            g3 = groups[:, :].rearrange("p (h r) -> p h r", r=DH)
            pool.affine_select(out=g3, in_=g3, compare_op=ALU.is_ge, fill=0.0, base=0,
                               pattern=[[-DH, P // DH], [0, DH]], channel_multiplier=1).then_inc(groups_ready, 1)
            pool.wait_ge(groups_ready, 4 + HEAD)
            pool.affine_select(out=g3, in_=g3, compare_op=ALU.is_ge, fill=0.0, base=DH - 1,
                               pattern=[[DH, P // DH], [0, DH]], channel_multiplier=-1).then_inc(groups_ready, 1)

            def norm_root(n):
                wait_alone(pool, stood_p, (measured, n + 1))
                inverse_root(pool, rstd[:, :], aggr[:, :, 1], 1.0, LN_EPS, minus_half[:, :], var_eps, rstd_ready, n, stood_p)

            norm_root(0)
            norm_root(1)
            norm_root(2)
            for b, h, s in turns(pool, ahead=3):
                wait_alone(pool, stood_p, (sum_sq_ready, b + 1))
                inverse_root(pool, rms[:, :], sum_sq[:, :], 1.0 / D, 1e-6, minus_half[:, :], mean_eps, rms_ready, b, stood_p)
                if has_next(b, 3):
                    norm_root(b + 3)

        @block.tensor
        def _(pe):
            pe.wait_ge(loaded, 16 * n_loads)
            pe.wait_ge(ident_ready, 2 + HEAD)
            for ct in range(DC):
                for ot in range(DC):
                    last = pe.transpose(p_t[0][:, (ct * DC + ot) * P:(ct * DC + ot + 1) * P],
                                        w_nat[:, ot, ct * P:(ct + 1) * P], ident[:, :])
            last.then_inc(turned, 1)
            pe.wait_ge(groups_ready, 5 + HEAD)
            pe.wait_ge(qk_ready, 1 + HEAD)
            pe.matmul(p_t[1][:, 0:DC], groups[:, :], qk[:, :], start=True, stop=True).then_inc(coef_sum, 1)
            pe.wait_ge(wt_ready, DC + HEAD)
            pe.wait_ge(consts, 1 + HEAD)

            def turn_input(n, s):
                pe.wait_ge(normed, n + 1 + HEAD)
                if not first(n):
                    pe.wait_ge(v_ready, n + HEAD)
                for c in range(DC):
                    for t in range(TB):
                        last = pe.transpose(p_t[0][:, c * S + t * P:c * S + (t + 1) * P],
                                            xn[:, s, t, c * P:(c + 1) * P], ident[:, :])
                last.then_inc(turned_x, 1)

            def project(n, s):
                pe.wait_ge(scanned, n + 1 + HEAD)
                pe.wait_ge(squared, n + 1 + HEAD)
                if not first(n):
                    pe.wait_ge(added, n - 1 + HEAD)
                for t in range(TB):
                    for c in range(DC):
                        pe.matmul(p_m[s][:, t:t + 1], osq[:, s, c, t * P:(t + 1) * P], ones[:, :],
                                  start=(c == 0), stop=(c == DC - 1))
                for t in range(TB):
                    for c in range(DC):
                        last = pe.matmul(p_y[s][:, t * D:(t + 1) * D], o[:, s, c, t * P:(t + 1) * P],
                                         wt[:, c, :], start=(c == 0), stop=(c == DC - 1))
                last.then_inc(y_ready, 1)

            turn_input(0, 0)
            turn_input(1, 1)
            project(0, 0)
            for b, h, s in turns(pe, ahead=3):
                if has_next(b, 2):
                    turn_input(b + 2, s)
                if has_next(b):
                    project(b + 1, 1 - s)

        @block.scalar
        def _(act):
            act.wait_ge(loaded, 16 * n_loads)
            act.activation(lam[:, :], ld[:, :], ACT.Exp, scale=-1.0).then_inc(chain_a, 1)
            act.wait_ge(turned, 1 + HEAD)
            for c in range(DC):
                act.activation(wt[:, c, :], p_t[0][:, c * D:(c + 1) * D], ACT.Copy, scale=nw[:, c:c + 1]).then_inc(wt_ready, 1)
            act.wait_ge(consts, 1 + HEAD)

            def values(n, s):
                act.wait_ge(turned_x, n + 1 + HEAD)
                if not first(n):
                    act.wait_ge(scanned, n - 1 + HEAD)
                for c in range(DC):
                    last = act.activation(v[:, s, c, :], p_t[0][:, c * S:(c + 1) * S], ACT.Copy, scale=coef[:, c:c + 1])
                last.then_inc(v_ready, 1)

            def squares(n, s):
                act.wait_ge(scanned, n + 1 + HEAD)
                if not first(n):
                    act.wait_ge(y_ready, n - 1 + HEAD)
                act.activation(osq[:, s, :, :], o[:, s, :, :], ACT.Square).then_inc(squared, 1)

            values(0, 0)
            values(1, 1)
            squares(0, 0)
            for b, h, s in turns(act, ahead=3):
                if has_next(b):
                    squares(b + 1, 1 - s)
                if has_next(b, 2):
                    values(b + 2, s)

        @block.vector
        def _(dve):
            dve.wait_ge(loaded, 16 * n_loads)
            dve.tensor_tensor(qk[:, :], q_col[:, :], k_col[:, :], ALU.mult).then_inc(qk_ready, 1)
            dve.wait_ge(chain_a, 1)
            chain = Chain(dve, chain_v)
            chain.done(dve.tensor_scalar(lam[:, :], lam[:, :], 1.0, None, ALU.add))
            chain.wait()
            chain.done(dve.reciprocal(lam[:, :], lam[:, :]))
            dve.wait_ge(coef_sum, 1 + HEAD)
            dve.tensor_copy(coef[:, :], p_t[1][:, 0:DC]).then_inc(consts, 1)
            chain.close()

            def measure(n):
                layer_norm_stats(dve, chain, lambda t: tile_of(X, n, t), stats, aggr, measured)

            def norm(n, s):
                dve.wait_ge(rstd_ready, n + 1 + HEAD)
                layer_norm_apply(dve, lambda t: tile_of(X, n, t), lambda t: xn[:, s, t, :], aggr, rstd, normed)

            def scan(n, s):
                dve.wait_ge(v_ready, n + 1 + HEAD)
                for c in range(DC):
                    last = dve.tensor_tensor_scan(o[:, s, c, :], lam[:, c:c + 1].broadcast_to([P, S]),
                                                  v[:, s, c, :], 0.0, ALU.mult, ALU.add)
                last.then_inc(scanned, 1)

            for q in range(4):
                dve.wait_ge(x_in[q], 16)
            measure(0)
            norm(0, 0)
            measure(1)
            norm(1, 1)
            measure(2)
            scan(0, 0)
            chain.close()
            for b, h, s in turns(dve, ahead=3):
                if has_next(b, 2):
                    norm(b + 2, s)
                if has_next(b):
                    scan(b + 1, 1 - s)
                dve.wait_ge(y_ready, b + 1 + HEAD)
                dve.tensor_copy(sum_sq[:, :], p_m[s][:, 0:TB]).then_inc(sum_sq_ready, 1)
                if has_next(b, 3):
                    measure(b + 3)
                dve.wait_ge(rms_ready, b + 1 + HEAD)
                for t in range(TB):
                    last = dve.scalar_tensor_tensor(tile_of(X, b, t), p_y[s][:, t * D:(t + 1) * D], rms[:, t:t + 1],
                                                    tile_of(X, b, t), ALU.mult, ALU.add)
                last.then_inc(added, 1)
                chain.close()
            dve.wait_ge(added, B + HEAD)


PAIRS = H // 2
UNITS = TB * PAIRS
RB = 4
OFF = 1e30
VW = 2 * DH
HG = P // VW


def cross_attention(nc, ins, X, layer, causal):
    low = causal
    DT = BF16 if low else F32
    name = f"L{layer}_xattn_"
    with Phase(nc, f"xa{layer}") as ph:
        ident = ph.sb("ident", [P, P], F32)
        ident_d = ph.sb("ident_d", [P, P], DT) if low else ident
        w_nat = ph.sb("w_nat", [P, 4, DC, D])
        w = ph.sb("w", [P, 4, DC, D], DT)
        cols = ph.sb("cols", [P, 2, DC])
        cols_d = ph.sb("cols_d", [P, 2, DC])
        rows = ph.sb("rows", [P, 2, D])
        rows_d = ph.sb("rows_d", [P, 2, D], DT) if low else rows
        side = ph.sb("side", [P, 2, 4])
        parity = ph.sb("parity", [P, 2])
        q_bias = ph.sb("q_bias", [P, DC, 2])
        lam_b = ph.sb("lam_b", [P, 1])
        minus_half = ph.sb("minus_half", [P, TB])
        stats = ph.sb("stats", [P, TB, 6])
        aggr = ph.sb("aggr", [P, TB, 2])
        rstd = ph.sb("rstd", [P, TB])
        ctx = ph.sb("ctx", [P, 2, TB, D])
        ctx_d = ph.sb("ctx_d", [P, TB, D], DT) if low else None
        xn = ph.sb("xn", [P, TB, D], DT)
        xT = ph.sb("xT", [P, DC, S], DT)
        cT = ph.sb("cT", [P, DC, S], DT)
        raw = ph.sb("raw", [P, 2, S], I32) if causal else ph.sb("raw", [P, 2, TB, S])
        key_off = ph.sb("key_off", [P, 2, S]) if causal else None
        neg = ph.sb("neg", [P, 2, TB, S])
        q_r = ph.sb("q_r", [P, DC, S], DT) if low else None
        q_f = ph.sb("q_f", [P, DC, S], DT) if low else None
        k_r = ph.sb("k_r", [P, DC, S], DT) if low else None
        v_r = ph.sb("v_r", [P, TB, D], DT) if low else None
        v_f = ph.sb("v_f", [P, TB, D], DT) if low else None
        q = ph.sb("q", [P, 2, 2, DC, S], DT)
        k = ph.sb("k", [P, 2, DC, S], DT)
        v = ph.sb("v", [P, 2, TB, H, VW])
        sc = ph.sb("sc", [P, RB, 2, S])
        nmax = ph.sb("nmax", [P, RB, 2])
        pr = ph.sb("pr", [P, RB, 2, S])
        prT = ph.sb("prT", [P, RB, 2, TB, P])
        sums = ph.sb("sums", [P, H // HG, P])
        inv = ph.sb("inv", [P, TB, H])
        o = ph.sb("o", [P, TB, D], DT)
        oT = ph.sb("oT", [P, DC, S], DT)
        y_r = ph.sb("y_r", [P, TB, D], DT) if low else None
        y_f = ph.sb("y_f", [P, TB, D], DT if low else F32)
        p_a = [ph.ps(f"p_a{i}") for i in range(2)]
        p_ad = [a[:, :].bitcast(BF16)[:, 0:512] if low else a for a in p_a]
        p_s = [ph.ps(f"p_s{i}") for i in range(2)]
        p_p = [ph.ps(f"p_p{i}") for i in range(2)]
        p_o = [ph.ps(f"p_o{i}") for i in range(2)]

        names = ("loaded_w loaded_c ident_ready turned freed consts cast ones_set "
                 "measured var_eps rstd_ready normed turned_x x_ready c_ready k_proj k_read q_proj q_read v_proj v_read "
                 "q_ready k_ready v_ready off_ready neg_ready scored shifted exped p_turned p_copied_a p_copied_v pv sums_read sums_turned "
                 "o_ready turned_o oT_ready y_ready y_read y_biased added chain_v chain_a chain_p stood_v stood_p").split()
        (loaded_w, loaded_c, ident_ready, turned, freed, consts, cast, ones_set,
         measured, var_eps, rstd_ready, normed, turned_x, x_ready, c_ready, k_proj, k_read, q_proj, q_read, v_proj, v_read,
         q_ready, k_ready, v_ready, off_ready, neg_ready, scored, shifted, exped, p_turned, p_copied_a, p_copied_v, pv, sums_read, sums_turned,
         o_ready, turned_o, oT_ready, y_ready, y_read, y_biased, added, chain_v, chain_a, chain_p, stood_v, stood_p) = (
            ph.own(n) if n.startswith(OWN) else ph.sem(n) for n in names)
        if not low:
            k_read, q_read, v_read, y_read = k_ready, q_ready, v_ready, y_biased
        ctx_in = [ph.own(f"ctx_in{s}") for s in range(2)]
        raw_in = [ph.own(f"raw_in{s}") for s in range(2)]
        block = ph.block()

        TURN, SUM = 2, 4
        AT_NORM, AT_X, AT_O, AT_K, AT_Y, AT_Q, AT_V = 1, 4, 7, 6, 9, 10, 12

        def keys(t):
            return (t + 1) * P if causal else S

        def live(b, m):
            return m >= 0 or not at(b, 0)

        def at(b, n):
            return isinstance(b, int) and b == n

        def has_before(b):
            return not at(b, 0)

        def tile_done(b, n):
            if n % PAIRS or not live(b, n - 1) or (at(b, B) and n > 0):
                return None
            return TB * b + n // PAIRS

        def has_next(b):
            return not isinstance(b, int) or b < B - 1

        @block.sync
        def _(sp):
            def load(b, h, s):
                sp.dma_start(ctx[:, s, :, :], ins["ctx_1024"][bass.ds(b, 1), :, :].rearrange("a (t p) d -> p (a t) d", p=P)).then_inc(ctx_in[s], 16)
                if causal:
                    sp.dma_start(raw[:, s, :], ins["mask_BxS2_if1"][bass.ds(b, 1), :].rearrange("a k -> (a k)").partition_broadcast(P)).then_inc(raw_in[s], 16)
                else:
                    sp.dma_start(raw[:, s, :, :], ins["fside_BxSxS2_0"][bass.ds(b, 1), :, :].rearrange("a (t p) k -> p (a t) k", p=P)).then_inc(raw_in[s], 16)

            load(0, 0, 0)
            for n, m in enumerate(("Wq", "Wk", "Wv", "Wo")):
                sp.dma_start(w_nat[:, n, :, :], ins[name + m].rearrange("(c p) d -> p c d", p=P)).then_inc(loaded_w, 16)
            with nc.allow_non_contiguous_dma(reason="vectors of 256 numbers"):
                for n, m in enumerate(("bq", "bk")):
                    sp.dma_start(cols[:, n, :], columns(ins[name + m])).then_inc(loaded_c, 16)
                for n, m in enumerate(("bv", "bo")):
                    sp.dma_start(rows[:, n, :], ins[name + m].partition_broadcast(P)).then_inc(loaded_c, 16)
                if not causal:
                    sp.dma_start(lam_b[:, :], ins["L1_xattn_lambda_bias"].partition_broadcast(P)).then_inc(loaded_c, 16)
            for b, h, s in turns(sp):
                if has_next(b):
                    if has_before(b):
                        sp.wait_ge(cast if low else turned_x, b + HEAD)
                        sp.wait_ge(neg_ready, b + HEAD)
                    load(b + 1, h + s, 1 - s)

        n_cols = 4 if causal else 5

        @block.gpsimd
        def _(pool):
            make_identity(pool, ident[:, :], ident_ready)
            chain = Chain(pool, chain_p)
            pool.wait_ge(ident_ready, 2 + HEAD)
            if low:
                chain.done(pool.tensor_copy(ident_d[:, :], ident[:, :]))
            chain.done(pool.memset(minus_half[:, :], -0.5))
            chain.done(pool.memset(v[:, :, :, :, :], 1.0))
            chain.done(pool.memset(side[:, :, :], -1.0 / DH ** 0.5))
            chain.wait()
            for n in range(2):
                chain.done(pool.affine_select(out=side[:, n, :], in_=side[:, n, :], compare_op=ALU.is_ge, fill=0.0,
                                              base=-DH * n, pattern=[[-2 * DH, 4]], channel_multiplier=1))
            chain.wait()
            for n in range(2):
                chain.done(pool.affine_select(out=side[:, n, :], in_=side[:, n, :], compare_op=ALU.is_ge, fill=0.0,
                                              base=DH * n + DH - 1, pattern=[[2 * DH, 4]], channel_multiplier=-1))
            chain.wait()
            pool.sem_inc(ones_set, 1)

            def prepare(b, h, s):
                if low:
                    pool.wait_ge(ctx_in[s], 16 * h + 16)
                    wait_alone(pool, stood_p, (turned_x, b))
                    pool.tensor_copy(ctx_d[:, :, :], ctx[:, s, :, :]).then_inc(cast, 1)
                wait_alone(pool, stood_p, (measured, b + 1))
                inverse_root(pool, rstd[:, :], aggr[:, :, 1], 1.0, LN_EPS, minus_half[:, :], var_eps, rstd_ready, b, stood_p)
                pool.wait_ge(raw_in[s], 16 * h + 16)
                if not isinstance(b, int) or b >= 2:
                    pool.wait_ge(shifted, UNITS * (b - 1) + HEAD)
                pool.sem_inc(stood_p, 1)
                if causal:
                    pool.tensor_scalar(key_off[:, s, :], raw[:, s, :], 0.0, OFF, ALU.is_le, ALU.mult).then_inc(off_ready, 1)
                    wait_alone(pool, stood_p, (off_ready, b + 1))
                    for t in range(TB):
                        last = pool.affine_select(out=neg[:, s, t, :], in_=key_off[:, s, :], compare_op=ALU.is_ge,
                                                  fill=OFF, base=t * P, pattern=[[-1, S]], channel_multiplier=1)
                    last.then_inc(neg_ready, 1)
                else:
                    pool.tensor_scalar(neg[:, s, :, :], raw[:, s, :, :], lam_b[:, 0:1], None, ALU.mult).then_inc(neg_ready, 1)

            if not causal:
                pool.wait_ge(consts, 1 + HEAD)
            def finish_values(b, s):
                wait_alone(pool, stood_p, (v_read, b + 1))
                if not at(b, 0):
                    wait_alone(pool, stood_p, (pv, UNITS * (b - 1)))
                for t in range(TB):
                    chain.done(pool.tensor_tensor(v_f[:, t, :], v_r[:, t, :], rows_d[:, 0, :], ALU.add))
                chain.wait()
                pool.tensor_copy(v[:, s, :, :, 0:DH], v_f[:, :, :].rearrange("p t (h r) -> p t h r", r=DH)).then_inc(v_ready, 1)

            def add(b):
                wait_alone(pool, stood_p, (y_biased, b + 1))
                pool.tensor_tensor(X[:, bass.ds(TB * b, TB), :], y_f[:, :, :], X[:, bass.ds(TB * b, TB), :], ALU.add).then_inc(added, 1)

            prepare(0, 0, 0)
            if low:
                pool.wait_ge(consts, 1 + HEAD)
                finish_values(0, 0)
            chain.close()
            for b, h, s in turns(pool, drain=True):
                if has_next(b):
                    prepare(b + 1, h + s, 1 - s)
                if has_before(b):
                    add(b - 1)
                if has_next(b) and low:
                    finish_values(b + 1, 1 - s)
                chain.close()

        def copied(m):
            return (p_copied_a, (m + 1) // 2) if m % 2 else (p_copied_v, m // 2 + 1)

        @block.tensor
        def _(pe):
            def turn(bank, tiles, done):
                for c in range(DC):
                    for t in range(TB):
                        last = pe.transpose(bank[:, c * S + t * P:c * S + (t + 1) * P], tiles(t)[:, c * P:(c + 1) * P], ident_d[:, :])
                if done is not None:
                    last.then_inc(done, 1)

            def project(bank, n, src, done):
                for oc in range(DC):
                    for ic in range(DC):
                        last = pe.matmul(bank[:, oc * S:(oc + 1) * S], w[:, n, ic, oc * P:(oc + 1) * P],
                                         src[:, ic, :], start=(ic == 0), stop=(ic == DC - 1))
                last.then_inc(done, 1)

            def project_rows(bank, src, n, done):
                for t in range(TB):
                    for ic in range(DC):
                        last = pe.matmul(bank[:, t * D:(t + 1) * D], src[:, ic, t * P:(t + 1) * P], w[:, n, ic, :],
                                         start=(ic == 0), stop=(ic == DC - 1))
                last.then_inc(done, 1)

            def turn_inputs(b, h, s):
                pe.wait_ge(normed, b + 1 + HEAD)
                if low:
                    pe.wait_ge(cast, b + 1 + HEAD)
                else:
                    pe.wait_ge(ctx_in[s], 16 * h + 16)
                if not at(b, 0):
                    pe.wait_ge(v_read, b + HEAD)
                    pe.wait_ge(q_read, b + HEAD)
                turn(p_ad[0], lambda t: xn[:, t, :], None)
                turn(p_ad[1], lambda t: ctx_d[:, t, :] if low else ctx[:, s, t, :], turned_x)

            def project_keys(b):
                pe.wait_ge(c_ready, b + 1 + HEAD)
                project(p_a[1], 1, cT, k_proj)

            def project_queries(b):
                pe.wait_ge(x_ready, b + 1 + HEAD)
                pe.wait_ge(k_read, b + 1 + HEAD)
                project(p_a[1], 0, xT, q_proj)

            def project_values(b):
                if not at(b, 0) and not at(b, 1):
                    pe.wait_ge(y_read, b - 1 + HEAD)
                project_rows(p_a[0], cT, 2, v_proj)

            def scores(b, s, n):
                t, j = divmod(n, PAIRS)
                if n == 0:
                    pe.wait_ge(q_ready, b + 1 + HEAD)
                    pe.wait_ge(k_ready, b + 1 + HEAD)
                if live(b, n - 2):
                    pe.wait_ge(shifted, UNITS * b + n - 1 + HEAD)
                for e in range(2):
                    h = 2 * j + e
                    c, r = h // 8, 32 * (h % 8 // 2)
                    last = pe.matmul(p_s[n % 2][:, e * S:e * S + keys(t)], q[r:r + 32, s, e, c, t * P:(t + 1) * P],
                                     k[r:r + 32, s, c, 0:keys(t)], start=True, stop=True)
                last.then_inc(scored, 1)

            def turn_unit(b, m):
                t = m % UNITS // PAIRS
                pe.wait_ge(exped, UNITS * b + m + 1 + HEAD)
                if live(b, m - 2):
                    former, count = copied(m - 2)
                    pe.wait_ge(former, UNITS // 2 * b + count + HEAD)
                for e in range(2):
                    for kt in range(keys(t) // P):
                        last = pe.transpose(p_p[m % 2][:, (e * TB + kt) * P:(e * TB + kt + 1) * P],
                                            pr[:, m % RB, e, kt * P:(kt + 1) * P], ident[:, :])
                last.then_inc(p_turned, 1)

            def sum_unit(b, s, m):
                t, j = divmod(m % UNITS, PAIRS)
                nk = keys(t) // P
                own, count = copied(m)
                pe.wait_ge(own, UNITS // 2 * b + count + HEAD)
                if j == 0:
                    if t == 0:
                        pe.wait_ge(v_ready, b + 1 + HEAD)
                    if not at(b, 0):
                        pe.wait_ge(o_ready, TB * (b - 1) + t + 1 + HEAD)
                for e in range(2):
                    h = 2 * j + e
                    for kt in range(nk):
                        last = pe.matmul(p_o[t][h % HG * VW:(h % HG + 1) * VW, h // HG * P:(h // HG + 1) * P], v[:, s, kt, h, :],
                                         prT[:, m % RB, e, kt, :], start=(kt == 0), stop=(kt == nk - 1))
                last.then_inc(pv, 1)

            def turn_sums(t, done):
                pe.wait_ge(sums_read, done + HEAD)
                for g in range(H // HG):
                    last = pe.transpose(p_o[t][:, g * P:(g + 1) * P], sums[:, g, :], ident[:, :])
                last.then_inc(sums_turned, 1)

            pe.wait_ge(ident_ready, 2 + HEAD)
            pe.wait_ge(ones_set, 1 + HEAD)
            if not low:
                pe.wait_ge(loaded_w, 64)
                blocks = [w_nat[:, n, ot, ct * P:(ct + 1) * P] for n in range(4) for ct in range(DC) for ot in range(DC)]
                transpose_blocks(pe, blocks, p_a, ident[:, :], turned, freed)
            pe.wait_ge(freed, (1 if low else 4) + HEAD)
            pe.wait_ge(consts, 1 + HEAD)
            turn_inputs(0, 0, 0)
            project_keys(0)
            project_queries(0)
            project_values(0)
            for b, h, s in turns(pe, drain=True):
                for n in range(UNITS):
                    if at(b, B) and n > AT_Y:
                        break
                    if not at(b, B):
                        scores(b, s, n)
                    summing = live(b, n - SUM) and (not at(b, B) or n < SUM)
                    if summing and not low:
                        sum_unit(b, s if n >= SUM else 1 - s, n - SUM)
                    if live(b, n - TURN) and (not at(b, B) or n < TURN):
                        turn_unit(b, n - TURN)
                    if summing and low:
                        sum_unit(b, s if n >= SUM else 1 - s, n - SUM)
                    done = tile_done(b, n - SUM - 1)
                    if done is not None:
                        turn_sums((n - SUM - 2) % UNITS // PAIRS, done)
                    if n == AT_X and has_next(b):
                        turn_inputs(b + 1, h + s, 1 - s)
                    if n == AT_O and has_before(b):
                        pe.wait_ge(o_ready, TB * b + HEAD)
                        if has_next(b):
                            pe.wait_ge(x_ready, b + 2 + HEAD)
                        turn(p_ad[0], lambda t: o[:, t, :], turned_o)
                    if n == AT_K and has_next(b):
                        project_keys(b + 1)
                    if n == AT_Y and has_before(b):
                        pe.wait_ge(oT_ready, b + HEAD)
                        project_rows(p_a[0], oT, 3, y_ready)
                    if n == AT_Q and has_next(b):
                        project_queries(b + 1)
                    if n == AT_V and has_next(b):
                        project_values(b + 1)

        def turned_unit(m):
            nk = keys(m % UNITS // PAIRS) // P
            return prT[:, m % RB, :, 0:nk, :], p_p[m % 2][:, :].rearrange("p (e k q) -> p e k q", e=2, k=TB)[:, :, 0:nk, :]

        @block.scalar
        def _(act):
            def read_x(b):
                act.wait_ge(turned_x, b + 1 + HEAD)
                if not at(b, 0):
                    act.wait_ge(q_proj, b + HEAD)
                act.activation(flat(xT[:, :, :]), p_ad[0][:, :], ACT.Copy).then_inc(x_ready, 1)

            def read_keys(b):
                act.wait_ge(k_proj, b + 1 + HEAD)
                if not at(b, 0):
                    act.wait_ge(k_ready, b + HEAD)
                act.activation(flat(k_r[:, :, :]), p_a[1][:, :], ACT.Copy).then_inc(k_read, 1)

            def read_queries(b, s):
                act.wait_ge(q_proj, b + 1 + HEAD)
                if low:
                    if not at(b, 0):
                        act.wait_ge(q_ready, b + HEAD)
                    act.activation(flat(q_r[:, :, :]), p_a[1][:, :], ACT.Copy).then_inc(q_read, 1)
                else:
                    if not at(b, 0):
                        act.wait_ge(scored, UNITS * (b - 1) + HEAD)
                    for e in range(2):
                        for c in range(DC):
                            last = act.activation(q[:, s, e, c, :], p_a[1][:, c * S:(c + 1) * S], ACT.Identity,
                                                  bias=q_bias[:, c, e:e + 1], scale=parity[:, e:e + 1])
                    last.then_inc(q_ready, 1)

            def read_values(b):
                act.wait_ge(v_proj, b + 1 + HEAD)
                if not at(b, 0):
                    act.wait_ge(v_ready, b + HEAD)
                act.activation(flat(v_r[:, :, :]), p_a[0][:, :], ACT.Copy).then_inc(v_read, 1)

            act.wait_ge(loaded_w, 64)
            if low:
                act.activation(w[:, :, :, :], w_nat[:, :, :, :], ACT.Copy).then_inc(freed, 1)
            else:
                evacuate_blocks(act, [flat(w[:, n, :, :]) for n in range(4)], p_a, turned, freed)
            act.wait_ge(consts, 1 + HEAD)
            read_x(0)
            if low:
                read_keys(0)
            read_queries(0, 0)
            if low:
                read_values(0)
            for b, h, s in turns(act, drain=True):
                for n in range(UNITS):
                    if at(b, B) and n > AT_Y:
                        break
                    if not at(b, B):
                        t = n // PAIRS
                        act.wait_ge(shifted, UNITS * b + n + 1 + HEAD)
                        if live(b, n - RB):
                            act.wait_ge(p_turned, UNITS * b + n - RB + 1 + HEAD)
                        for e in range(2):
                            last = act.activation(pr[:, n % RB, e, 0:keys(t)], sc[:, n % RB, e, 0:keys(t)], ACT.Exp,
                                                  bias=nmax[:, n % RB, e:e + 1], scale=-1.0)
                        last.then_inc(exped, 1)
                    m = n - TURN
                    if m % 2 == 1 and live(b, m) and (not at(b, B) or n < TURN):
                        act.wait_ge(p_turned, UNITS * b + m + 1 + HEAD)
                        if live(b, m - RB):
                            act.wait_ge(pv, UNITS * b + m - RB + 1 + HEAD)
                        act.activation(*turned_unit(m), ACT.Copy).then_inc(p_copied_a, 1)
                    done = tile_done(b, n - SUM)
                    if done is not None:
                        act.wait_ge(pv, UNITS * b + n - SUM + HEAD)
                        if not (at(b, 0)):
                            act.wait_ge(sums_turned, done - 1 + HEAD)
                        act.activation(flat(sums[:, :, :]), p_o[(n - SUM - 1) % UNITS // PAIRS][:, :], ACT.Copy).then_inc(sums_read, 1)
                    if n == AT_X and has_next(b):
                        read_x(b + 1)
                    if n == AT_O and has_before(b):
                        act.wait_ge(turned_o, b + HEAD)
                        if not at(b, 1):
                            act.wait_ge(y_ready, b - 1 + HEAD)
                        act.activation(flat(oT[:, :, :]), p_ad[0][:, :], ACT.Copy).then_inc(oT_ready, 1)
                    if n == AT_K and has_next(b) and low:
                        read_keys(b + 1)
                    if n == AT_Y and has_before(b) and low:
                        act.wait_ge(y_ready, b + HEAD)
                        if not at(b, 1):
                            act.wait_ge(y_biased, b - 1 + HEAD)
                        act.activation(flat(y_r[:, :, :]), p_a[0][:, :], ACT.Copy).then_inc(y_read, 1)
                    if n == AT_Q and has_next(b):
                        read_queries(b + 1, 1 - s)
                    if n == AT_V and has_next(b) and low:
                        read_values(b + 1)

        @block.vector
        def _(dve):
            chain = Chain(dve, chain_v)

            def measure(b):
                layer_norm_stats(dve, chain, lambda t: tile_of(X, b, t), stats, aggr, measured)

            def norm(b):
                dve.wait_ge(rstd_ready, b + 1 + HEAD)
                if not at(b, 0):
                    dve.wait_ge(turned_x, b + HEAD)
                layer_norm_apply(dve, lambda t: tile_of(X, b, t), lambda t: xn[:, t, :], aggr, rstd, normed)

            def read_context(b):
                dve.wait_ge(turned_x, b + 1 + HEAD)
                if not at(b, 0):
                    dve.wait_ge(v_proj, b + HEAD)
                dve.tensor_copy(flat(cT[:, :, :]), p_ad[1][:, :]).then_inc(c_ready, 1)

            def finish_keys(b, s):
                dve.wait_ge(k_read if low else k_proj, b + 1 + HEAD)
                if not at(b, 0):
                    dve.wait_ge(scored, UNITS * (b - 1) + HEAD)
                for c in range(DC):
                    last = dve.tensor_scalar(k[:, s, c, :], k_r[:, c, :] if low else p_a[1][:, c * S:(c + 1) * S],
                                             cols_d[:, 1, c:c + 1], None, ALU.add)
                    if c < DC - 1:
                        chain.done(last)
                last.then_inc(k_ready, 1)

            def finish_queries(b, s):
                dve.wait_ge(q_read, b + 1 + HEAD)
                if not at(b, 0):
                    dve.wait_ge(scored, UNITS * (b - 1) + HEAD)
                for c in range(DC):
                    chain.done(dve.tensor_scalar(q_f[:, c, :], q_r[:, c, :], cols_d[:, 0, c:c + 1], None, ALU.add))
                chain.wait()
                for e in range(2):
                    last = dve.tensor_scalar(q[:, s, e, :, :], q_f[:, :, :], parity[:, e:e + 1], None, ALU.mult)
                last.then_inc(q_ready, 1)

            def finish_values(b, s):
                dve.wait_ge(v_proj, b + 1 + HEAD)
                if not at(b, 0):
                    dve.wait_ge(pv, UNITS * (b - 1) + HEAD)
                for t in range(TB):
                    last = dve.tensor_tensor(v[:, s, t, :, 0:DH], p_a[0][:, t * D:(t + 1) * D].rearrange("p (h r) -> p h r", r=DH),
                                             rows[:, 0, :].rearrange("p (h r) -> p h r", r=DH), ALU.add)
                last.then_inc(v_ready, 1)

            dve.wait_ge(loaded_c, 16 * n_cols)
            dve.wait_ge(ones_set, 1 + HEAD)
            chain.done(dve.tensor_reduce(parity[:, :], side[:, :, :], AX.X, ALU.add))
            if low:
                chain.done(dve.tensor_copy(rows_d[:, :, :], rows[:, :, :]))
                chain.done(dve.tensor_copy(q_r[:, 0, 0:2 * DC], flat(cols[:, :, :])))
                chain.wait()
                chain.done(dve.tensor_copy(flat(cols_d[:, :, :]), q_r[:, 0, 0:2 * DC]))
            else:
                chain.wait()
                for e in range(2):
                    chain.done(dve.tensor_scalar(q_bias[:, :, e], cols[:, 0, :], parity[:, e:e + 1], None, ALU.mult))
                chain.done(dve.tensor_copy(cols_d[:, :, :], cols[:, :, :]))
                chain.done(dve.tensor_scalar(lam_b[:, :], lam_b[:, :], -1.0, None, ALU.mult))
            chain.wait()
            dve.sem_inc(consts, 1)
            measure(0)
            norm(0)
            read_context(0)
            finish_keys(0, 0)
            if low:
                finish_queries(0, 0)
            else:
                finish_values(0, 0)
            chain.close()
            for b, h, s in turns(dve, drain=True):
                for n in range(UNITS):
                    if at(b, B) and n > AT_Y + 1:
                        break
                    if not at(b, B):
                        t = n // PAIRS
                        if n == 0:
                            dve.wait_ge(neg_ready, b + 1 + HEAD)
                            dve.sem_inc(stood_v, 1)
                        if live(b, n - RB):
                            wait_alone(dve, stood_v, (scored, UNITS * b + n + 1), (exped, UNITS * b + n - RB + 1))
                        else:
                            dve.wait_ge(scored, UNITS * b + n + 1 + HEAD)
                        for e in range(2):
                            last = dve.tensor_tensor_reduce(
                                out=sc[:, n % RB, e, 0:keys(t)], in0=p_s[n % 2][:, e * S:e * S + keys(t)],
                                in1=neg[:, s, t, 0:keys(t)], scale=1.0, scalar=3e38, op0=ALU.add, op1=ALU.min,
                                accum_out=nmax[:, n % RB, e:e + 1])
                        last.then_inc(shifted, 1)
                    m = n - TURN
                    if m % 2 == 0 and live(b, m) and (not at(b, B) or n < TURN):
                        dve.wait_ge(p_turned, UNITS * b + m + 1 + HEAD)
                        if live(b, m - RB):
                            dve.wait_ge(pv, UNITS * b + m - RB + 1 + HEAD)
                        dve.tensor_copy(*turned_unit(m)).then_inc(p_copied_v, 1)
                    m = n - SUM - 2
                    done = tile_done(b, m)
                    if done is not None:
                        t = (m - 1) % UNITS // PAIRS
                        dve.wait_ge(sums_turned, done + HEAD)
                        heads = p_o[t][:, 0:H * VW].rearrange("p (h r) -> p h r", r=VW)
                        chain.done(dve.reciprocal(inv[:, t, :], heads[:, :, DH]))
                        chain.wait()
                        if m > 0 and not at(b, 0) and not at(b, 1):
                            dve.wait_ge(turned_o, b - 1 + HEAD)
                        dve.tensor_tensor(o[:, t, :].rearrange("p (h r) -> p h r", r=DH), heads[:, :, 0:DH],
                                          inv[:, t, :].unsqueeze(2).broadcast_to([P, H, DH]), ALU.mult).then_inc(o_ready, 1)
                    if n == AT_NORM and has_next(b):
                        measure(b + 1)
                    if n == AT_NORM + 1 and has_next(b):
                        norm(b + 1)
                    if n == AT_X and has_next(b):
                        read_context(b + 1)
                    if n == AT_K + 1 and has_next(b):
                        finish_keys(b + 1, 1 - s)
                    if n == AT_Y + 1 and has_before(b):
                        dve.wait_ge(y_read if low else y_ready, b + HEAD)
                        y_src = flat(y_r[:, :, :]) if low else p_a[0][:, :]
                        if not at(b, 1):
                            dve.wait_ge(added, b - 1 + HEAD)
                        for t in range(TB):
                            last = dve.tensor_tensor(y_f[:, t, :], y_src[:, t * D:(t + 1) * D], rows_d[:, 1, :], ALU.add)
                        last.then_inc(y_biased, 1)
                    if n == AT_Q + 1 and has_next(b) and low:
                        finish_queries(b + 1, 1 - s)
                    if n == AT_V + 1 and has_next(b) and not low:
                        finish_values(b + 1, 1 - s)
                chain.close()
            dve.wait_ge(added, B + HEAD)


G = 256
TG = G // P
NG = 2 * B * S // G + E - 1
RING = 3
GR = 8


def experts_ffn(nc, ins, X):
    rows_in = nc.dram_tensor("moe_rows_in", (NG * G, D), F32, kind="Internal").ap()
    rows_out = nc.dram_tensor("moe_rows_out", (NG * G, D), F32, kind="Internal").ap()
    with Phase(nc, "moe") as ph:
        ident = ph.sb("ident", [P, P])
        below = ph.sb("below", [P, P])
        ones = ph.sb("ones", [P, P])
        zeros = ph.sb("zeros", [P, D])
        minus_half = ph.sb("minus_half", [P, TB])
        gate = ph.sb("gate", [E, D])
        gateT = ph.sb("gateT", [P, DC, E])
        b1_nat = ph.sb("b1_nat", [E * HC, P])
        b1 = ph.sb("b1", [P, E * HC])
        b2 = ph.sb("b2", [P, E, D])
        stats = ph.sb("stats", [P, TB, 6])
        aggr = ph.sb("aggr", [P, TB, 2])
        rstd = ph.sb("rstd", [P, TB])
        XN = ph.sb("XN", [P, NT, D])
        XN_s = [ph.sb(f"XN_s{i}", [P, TB, D]) for i in range(2)]
        xT = ph.sb("xT", [P, 2, DC, S])
        lg = ph.sb("lg", [P, NT, E])
        falling = ph.sb("falling", [P, E])
        ramp_i = ph.sb("ramp_i", [P, NG], I32)
        ramp = ph.sb("ramp", [P, NG])
        steps = ph.sb("steps", [P, B])
        best = ph.sb("best", [P, 2, NT])
        pick = ph.sb("pick", [P, 2, NT, E])
        cand = ph.sb("cand", [P, NT, E])
        cmax = ph.sb("cmax", [P, NT])
        lg2 = ph.sb("lg2", [P, NT, E])
        probs = ph.sb("probs", [P, NT, E])
        zsum = ph.sb("zsum", [P, NT])
        gap = ph.sb("gap", [P, NT])
        wsum = ph.sb("wsum", [P, NT])
        wt = ph.sb("wt", [P, 2, NT])
        both = ph.sb("both", [P, NT, E])
        before = ph.sb("before", [P, NT, E])
        total = ph.sb("total", [P, NT, E])
        upto = ph.sb("upto", [P, NT, E])
        over = ph.sb("over", [P, E, B])
        ngroups = ph.sb("ngroups", [P, E])
        gend = ph.sb("gend", [P, E])
        gstart = ph.sb("gstart", [P, E])
        passed = ph.sb("passed", [P, NG, E - 1])
        owner = ph.sb("owner", [P, NG])
        owner_i = ph.sb("owner_i", [P, NG], I32)
        place = ph.sb("place", [P, 2, NT])
        place_i = ph.sb("place_i", [P, 2, NT], U32)
        w1 = ph.sb("w1", [P, RING, DC, HID])
        w2 = ph.sb("w2", [P, RING, HC, D])
        gx = ph.sb("gx", [P, RING, TG, D])
        gT = ph.sb("gT", [P, RING, DC, G])
        hT = ph.sb("hT", [P, HC, G])
        gy = ph.sb("gy", [P, RING, TG, D])
        got = ph.sb("got", [P, GR, D])
        p_t = ph.ps("p_t")
        p_c = ph.ps("p_c")
        p_h = [ph.ps(f"p_h{i}") for i in range(3)]
        p_y = ph.ps("p_y")
        names = ("loaded zeroed ident_ready set_up turned freed measured var_eps rstd_ready normed noted turned_x xT_ready logits lg_read "
                 "gap_ready exp_ready both_ready counted routed scattered gT_turned gT_ready hidden gelu_ready y_ready gy_ready stored "
                 "combined chain_v chain_p stood_p").split()
        s_ = {n: ph.own(n) if n.startswith(OWN) else ph.sem(n) for n in names}
        fed = [ph.own(f"fed{i}") for i in range(RING)]
        kept = [ph.sem(f"kept{i}") for i in range(RING)]
        gathered = [ph.own(f"gathered{i}") for i in range(GR)]
        block = ph.block()

        def groups(eng):
            for r in range(RING):
                yield 0, r, r
            with eng.Fori(0, NG // RING - 2) as i:
                for r in range(RING):
                    yield i + 1, RING * (i + 1) + r, r
            for r in range(RING):
                yield NG // RING - 1, NG - RING + r, r

        def is_group(j, n):
            return isinstance(j, int) and j == n

        def expert_of(eng, j):
            return eng.value_load(owner_i[0:1, bass.ds(j, 1)], min_val=0, max_val=E - 1)

        @block.sync
        def _(sp):
            sp.dma_start(gate[:, :], ins["L0_ffn_gate_w"]).then_inc(s_["loaded"], 16)
            sp.dma_start(b1_nat[:, :], ins["L0_ffn_b1"].rearrange("e (c p) -> (e c) p", p=P)).then_inc(s_["loaded"], 16)
            sp.dma_start(b2[:, :, :], ins["L0_ffn_b2"].partition_broadcast(P)).then_inc(s_["loaded"], 16)
            sp.wait_ge(s_["set_up"], 1 + HEAD)
            zero_src = zeros[:, :].unsqueeze(1).broadcast_to([P, NG * TG, D])
            sp.dma_start(rows_in.rearrange("(n p) d -> p n d", p=P), zero_src).then_inc(s_["zeroed"], 16)
            def load_weights(j, r):
                e = expert_of(sp, j)
                sp.dma_start(w1[:, r, :, :], ins["L0_ffn_w1"][bass.ds(e, 1), :, :].rearrange("a (c p) h -> p (a c) h", p=P)).then_inc(fed[r], 16)
                sp.dma_start(w2[:, r, :, :], ins["L0_ffn_w2"][bass.ds(e, 1), :, :].rearrange("a (c p) d -> p (a c) d", p=P)).then_inc(fed[r], 16)

            def load_rows(j, r):
                sp.dma_start(gx[:, r, :, :], rows_in[bass.ds(j * G, G), :].rearrange("(t p) d -> p t d", p=P)).then_inc(fed[r], 16)

            sp.wait_ge(s_["routed"], 1 + HEAD)
            for i, j, r in groups(sp):
                if isinstance(j, int) and j < RING:
                    load_weights(j, r)
                    if j == RING - 1:
                        sp.wait_ge(s_["scattered"], 16 * 2 * NT)
                        for k in range(RING):
                            load_rows(k, k)
                else:
                    sp.wait_ge(s_["y_ready"], j - RING + 1 + HEAD)
                    load_rows(j, r)
                    load_weights(j, r)

        @block.gpsimd
        def _(pool):
            make_identity(pool, ident[:, :], s_["ident_ready"])
            chain = Chain(pool, s_["chain_p"])
            chain.done(pool.memset(zeros[:, :], 0.0))
            chain.done(pool.memset(ones[:, :], 1.0))
            chain.done(pool.memset(minus_half[:, :], -0.5))
            chain.done(pool.iota(ramp_i[:, :], [[1, NG]], base=0, channel_multiplier=0))
            chain.wait()
            chain.done(pool.tensor_copy(ramp[:, :], ramp_i[:, :]))
            chain.done(pool.affine_select(out=below[:, :], in_=ones[:, :], compare_op=ALU.is_gt, fill=0.0, base=0,
                                          pattern=[[1, P]], channel_multiplier=-1))
            chain.wait()
            chain.done(pool.tensor_scalar(falling[:, :], ramp[:, 0:E], -1.0, float(E), ALU.mult, ALU.add))
            chain.done(pool.tensor_scalar(steps[:, :], ramp[:, 0:B], float(G), None, ALU.mult))
            chain.wait()
            pool.sem_inc(s_["set_up"], 1)
            for b in range(3):
                wait_alone(pool, s_["stood_p"], (s_["measured"], b + 1))
                inverse_root(pool, rstd[:, :], aggr[:, :, 1], 1.0, LN_EPS, minus_half[:, :], s_["var_eps"], s_["rstd_ready"], b, s_["stood_p"])
            for b, h, s in turns(pool, ahead=3):
                if has_next(b, 3):
                    wait_alone(pool, s_["stood_p"], (s_["measured"], b + 4))
                    inverse_root(pool, rstd[:, :], aggr[:, :, 1], 1.0, LN_EPS, minus_half[:, :], s_["var_eps"], s_["rstd_ready"], b + 3, s_["stood_p"])
            pool.wait_ge(s_["routed"], 1 + HEAD)
            pool.wait_ge(s_["noted"], B + HEAD)
            pool.wait_ge(s_["zeroed"], 16)
            for t in range(NT):
                for k in range(2):
                    pool.indirect_dma_start(rows_in, bass.IndirectOffsetOnAxis(ap=place_i[:, k, t:t + 1], axis=0),
                                            XN[:, t, :], None).then_inc(s_["scattered"], 16)
            for r in range(RING):
                pool.wait_ge(kept[r], 16 * (NG // RING) + HEAD)
            for n in range(2 * NT):
                t, k = divmod(n, 2)
                if n >= GR:
                    pool.wait_ge(s_["combined"], n - GR + 1 + HEAD)
                pool.indirect_dma_start(got[:, n % GR, :], None, rows_out,
                                        bass.IndirectOffsetOnAxis(ap=place_i[:, k, t:t + 1], axis=0)).then_inc(gathered[n % GR], 16)

        @block.tensor
        def _(pe):
            pe.wait_ge(s_["loaded"], 48)
            pe.wait_ge(s_["ident_ready"], 2 + HEAD)
            for c in range(DC):
                pe.transpose(p_t[:, c * E:(c + 1) * E], gate[:, c * P:(c + 1) * P], ident[0:E, 0:E])
            pe.transpose(p_t[:, 2 * P:2 * P + E * HC], b1_nat[:, :], ident[0:E * HC, 0:E * HC]).then_inc(s_["turned"], 1)
            pe.wait_ge(s_["freed"], 1 + HEAD)

            def turn_input(n, s):
                pe.wait_ge(s_["normed"], n + 1 + HEAD)
                if not first(n):
                    pe.wait_ge(s_["xT_ready"], n + HEAD)
                for c in range(DC):
                    for t in range(TB):
                        last = pe.transpose(p_t[:, c * S + t * P:c * S + (t + 1) * P], XN_s[s][:, t, c * P:(c + 1) * P], ident[:, :])
                last.then_inc(s_["turned_x"], 1)

            def gate_tokens(n, s):
                pe.wait_ge(s_["xT_ready"], n + 1 + HEAD)
                if not first(n):
                    pe.wait_ge(s_["lg_read"], n - 1 + HEAD)
                for t in range(TB):
                    for ic in range(DC):
                        last = pe.matmul(p_h[s][:, t * E:(t + 1) * E], xT[:, s, ic, t * P:(t + 1) * P], gateT[:, ic, :],
                                         start=(ic == 0), stop=(ic == DC - 1))
                last.then_inc(s_["logits"], 1)

            turn_input(0, 0)
            turn_input(1, 1)
            gate_tokens(0, 0)
            for b, h, s in turns(pe, ahead=3):
                if has_next(b, 2):
                    turn_input(b + 2, s)
                if has_next(b):
                    gate_tokens(b + 1, 1 - s)
            pe.wait_ge(s_["both_ready"], 1 + HEAD)
            pe.wait_ge(s_["lg_read"], B + HEAD)
            both_v = both[:, :, :].rearrange("p t e -> p (t e)")
            pe.matmul(p_c[:, 0:NT * E], below[:, :], both_v, start=True, stop=True)
            pe.matmul(p_t[:, 0:NT * E], ones[:, :], both_v, start=True, stop=True).then_inc(s_["counted"], 1)
            pe.wait_ge(s_["routed"], 1 + HEAD)

            def turn_rows(i, j, r):
                pe.wait_ge(fed[r], 48 * i + 48)
                if not is_group(j, 0):
                    pe.wait_ge(s_["gT_ready"], j + HEAD)
                for c in range(DC):
                    for t in range(TG):
                        last = pe.transpose(p_t[:, c * G + t * P:c * G + (t + 1) * P], gx[:, r, t, c * P:(c + 1) * P], ident[:, :])
                last.then_inc(s_["gT_turned"], 1)

            turn_rows(0, 0, 0)
            for i, j, r in groups(pe):
                pe.wait_ge(s_["gT_ready"], j + 1 + HEAD)
                for n in range(HC // 2):
                    pe.wait_ge(s_["gelu_ready"], HC // 2 * j + max(n - 2, 0) + HEAD)
                    for k in range(2):
                        for ic in range(DC):
                            last = pe.matmul(p_h[n % 3][:, k * G:(k + 1) * G], w1[:, r, ic, (2 * n + k) * P:(2 * n + k + 1) * P], gT[:, r, ic, :],
                                             start=(ic == 0), stop=(ic == DC - 1))
                    last.then_inc(s_["hidden"], 1)
                if not is_group(j, NG - 1):
                    turn_rows(i + (r + 1) // RING, j + 1, (r + 1) % RING)
                pe.wait_ge(s_["gy_ready"], j + HEAD)
                for t in range(TG):
                    for hc in range(HC):
                        if t == 0 and hc % 2 == 0:
                            pe.wait_ge(s_["gelu_ready"], HC // 2 * j + hc // 2 + 1 + HEAD)
                        last = pe.matmul(p_y[:, t * D:(t + 1) * D], hT[:, hc, t * P:(t + 1) * P], w2[:, r, hc, :],
                                         start=(hc == 0), stop=(hc == HC - 1))
                last.then_inc(s_["y_ready"], 1)

        @block.scalar
        def _(act):
            act.wait_ge(s_["turned"], 1 + HEAD)
            act.activation(gateT[:, :, :].rearrange("p c e -> p (c e)"), p_t[:, 0:DC * E], ACT.Copy)
            act.activation(b1[:, :], p_t[:, 2 * P:2 * P + E * HC], ACT.Copy).then_inc(s_["freed"], 1)

            def read_input(n, s):
                act.wait_ge(s_["turned_x"], n + 1 + HEAD)
                if not first(n):
                    act.wait_ge(s_["logits"], n - 1 + HEAD)
                act.activation(flat(xT[:, s, :, :]), p_t[:, :], ACT.Copy).then_inc(s_["xT_ready"], 1)
                act.activation(XN[:, bass.ds(TB * n, TB), :], XN_s[s][:, :, :], ACT.Copy).then_inc(s_["noted"], 1)

            read_input(0, 0)
            read_input(1, 1)
            for b, h, s in turns(act, ahead=3):
                if has_next(b, 2):
                    read_input(b + 2, s)
            act.wait_ge(s_["gap_ready"], 1 + HEAD)
            act.activation(probs[:, :, :], probs[:, :, :], ACT.Exp)
            act.activation(gap[:, :], gap[:, :], ACT.Exp).then_inc(s_["exp_ready"], 1)
            act.wait_ge(s_["routed"], 1 + HEAD)

            def store(j, r):
                act.wait_ge(s_["gy_ready"], j + 1 + HEAD)
                act.dma_start(rows_out[bass.ds(j * G, G), :].rearrange("(t p) d -> p t d", p=P), gy[:, r, :, :]).then_inc(kept[r], 16)

            for i, j, r in groups(act):
                e = expert_of(act, j)
                for n in range(HC // 2):
                    act.wait_ge(s_["hidden"], HC // 2 * j + n + 1 + HEAD)
                    if n == 0:
                        act.wait_ge(s_["y_ready"], j + HEAD)
                    for k in range(2):
                        last = act.activation(hT[:, 2 * n + k, :], p_h[n % 3][:, k * G:(k + 1) * G], ACT.Gelu,
                                              bias=b1[:, bass.ds(e * HC + 2 * n + k, 1)])
                    last.then_inc(s_["gelu_ready"], 1)
                    if n == 0 and not is_group(j, 0):
                        store(j - 1, (r - 1) % RING)
            store(NG - 1, RING - 1)

        @block.vector
        def _(dve):
            chain = Chain(dve, s_["chain_v"])

            def step(ins_):
                chain.done(ins_)
                chain.wait()

            dve.wait_ge(s_["set_up"], 1 + HEAD)

            def measure(n):
                layer_norm_stats(dve, chain, lambda t: tile_of(X, n, t), stats, aggr, s_["measured"])

            def norm(n, s):
                dve.wait_ge(s_["rstd_ready"], n + 1 + HEAD)
                if not first(n):
                    dve.wait_ge(s_["turned_x"], n - 1 + HEAD)
                    dve.wait_ge(s_["noted"], n - 1 + HEAD)
                layer_norm_apply(dve, lambda t: tile_of(X, n, t), lambda t: XN_s[s][:, t, :], aggr, rstd, s_["normed"])

            measure(0)
            norm(0, 0)
            measure(1)
            norm(1, 1)
            measure(2)
            chain.close()
            for b, h, s in turns(dve, ahead=3):
                if has_next(b, 2):
                    norm(b + 2, s)
                if has_next(b, 3):
                    measure(b + 3)
                dve.wait_ge(s_["logits"], b + 1 + HEAD)
                dve.tensor_copy(lg[:, bass.ds(TB * b, TB), :], p_h[s][:, 0:TB * E].rearrange("p (t e) -> p t e", t=TB)).then_inc(s_["lg_read"], 1)
                chain.close()
            dve.wait_ge(s_["lg_read"], B + HEAD)

            def by_tile(ap):
                return ap.unsqueeze(2).broadcast_to([P, NT, E])

            def by_expert(ap):
                return ap.unsqueeze(1).broadcast_to([P, NT, E])

            for k, src in ((0, lg), (1, lg2)):
                step(dve.tensor_reduce(best[:, k, :], src[:, :, :], AX.X, ALU.max))
                step(dve.tensor_tensor(cand[:, :, :], src[:, :, :], by_tile(best[:, k, :]), ALU.is_equal))
                step(dve.tensor_tensor(cand[:, :, :], cand[:, :, :], by_expert(falling[:, :]), ALU.mult))
                step(dve.tensor_reduce(cmax[:, :], cand[:, :, :], AX.X, ALU.max))
                step(dve.tensor_tensor(pick[:, k, :, :], cand[:, :, :], by_tile(cmax[:, :]), ALU.is_equal))
                if k == 0:
                    step(dve.scalar_tensor_tensor(flat(lg2[:, :, :]), flat(pick[:, 0, :, :]), -OFF, flat(lg[:, :, :]), ALU.mult, ALU.add))
            dve.tensor_tensor(both[:, :, :], pick[:, 0, :, :], pick[:, 1, :, :], ALU.add).then_inc(s_["both_ready"], 1)
            chain.done(dve.tensor_tensor(probs[:, :, :], lg[:, :, :], by_tile(best[:, 0, :]), ALU.subtract))
            chain.done(dve.tensor_tensor(gap[:, :], best[:, 1, :], best[:, 0, :], ALU.subtract))
            chain.wait()
            dve.sem_inc(s_["gap_ready"], 1)
            dve.wait_ge(s_["exp_ready"], 1 + HEAD)
            step(dve.tensor_reduce(zsum[:, :], probs[:, :, :], AX.X, ALU.add))
            step(dve.reciprocal(wt[:, 0, :], zsum[:, :]))
            step(dve.tensor_tensor(wt[:, 1, :], gap[:, :], wt[:, 0, :], ALU.mult))
            step(dve.tensor_tensor(wsum[:, :], wt[:, 0, :], wt[:, 1, :], ALU.add))
            step(dve.tensor_scalar(wsum[:, :], wsum[:, :], 1e-9, None, ALU.add))
            step(dve.reciprocal(wsum[:, :], wsum[:, :]))
            for k in range(2):
                chain.done(dve.tensor_tensor(wt[:, k, :], wt[:, k, :], wsum[:, :], ALU.mult))
            dve.wait_ge(s_["counted"], 1 + HEAD)
            step(dve.tensor_copy(total[:, :, :].rearrange("p t e -> p (t e)"), p_t[:, 0:NT * E]))
            for e in range(E):
                chain.done(dve.tensor_tensor_scan(upto[:, :, e], ones[:, 0:NT], total[:, :, e], 0.0, ALU.mult, ALU.add))
            chain.wait()
            step(dve.tensor_tensor(over[:, :, :], upto[:, NT - 1, :].unsqueeze(2).broadcast_to([P, E, B]),
                                   steps[:, :].unsqueeze(1).broadcast_to([P, E, B]), ALU.is_gt))
            step(dve.tensor_reduce(ngroups[:, :], over[:, :, :], AX.X, ALU.add))
            step(dve.tensor_tensor_scan(gend[:, :], ones[:, 0:E], ngroups[:, :], 0.0, ALU.mult, ALU.add))
            step(dve.tensor_tensor(gstart[:, :], gend[:, :], ngroups[:, :], ALU.subtract))
            step(dve.tensor_scalar(gstart[:, :], gstart[:, :], float(G), None, ALU.mult))
            step(dve.tensor_tensor(upto[:, :, :], upto[:, :, :], total[:, :, :], ALU.subtract))
            step(dve.tensor_tensor(before[:, :, :], p_c[:, 0:NT * E].rearrange("p (t e) -> p t e", e=E), upto[:, :, :], ALU.add))
            step(dve.tensor_tensor(before[:, :, :], before[:, :, :], by_expert(gstart[:, :]), ALU.add))
            for k in range(2):
                step(dve.tensor_tensor(cand[:, :, :], pick[:, k, :, :], before[:, :, :], ALU.mult))
                step(dve.tensor_reduce(place[:, k, :], cand[:, :, :], AX.X, ALU.add))
            step(dve.tensor_copy(place_i[:, :, :], place[:, :, :]))
            step(dve.tensor_tensor(passed[:, :, :], ramp[:, :].unsqueeze(2).broadcast_to([P, NG, E - 1]),
                                   gend[:, 0:E - 1].unsqueeze(1).broadcast_to([P, NG, E - 1]), ALU.is_ge))
            step(dve.tensor_reduce(owner[:, :], passed[:, :, :], AX.X, ALU.add))
            step(dve.tensor_copy(owner_i[:, :], owner[:, :]))
            dve.sem_inc(s_["routed"], 1)
            chain.close()

            def read_rows(j, r):
                dve.wait_ge(s_["gT_turned"], j + 1 + HEAD)
                dve.tensor_copy(flat(gT[:, r, :, :]), p_t[:, :]).then_inc(s_["gT_ready"], 1)

            read_rows(0, 0)
            for i, j, r in groups(dve):
                e = expert_of(dve, j)
                if not is_group(j, NG - 1):
                    read_rows(j + 1, (r + 1) % RING)
                dve.wait_ge(s_["y_ready"], j + 1 + HEAD)
                dve.wait_ge(kept[r], 16 * i + HEAD)
                for t in range(TG):
                    last = dve.tensor_tensor(gy[:, r, t, :], p_y[:, t * D:(t + 1) * D], b2[:, bass.ds(e, 1), :].rearrange("p a d -> p (a d)"), ALU.add)
                last.then_inc(s_["gy_ready"], 1)
            for n in range(2 * NT):
                t, k = divmod(n, 2)
                dve.wait_ge(gathered[n % GR], 16 * (n // GR + 1))
                if k:
                    dve.wait_ge(s_["combined"], n + HEAD)
                dve.scalar_tensor_tensor(X[:, t, :], got[:, n % GR, :], wt[:, k, t:t + 1], X[:, t, :], ALU.mult, ALU.add).then_inc(s_["combined"], 1)
            dve.wait_ge(s_["combined"], 2 * NT + HEAD)


R_CAP = 85.0


def time_channel_mix(nc, ins, X):
    L = "L1_attn_"
    with Phase(nc, "mix") as ph:
        ident = ph.sb("ident", [P, P])
        minus_half = ph.sb("minus_half", [P, TB])
        w_nat = ph.sb("w_nat", [P, 5, DC, D])
        fk_nat = ph.sb("fk_nat", [P, HC, D])
        fv_nat = ph.sb("fv_nat", [P, DC, HID])
        w = ph.sb("w", [P, 5, DC, D])
        fk = ph.sb("fk", [P, DC, HID])
        fv = ph.sb("fv", [P, HC, D])
        vec_names = ("ln1_g", "ln1_b", "ln2_g", "ln2_b", "time_mix_k", "time_mix_v", "time_mix_r",
                     "cm_k", "cm_r", "time_decay", "time_first")
        vec = ph.sb("vec", [P, len(vec_names), DC])
        at = {n: i for i, n in enumerate(vec_names)}

        def col(n, c):
            return vec[:, at[n], c:c + 1]

        decay = ph.sb("decay", [P, DC])
        stats = ph.sb("stats", [P, 3, TB, 6])
        aggr = ph.sb("aggr", [P, 3, TB, 2])
        rstd = ph.sb("rstd", [P, 3, TB])
        Y = ph.sb("Y", [P, NT, D])
        yn = ph.sb("yn", [P, TB, D])
        zn = ph.sb("zn", [P, TB, D])
        xa = ph.sb("xa", [P, DC, S + 1])
        xc = ph.sb("xc", [P, DC, S + 1])
        dif = ph.sb("dif", [P, DC, S])
        dif2 = ph.sb("dif2", [P, DC, S])
        mixed = ph.sb("mixed", [P, 3, DC, S])
        mixed2 = ph.sb("mixed2", [P, 2, DC, S])
        run = ph.sb("run", [P, DC, S + 1])
        num = ph.sb("num", [P, DC, S + 1])
        den = ph.sb("den", [P, DC, S + 1])
        vals = ph.sb("vals", [P, DC, S])
        top = ph.sb("top", [P, DC, S])
        fall = ph.sb("fall", [P, DC, S])
        gain = ph.sb("gain", [P, DC, S])
        gain_v = ph.sb("gain_v", [P, DC, S])
        e_old = ph.sb("e_old", [P, DC, S])
        e_new = ph.sb("e_new", [P, DC, S])
        e_r = ph.sb("e_r", [P, DC, S])
        a = ph.sb("a", [P, DC, S])
        a2 = ph.sb("a2", [P, DC, S])
        a3 = ph.sb("a3", [P, DC, S])
        mixed_out = ph.sb("mixed_out", [P, DC, S])
        hid = ph.sb("hid", [P, HC, S])
        hid_sq = ph.sb("hid_sq", [P, HC, S])
        e_r2 = ph.sb("e_r2", [P, TB, D])
        g = ph.sb("g", [P, TB, D])
        p_t = ph.ps("p_t")
        p_k, p_v, p_r = ph.ps("p_k"), ph.ps("p_v"), ph.ps("p_r")
        p_h = [ph.ps(f"p_h{i}") for i in range(2)]
        p_kv, p_y = ph.ps("p_kv"), ph.ps("p_y")
        banks = [p_t, p_k, p_v, p_r, p_h[0], p_h[1], p_kv, p_y]

        names = ("loaded ident_ready set_up turned freed consts turned_x xa_ready mixed_ready projected vals_ready run_ready "
                 "d_fall d_gain top_ready d_old d_new fall_ready gain_ready old_ready new_ready r_capped er_ready scans_ready "
                 "gain_v_ready den_ready den_part denom_ready dif_ready part_a part_b part_c out_ready att_ready turned_m xc_ready mixed2_ready hidden relu_ready squared r2_ready "
                 "r2_capped kv_ready er2_ready g_ready g_sum added chain_v chain_p stood_v stood_p").split()
        sems = {n: ph.own(n) if n.startswith(OWN) else ph.sem(n) for n in names}
        measured = [ph.sem(f"measured{k}") for k in range(3)]
        var_eps = [ph.sem(f"var_eps{k}") for k in range(3)]
        rstd_ready = [ph.sem(f"rstd_ready{k}") for k in range(3)]
        normed = [ph.sem(f"normed{k}") for k in range(3)]
        block = ph.block()
        s_ = sems

        n_blocks = (5 * 4 + 16 + 16) // 4

        @block.sync
        def _(sp):
            for n, m in enumerate(("att_Wk", "att_Wv", "att_Wr", "att_Wo", "ffn_Wr")):
                sp.dma_start(w_nat[:, n, :, :], ins[L + m].rearrange("(c p) d -> p c d", p=P)).then_inc(s_["loaded"], 16)
            sp.dma_start(fk_nat[:, :, :], ins[L + "ffn_Wk"].rearrange("(c p) d -> p c d", p=P)).then_inc(s_["loaded"], 16)
            sp.dma_start(fv_nat[:, :, :], ins[L + "ffn_Wv"].rearrange("(c p) d -> p c d", p=P)).then_inc(s_["loaded"], 16)
            with nc.allow_non_contiguous_dma(reason="vectors of 256 numbers"):
                for n, m in enumerate(vec_names):
                    sp.dma_start(vec[:, n, :], columns(ins[L + m])).then_inc(s_["loaded"], 16)

        n_loads = 7 + len(vec_names)

        @block.gpsimd
        def _(pool):
            make_identity(pool, ident[:, :], s_["ident_ready"])
            chain = Chain(pool, s_["chain_p"])
            chain.done(pool.memset(minus_half[:, :], -0.5))
            chain.done(pool.memset(xa[:, :, 0:1], 0.0))
            chain.done(pool.memset(xc[:, :, 0:1], 0.0))
            chain.done(pool.memset(run[:, :, 0:1], -1e38))
            chain.done(pool.memset(num[:, :, 0:1], 0.0))
            chain.done(pool.memset(den[:, :, 0:1], 0.0))
            chain.wait()
            pool.sem_inc(s_["set_up"], 1)
            chain.close()

            def root(k, b):
                wait_alone(pool, s_["stood_p"], (measured[k], b + 1))
                inverse_root(pool, rstd[:, k, :], aggr[:, k, :, 1], 1.0, LN_EPS, minus_half[:, :], var_eps[k], rstd_ready[k], b, s_["stood_p"])

            def compare(n):
                pool.wait_ge(s_["run_ready"], n + 1 + HEAD)
                pool.tensor_tensor(fall[:, :, :], run[:, :, 0:S], run[:, :, 1:S + 1], ALU.subtract).then_inc(s_["d_fall"], 1)
                pool.wait_ge(s_["top_ready"], n + 1 + HEAD)
                pool.tensor_tensor(e_old[:, :, :], run[:, :, 0:S], top[:, :, :], ALU.subtract).then_inc(s_["d_old"], 1)

            def weigh(n):
                pool.wait_ge(s_["gain_ready"], n + 1 + HEAD)
                pool.wait_ge(s_["vals_ready"], n + 1 + HEAD)
                pool.tensor_tensor(gain_v[:, :, :], gain[:, :, :], vals[:, :, :], ALU.mult).then_inc(s_["gain_v_ready"], 1)

            def change(n):
                pool.wait_ge(s_["xa_ready"], n + 1 + HEAD)
                pool.tensor_tensor(dif[:, :, :], xa[:, :, 1:S + 1], xa[:, :, 0:S], ALU.subtract).then_inc(s_["dif_ready"], 1)

            def combine(n):
                pool.wait_ge(s_["old_ready"], n + 1 + HEAD)
                pool.wait_ge(s_["den_ready"], n + 1 + HEAD)
                pool.tensor_tensor(a3[:, :, :], e_old[:, :, :], den[:, :, 0:S], ALU.mult).then_inc(s_["den_part"], 1)
                pool.wait_ge(s_["den_part"], n + 1 + HEAD)
                pool.wait_ge(s_["new_ready"], n + 1 + HEAD)
                pool.tensor_tensor(a3[:, :, :], a3[:, :, :], e_new[:, :, :], ALU.add).then_inc(s_["denom_ready"], 1)
                pool.tensor_tensor(a[:, :, :], e_new[:, :, :], vals[:, :, :], ALU.mult).then_inc(s_["part_a"], 1)
                pool.wait_ge(s_["scans_ready"], n + 1 + HEAD)
                pool.tensor_tensor(a2[:, :, :], e_old[:, :, :], num[:, :, 0:S], ALU.mult).then_inc(s_["part_b"], 1)
                pool.wait_ge(s_["part_b"], n + 1 + HEAD)
                pool.tensor_tensor(a[:, :, :], a[:, :, :], a2[:, :, :], ALU.add).then_inc(s_["part_c"], 1)

            def add(b):
                pool.wait_ge(s_["g_ready"], b + 1 + HEAD)
                pool.tensor_tensor(g[:, :, :], g[:, :, :], Y[:, bass.ds(TB * b, TB), :], ALU.add).then_inc(s_["g_sum"], 1)
                pool.wait_ge(s_["g_sum"], b + 1 + HEAD)
                pool.tensor_tensor(X[:, bass.ds(TB * b, TB), :], X[:, bass.ds(TB * b, TB), :], g[:, :, :], ALU.add).then_inc(s_["added"], 1)

            root(0, 0)
            root(1, 0)
            change(0)
            compare(0)
            weigh(0)
            combine(0)
            root(0, 1)
            root(1, 1)
            change(1)
            for b, h, s in turns(pool, ahead=2):
                root(2, b)
                if has_next(b, 2):
                    root(0, b + 2)
                if has_next(b):
                    compare(b + 1)
                    weigh(b + 1)
                if has_next(b, 2):
                    root(1, b + 2)
                if not first(b):
                    add(b - 1)
                if has_next(b):
                    combine(b + 1)
                if has_next(b, 2):
                    change(b + 2)
            add(B - 1)

        @block.tensor
        def _(pe):
            pe.wait_ge(s_["loaded"], 16 * n_loads)
            pe.wait_ge(s_["ident_ready"], 2 + HEAD)
            blocks = [w_nat[:, n, ot, ct * P:(ct + 1) * P] for n in range(5) for ct in range(DC) for ot in range(DC)]
            blocks += [fk_nat[:, ot, ct * P:(ct + 1) * P] for ct in range(DC) for ot in range(HC)]
            blocks += [fv_nat[:, ot, ct * P:(ct + 1) * P] for ct in range(HC) for ot in range(DC)]
            transpose_blocks(pe, blocks, banks, ident[:, :], s_["turned"], s_["freed"])
            pe.wait_ge(s_["freed"], n_blocks + HEAD)
            pe.wait_ge(s_["consts"], 1 + HEAD)

            def turn(src, bank, done):
                for c in range(DC):
                    for t in range(TB):
                        last = pe.transpose(bank[:, c * S + t * P:c * S + (t + 1) * P], src[:, t, c * P:(c + 1) * P], ident[:, :])
                last.then_inc(done, 1)

            def project(n, m0, m1):
                for m in range(m0, m1):
                    bank = (p_k, p_v, p_r)[m]
                    pe.wait_ge(s_["mixed_ready"], 3 * n + m + 1 + HEAD)
                    for oc in range(DC):
                        for ic in range(DC):
                            last = pe.matmul(bank[:, oc * S:(oc + 1) * S], w[:, m, ic, oc * P:(oc + 1) * P], mixed[:, m, ic, :],
                                             start=(ic == 0), stop=(ic == DC - 1))
                    last.then_inc(s_["projected"], 1)

            pe.wait_ge(normed[1], 1 + HEAD)
            turn(yn, p_t, s_["turned_x"])
            project(0, 0, 3)
            pe.wait_ge(normed[1], 2 + HEAD)
            turn(yn, p_t, s_["turned_x"])
            for b, h, s in turns(pe, ahead=2):
                pe.wait_ge(s_["out_ready"], b + 1 + HEAD)
                pe.wait_ge(s_["r2_capped"], b + HEAD)
                for t in range(TB):
                    for ic in range(DC):
                        last = pe.matmul(p_y[:, t * D:(t + 1) * D], mixed_out[:, ic, t * P:(t + 1) * P], w[:, 3, ic, :],
                                         start=(ic == 0), stop=(ic == DC - 1))
                last.then_inc(s_["att_ready"], 1)
                if has_next(b):
                    project(b + 1, 0, 2)
                pe.wait_ge(normed[2], b + 1 + HEAD)
                turn(zn, p_t, s_["turned_m"])
                if has_next(b):
                    project(b + 1, 2, 3)
                pe.wait_ge(s_["mixed2_ready"], 2 * b + 1 + HEAD)
                for t in range(TB):
                    for ic in range(DC):
                        last = pe.matmul(p_y[:, t * D:(t + 1) * D], mixed2[:, 1, ic, t * P:(t + 1) * P], w[:, 4, ic, :],
                                         start=(ic == 0), stop=(ic == DC - 1))
                last.then_inc(s_["r2_ready"], 1)
                pe.wait_ge(s_["mixed2_ready"], 2 * b + 2 + HEAD)
                for m in range(HC // 2):
                    pe.wait_ge(s_["relu_ready"], HC // 2 * b + max(m - 1, 0) + HEAD)
                    for k in range(2):
                        for ic in range(DC):
                            last = pe.matmul(p_h[m % 2][:, k * S:(k + 1) * S], fk[:, ic, (2 * m + k) * P:(2 * m + k + 1) * P], mixed2[:, 0, ic, :],
                                             start=(ic == 0), stop=(ic == DC - 1))
                    last.then_inc(s_["hidden"], 1)
                if has_next(b, 2):
                    pe.wait_ge(normed[1], b + 3 + HEAD)
                    turn(yn, p_t, s_["turned_x"])
                pe.wait_ge(s_["g_ready"], b + HEAD)
                pe.wait_ge(s_["squared"], HC // 2 * (b + 1) + HEAD)
                for t in range(TB):
                    for hc in range(HC):
                        last = pe.matmul(p_kv[:, t * D:(t + 1) * D], hid_sq[:, hc, t * P:(t + 1) * P], fv[:, hc, :],
                                         start=(hc == 0), stop=(hc == HC - 1))
                last.then_inc(s_["kv_ready"], 1)

        @block.scalar
        def _(act):
            act.wait_ge(s_["loaded"], 16 * n_loads)
            act.wait_ge(s_["set_up"], 1 + HEAD)
            dests = [flat(w[:, n, :, :]) for n in range(5)]
            dests += [fk[:, ct, g4 * 512:(g4 + 1) * 512] for ct in range(DC) for g4 in range(2)]
            dests += [flat(fv[:, 2 * g2:2 * g2 + 2, :]) for g2 in range(HC // 2)]
            evacuate_blocks(act, dests, banks, s_["turned"], s_["freed"])
            act.activation(decay[:, :], vec[:, at["time_decay"], :], ACT.Exp).then_inc(s_["freed"], 1)
            act.wait_ge(s_["consts"], 1 + HEAD)

            def read_input(n):
                act.wait_ge(s_["turned_x"], n + 1 + HEAD)
                for c in range(DC):
                    last = act.activation(xa[:, c, 1:S + 1], p_t[:, c * S:(c + 1) * S], ACT.Identity, scale=col("ln1_g", c), bias=col("ln1_b", c))
                last.then_inc(s_["xa_ready"], 1)

            def read_values(n):
                act.wait_ge(s_["projected"], 3 * n + 2 + HEAD)
                act.activation(flat(vals[:, :, :]), p_v[:, :], ACT.Copy).then_inc(s_["vals_ready"], 1)

            def time_mix(n):
                act.wait_ge(s_["d_gain"], n + 1 + HEAD)
                act.activation(gain[:, :, :], gain[:, :, :], ACT.Exp).then_inc(s_["gain_ready"], 1)
                act.wait_ge(s_["d_fall"], n + 1 + HEAD)
                for c in range(DC):
                    last = act.activation(fall[:, c, :], fall[:, c, :], ACT.Exp, bias=decay[:, c:c + 1])
                last.then_inc(s_["fall_ready"], 1)
                act.wait_ge(s_["d_new"], n + 1 + HEAD)
                for c in range(DC):
                    last = act.activation(e_new[:, c, :], e_new[:, c, :], ACT.Exp, bias=col("time_first", c))
                last.then_inc(s_["new_ready"], 1)
                act.wait_ge(s_["d_old"], n + 1 + HEAD)
                act.activation(e_old[:, :, :], e_old[:, :, :], ACT.Exp).then_inc(s_["old_ready"], 1)

            def gate(n):
                act.wait_ge(s_["r_capped"], n + 1 + HEAD)
                act.activation(e_r[:, :, :], e_r[:, :, :], ACT.Exp, scale=-1.0).then_inc(s_["er_ready"], 1)

            read_input(0)
            read_values(0)
            time_mix(0)
            gate(0)
            read_input(1)
            for b, h, s in turns(act, ahead=2):
                if has_next(b):
                    read_values(b + 1)
                act.wait_ge(s_["turned_m"], b + 1 + HEAD)
                for c in range(DC):
                    last = act.activation(xc[:, c, 1:S + 1], p_t[:, c * S:(c + 1) * S], ACT.Identity, scale=col("ln2_g", c), bias=col("ln2_b", c))
                last.then_inc(s_["xc_ready"], 1)
                if has_next(b):
                    time_mix(b + 1)
                act.wait_ge(s_["r2_capped"], b + 1 + HEAD)
                act.activation(e_r2[:, :, :], e_r2[:, :, :], ACT.Exp, scale=-1.0).then_inc(s_["er2_ready"], 1)
                for m in range(HC // 2 + 1):
                    if m < HC // 2:
                        act.wait_ge(s_["hidden"], HC // 2 * b + m + 1 + HEAD)
                        act.activation(flat(hid[:, 2 * m:2 * m + 2, :]), p_h[m % 2][:, :], ACT.Relu).then_inc(s_["relu_ready"], 1)
                    if m == 0:
                        act.wait_ge(s_["kv_ready"], b + HEAD)
                        if has_next(b):
                            gate(b + 1)
                    if m > 0:
                        act.wait_ge(s_["relu_ready"], HC // 2 * b + m + HEAD)
                        act.activation(hid_sq[:, 2 * m - 2:2 * m, :], hid[:, 2 * m - 2:2 * m, :], ACT.Square).then_inc(s_["squared"], 1)
                if has_next(b, 2):
                    read_input(b + 2)

        @block.vector
        def _(dve):
            chain = Chain(dve, s_["chain_v"])
            dve.wait_ge(s_["freed"], n_blocks + 1 + HEAD)
            chain.done(dve.tensor_scalar(decay[:, :], decay[:, :], -1.0, None, ALU.mult))
            chain.wait()
            dve.sem_inc(s_["consts"], 1)
            chain.close()

            def measure(k, src):
                layer_norm_stats(dve, chain, src, stats[:, k, :, :], aggr[:, k, :, :], measured[k])

            def norm(k, b, src, dst):
                dve.wait_ge(rstd_ready[k], b + 1 + HEAD)
                layer_norm_apply(dve, src, dst, aggr[:, k, :, :], rstd[:, k, :], normed[k])

            def mix(out, name, src, change, done):
                for c in range(DC):
                    last = dve.scalar_tensor_tensor(out[:, c, :], change[:, c, :], col(name, c), src[:, c, 0:S], ALU.mult, ALU.add)
                last.then_inc(done, 1)

            def measure_x(n):
                measure(0, lambda t: tile_of(X, n, t))

            def norm_x(n):
                norm(0, n, lambda t: tile_of(X, n, t), lambda t: tile_of(Y, n, t))

            def measure_y(n):
                wait_alone(dve, s_["stood_v"], (normed[0], n + 1))
                measure(1, lambda t: tile_of(Y, n, t))

            def norm_y(n):
                if not first(n):
                    dve.wait_ge(s_["turned_x"], n + HEAD)
                norm(1, n, lambda t: tile_of(Y, n, t), lambda t: yn[:, t, :])

            def mix_time(n):
                dve.wait_ge(s_["dif_ready"], n + 1 + HEAD)
                for m, nm in enumerate(("time_mix_k", "time_mix_v", "time_mix_r")):
                    mix(mixed[:, m, :, :], nm, xa, dif, s_["mixed_ready"])

            kk = p_k[:, :].rearrange("p (c n) -> p c n", c=DC)

            def run_max(n):
                dve.wait_ge(s_["projected"], 3 * n + 1 + HEAD)
                for c in range(DC):
                    last = dve.tensor_tensor_scan(run[:, c, 1:S + 1], decay[:, c:c + 1].broadcast_to([P, S]), kk[:, c, :], -1e38, ALU.add, ALU.max)
                last.then_inc(s_["run_ready"], 1)

            def compare(n):
                dve.wait_ge(s_["run_ready"], n + 1 + HEAD)
                dve.tensor_tensor(gain[:, :, :], kk, run[:, :, 1:S + 1], ALU.subtract).then_inc(s_["d_gain"], 1)
                for c in range(DC):
                    last = dve.scalar_tensor_tensor(top[:, c, :], kk[:, c, :], col("time_first", c), run[:, c, 0:S], ALU.add, ALU.max)
                last.then_inc(s_["top_ready"], 1)

            def compare_new(n):
                dve.wait_ge(s_["top_ready"], n + 1 + HEAD)
                dve.tensor_tensor(e_new[:, :, :], kk, top[:, :, :], ALU.subtract).then_inc(s_["d_new"], 1)
                dve.wait_ge(s_["projected"], 3 * n + 3 + HEAD)
                dve.tensor_scalar(flat(e_r[:, :, :]), p_r[:, :], -R_CAP, None, ALU.max).then_inc(s_["r_capped"], 1)

            def run_sums(n):
                dve.wait_ge(s_["gain_ready"], n + 1 + HEAD)
                dve.wait_ge(s_["fall_ready"], n + 1 + HEAD)
                for c in range(DC):
                    last = dve.tensor_tensor_scan(den[:, c, 1:S + 1], fall[:, c, :], gain[:, c, :], 0.0, ALU.mult, ALU.add)
                last.then_inc(s_["den_ready"], 1)
                dve.wait_ge(s_["gain_v_ready"], n + 1 + HEAD)
                for c in range(DC):
                    last = dve.tensor_tensor_scan(num[:, c, 1:S + 1], fall[:, c, :], gain_v[:, c, :], 0.0, ALU.mult, ALU.add)
                last.then_inc(s_["scans_ready"], 1)

            def finish_time(n):
                dve.wait_ge(s_["denom_ready"], n + 1 + HEAD)
                dve.wait_ge(s_["er_ready"], n + 1 + HEAD)
                chain.done(dve.scalar_tensor_tensor(flat(a3[:, :, :]), flat(e_r[:, :, :]), 1.0, flat(a3[:, :, :]), ALU.add, ALU.mult))
                chain.wait()
                chain.done(dve.reciprocal(a3[:, :, :], a3[:, :, :]))
                chain.wait()
                dve.wait_ge(s_["part_c"], n + 1 + HEAD)
                dve.tensor_tensor(mixed_out[:, :, :], a[:, :, :], a3[:, :, :], ALU.mult).then_inc(s_["out_ready"], 1)

            def cap_gate(b):
                dve.wait_ge(s_["r2_ready"], b + 1 + HEAD)
                dve.tensor_scalar(flat(e_r2[:, :, :]), p_y[:, :], -R_CAP, None, ALU.max).then_inc(s_["r2_capped"], 1)

            measure_x(0)
            norm_x(0)
            measure_y(0)
            norm_y(0)
            mix_time(0)
            run_max(0)
            compare(0)
            compare_new(0)
            run_sums(0)
            finish_time(0)
            measure_x(1)
            norm_x(1)
            measure_y(1)
            norm_y(1)
            mix_time(1)
            chain.close()
            for b, h, s in turns(dve, ahead=2):
                dve.wait_ge(s_["att_ready"], b + 1 + HEAD)
                for t in range(TB):
                    chain.done(dve.tensor_tensor(tile_of(Y, b, t), p_y[:, t * D:(t + 1) * D], tile_of(Y, b, t), ALU.add))
                chain.wait()
                measure(2, lambda t: tile_of(Y, b, t))
                if has_next(b, 2):
                    measure_x(b + 2)
                norm(2, b, lambda t: tile_of(Y, b, t), lambda t: zn[:, t, :])
                if has_next(b):
                    run_max(b + 1)
                    compare(b + 1)
                dve.wait_ge(s_["xc_ready"], b + 1 + HEAD)
                chain.done(dve.tensor_tensor(dif2[:, :, :], xc[:, :, 1:S + 1], xc[:, :, 0:S], ALU.subtract))
                chain.wait()
                for m, nm in ((1, "cm_r"), (0, "cm_k")):
                    mix(mixed2[:, m, :, :], nm, xc, dif2, s_["mixed2_ready"])
                if has_next(b):
                    compare_new(b + 1)
                if has_next(b, 2):
                    norm_x(b + 2)
                    measure_y(b + 2)
                cap_gate(b)
                if has_next(b):
                    run_sums(b + 1)
                if has_next(b, 2):
                    norm_y(b + 2)
                dve.wait_ge(s_["er2_ready"], b + 1 + HEAD)
                dve.wait_ge(s_["added"], b + HEAD)
                chain.done(dve.tensor_scalar(flat(g[:, :, :]), flat(e_r2[:, :, :]), 1.0, None, ALU.add))
                chain.wait()
                chain.done(dve.reciprocal(g[:, :, :], g[:, :, :]))
                if has_next(b):
                    finish_time(b + 1)
                if has_next(b, 2):
                    mix_time(b + 2)
                chain.wait()
                dve.wait_ge(s_["kv_ready"], b + 1 + HEAD)
                dve.tensor_tensor(flat(g[:, :, :]), p_kv[:, :], flat(g[:, :, :]), ALU.mult).then_inc(s_["g_ready"], 1)
                chain.close()
            dve.wait_ge(s_["added"], B + HEAD)


def float8_ffn(nc, ins, X, out):
    FAR = 128.0
    with Phase(nc, "ffn") as ph:
        ident = ph.sb("ident", [P, P])
        ident_b = ph.sb("ident_b", [P, P], BF16)
        minus_half = ph.sb("minus_half", [P, TB])
        w_nat = ph.sb("w_nat", [P, DC, D])
        near8 = ph.sb("near8", [P, DC, D], FP8)
        far8 = ph.sb("far8", [P, DC, D], FP8)
        near = ph.sb("near", [P, DC, D])
        far = ph.sb("far", [P, DC, D])
        is_far = ph.sb("is_far", [P, DC, D])
        w_q = ph.sb("w_q", [P, DC, D], BF16)
        wt = ph.sb("wt", [P, DC, D], BF16)
        bias = ph.sb("bias", [P, D])
        stats = ph.sb("stats", [P, TB, 6])
        aggr = ph.sb("aggr", [P, TB, 2])
        rstd = ph.sb("rstd", [P, TB])
        xn = ph.sb("xn", [P, TB, D])
        x8 = ph.sb("x8", [P, TB, D], FP8)
        xq = ph.sb("xq", [P, 2, TB, D], BF16)
        xT = ph.sb("xT", [P, 2, DC, S], BF16)
        y16 = ph.sb("y16", [P, 2, TB, D], F16)
        y = ph.sb("y", [P, 2, TB, D])
        p_t = [ph.ps(f"p_t{i}", (P, 1024), BF16) for i in range(2)]
        p_y = [ph.ps(f"p_y{i}") for i in range(2)]
        names = ("loaded ident_ready ident_b_ready w_ready w_turned wt_ready measured var_eps rstd_ready normed quantised turned_x xT_ready "
                 "y_ready y_read biased added stored chain_v stood_p").split()
        s_ = {n: ph.own(n) if n.startswith(OWN) else ph.sem(n) for n in names}
        block = ph.block()

        @block.sync
        def _(sp):
            sp.dma_start(w_nat[:, :, :], ins["L1_ffn_weight"].rearrange("(c p) d -> p c d", p=P)).then_inc(s_["loaded"], 16)
            sp.dma_start(bias[:, :], ins["L1_ffn_bias"].partition_broadcast(P)).then_inc(s_["loaded"], 16)
            out_v = out.rearrange("b (t p) d -> p (b t) d", p=P)
            for b0, b1 in ((0, 5), (5, 10), (10, 14), (14, 16)):
                sp.wait_ge(s_["added"], b1 + HEAD)
                sp.dma_start(out_v[:, b0 * TB:b1 * TB, :], X[:, b0 * TB:b1 * TB, :]).then_inc(s_["stored"], 16)
            sp.wait_ge(s_["stored"], 64)

        @block.gpsimd
        def _(pool):
            make_identity(pool, ident[:, :], s_["ident_ready"])
            pool.memset(minus_half[:, :], -0.5).then_inc(s_["ident_b_ready"], 1)
            pool.wait_ge(s_["ident_ready"], 2 + HEAD)
            pool.tensor_copy(ident_b[:, :], ident[:, :]).then_inc(s_["ident_b_ready"], 1)
            pool.wait_ge(s_["ident_b_ready"], 2 + HEAD)

            def norm_root(n):
                wait_alone(pool, s_["stood_p"], (s_["measured"], n + 1))
                inverse_root(pool, rstd[:, :], aggr[:, :, 1], 1.0, LN_EPS, minus_half[:, :], s_["var_eps"], s_["rstd_ready"], n, s_["stood_p"])

            norm_root(0)
            norm_root(1)
            norm_root(2)
            for b, h, s in turns(pool, ahead=3):
                if has_next(b, 3):
                    norm_root(b + 3)
                pool.wait_ge(s_["biased"], b + 1 + HEAD)
                pool.tensor_tensor(X[:, bass.ds(TB * b, TB), :], y[:, s, :, :], X[:, bass.ds(TB * b, TB), :], ALU.add).then_inc(s_["added"], 1)

        @block.tensor
        def _(pe):
            pe.wait_ge(s_["ident_b_ready"], 2 + HEAD)
            pe.wait_ge(s_["w_ready"], 1 + HEAD)
            for ct in range(DC):
                for ot in range(DC):
                    last = pe.transpose(p_t[0][:, (ct * DC + ot) * P:(ct * DC + ot + 1) * P], w_q[:, ot, ct * P:(ct + 1) * P], ident_b[:, :])
            last.then_inc(s_["w_turned"], 1)
            pe.wait_ge(s_["wt_ready"], 1 + HEAD)

            def turn_input(n, s):
                pe.wait_ge(s_["quantised"], n + 1 + HEAD)
                for c in range(DC):
                    for t in range(TB):
                        last = pe.transpose(p_t[s][:, c * S + t * P:c * S + (t + 1) * P], xq[:, s, t, c * P:(c + 1) * P], ident_b[:, :])
                last.then_inc(s_["turned_x"], 1)

            def multiply(n, s):
                pe.wait_ge(s_["xT_ready"], n + 1 + HEAD)
                if not first(n):
                    pe.wait_ge(s_["y_read"], n - 1 + HEAD)
                for t in range(TB):
                    for ic in range(DC):
                        last = pe.matmul(p_y[s][:, t * D:(t + 1) * D], xT[:, s, ic, t * P:(t + 1) * P], wt[:, ic, :],
                                         start=(ic == 0), stop=(ic == DC - 1))
                last.then_inc(s_["y_ready"], 1)

            turn_input(0, 0)
            turn_input(1, 1)
            multiply(0, 0)
            for b, h, s in turns(pe, ahead=3):
                if has_next(b):
                    multiply(b + 1, 1 - s)
                if has_next(b, 2):
                    turn_input(b + 2, s)

        @block.scalar
        def _(act):
            act.wait_ge(s_["w_turned"], 1 + HEAD)
            act.activation(flat(wt[:, :, :]), p_t[0][:, 0:512], ACT.Copy).then_inc(s_["wt_ready"], 1)

            def read_input(n, s):
                act.wait_ge(s_["turned_x"], n + 1 + HEAD)
                if not first(n):
                    act.wait_ge(s_["y_ready"], n - 1 + HEAD)
                act.activation(flat(xT[:, s, :, :]), p_t[s][:, 0:512], ACT.Copy).then_inc(s_["xT_ready"], 1)

            def read_product(n, s):
                act.wait_ge(s_["y_ready"], n + 1 + HEAD)
                if not first(n):
                    act.wait_ge(s_["biased"], n - 1 + HEAD)
                act.activation(flat(y16[:, s, :, :]), p_y[s][:, :], ACT.Copy).then_inc(s_["y_read"], 1)

            read_input(0, 0)
            read_input(1, 1)
            read_product(0, 0)
            for b, h, s in turns(act, ahead=3):
                if has_next(b):
                    read_product(b + 1, 1 - s)
                if has_next(b, 2):
                    read_input(b + 2, s)

        @block.vector
        def _(dve):
            chain = Chain(dve, s_["chain_v"])

            def step(ins_):
                chain.done(ins_)
                chain.wait()

            dve.wait_ge(s_["loaded"], 32)
            step(dve.tensor_scalar(w_nat[:, :, :], w_nat[:, :, :], 448.0, -448.0, ALU.min, ALU.max))
            step(dve.tensor_scalar(near[:, :, :], w_nat[:, :, :], FAR, -FAR, ALU.min, ALU.max))
            step(dve.tensor_copy(near8[:, :, :], near[:, :, :], saturate=False))
            step(dve.tensor_copy(near[:, :, :], near8[:, :, :]))
            step(dve.tensor_scalar(far[:, :, :], w_nat[:, :, :], 0.25, None, ALU.mult))
            step(dve.tensor_copy(far8[:, :, :], far[:, :, :], saturate=False))
            step(dve.tensor_copy(far[:, :, :], far8[:, :, :]))
            step(dve.tensor_tensor(is_far[:, :, :], w_nat[:, :, :], w_nat[:, :, :], ALU.mult))
            step(dve.tensor_scalar(is_far[:, :, :], is_far[:, :, :], FAR * FAR, None, ALU.is_gt))
            step(dve.scalar_tensor_tensor(flat(far[:, :, :]), flat(far[:, :, :]), 4.0, flat(near[:, :, :]), ALU.mult, ALU.subtract))
            step(dve.tensor_tensor(far[:, :, :], far[:, :, :], is_far[:, :, :], ALU.mult))
            step(dve.tensor_tensor(w_q[:, :, :], near[:, :, :], far[:, :, :], ALU.add))
            dve.sem_inc(s_["w_ready"], 1)
            chain.close()

            def measure(n):
                layer_norm_stats(dve, chain, lambda t: tile_of(X, n, t), stats, aggr, s_["measured"])

            def norm(n):
                dve.wait_ge(s_["rstd_ready"], n + 1 + HEAD)
                for t in range(TB):
                    chain.done(dve.tensor_scalar(xn[:, t, :], tile_of(X, n, t), aggr[:, t, 0:1], rstd[:, t:t + 1], ALU.subtract, ALU.mult))
                chain.wait()

            def quantise(n, s):
                step(dve.tensor_copy(x8[:, :, :], xn[:, :, :], saturate=False))
                if not first(n):
                    dve.wait_ge(s_["turned_x"], n - 1 + HEAD)
                dve.tensor_copy(xq[:, s, :, :], x8[:, :, :]).then_inc(s_["quantised"], 1)

            for n in range(2):
                measure(n)
                norm(n)
                quantise(n, n)
            measure(2)
            chain.close()
            for b, h, s in turns(dve, ahead=3):
                if has_next(b, 2):
                    norm(b + 2)
                    quantise(b + 2, s)
                if has_next(b, 3):
                    measure(b + 3)
                dve.wait_ge(s_["y_read"], b + 1 + HEAD)
                if not first(b):
                    dve.wait_ge(s_["added"], b - 1 + HEAD)
                last = dve.tensor_tensor(y[:, s, :, :], y16[:, s, :, :], bias[:, :].unsqueeze(1).broadcast_to([P, TB, D]), ALU.add)
                last.then_inc(s_["biased"], 1)
                chain.close()
            dve.wait_ge(s_["added"], B + HEAD)


def build(nc, ins, out):
    with ExitStack() as ctx:
        X = ctx.enter_context(nc.sbuf_tensor("X", [P, NT, D], F32))
        decay_attention(nc, ins, X, ins["x"])
        cross_attention(nc, ins, X, 0, True)
        experts_ffn(nc, ins, X)
        time_channel_mix(nc, ins, X)
        cross_attention(nc, ins, X, 1, False)
        float8_ffn(nc, ins, X, out)


_INS = [
    "x", "ctx_1024", "fside_BxSxS2_0", "mask_BxS2_if1",
    "L0_attn_q", "L0_attn_k", "L0_attn_log_decay", "L0_attn_norm_weight", "L0_attn_o_w",
    "L0_xattn_Wq", "L0_xattn_bq", "L0_xattn_Wk", "L0_xattn_bk", "L0_xattn_Wv", "L0_xattn_bv", "L0_xattn_Wo", "L0_xattn_bo",
    "L0_ffn_gate_w", "L0_ffn_w1", "L0_ffn_b1", "L0_ffn_w2", "L0_ffn_b2",
    "L1_attn_ln1_g", "L1_attn_ln1_b", "L1_attn_ln2_g", "L1_attn_ln2_b", "L1_attn_time_decay", "L1_attn_time_first",
    "L1_attn_time_mix_k", "L1_attn_time_mix_v", "L1_attn_time_mix_r",
    "L1_attn_att_Wk", "L1_attn_att_Wv", "L1_attn_att_Wr", "L1_attn_att_Wo", "L1_attn_cm_k", "L1_attn_cm_r",
    "L1_attn_ffn_Wk", "L1_attn_ffn_Wr", "L1_attn_ffn_Wv",
    "L1_xattn_Wq", "L1_xattn_bq", "L1_xattn_Wk", "L1_xattn_bk", "L1_xattn_Wv", "L1_xattn_bv", "L1_xattn_Wo", "L1_xattn_bo",
    "L1_xattn_lambda_bias", "L1_ffn_weight", "L1_ffn_bias",
]


def kernel(**inputs):
    import numpy as np
    import concourse.bacc as bacc
    from concourse.bass_utils import run_bass_kernel_spmd

    nc = bacc.Bacc("TRN2", target_bir_lowering=False, num_devices=1)
    arrays, ins = {}, {}
    for name in _INS:
        a = np.ascontiguousarray(inputs[name])
        a = a.reshape(a.shape or (1,))
        arrays[f"in_{name}_dram"] = a
        ins[name] = nc.dram_tensor(f"in_{name}_dram", a.shape, mybir.dt.from_np(a.dtype), kind="ExternalInput").ap()
    out = nc.dram_tensor("out_0_dram", (B, S, D), F32, kind="ExternalOutput").ap()
    build(nc, ins, out)
    r = run_bass_kernel_spmd(nc, [arrays], core_ids=[0])
    return r.results[0]["out_0_dram"]
```
